# Optimizing a Trainium2 kernel written in Bass

```python
import numpy as np
import jax
import jax.numpy as jnp

def _softmax(x, axis=-1):
    return jax.nn.softmax(x, axis=axis)

def _gelu(x):
    return jax.nn.gelu(x, approximate=True)

def _silu(x):
    return jax.nn.silu(x)

def _sigmoid(x):
    return jax.nn.sigmoid(x)

def _layernorm(x, axis=-1, eps=1e-05):
    m = jnp.mean(x, axis=axis, keepdims=True)
    v = jnp.var(x, axis=axis, keepdims=True)
    return (x - m) / jnp.sqrt(v + eps)

def _scatter_add(tgt, idx, src, axis=0):
    return tgt.at[idx].add(src)

def _segment_sum(src, seg, n):
    return jax.ops.segment_sum(src, seg, n)
kernel_name = 'mk_seq_preln_d1_jaxref_r4_90596e'

def setup_inputs(seed: int=0):
    np.random.seed(seed)
    _w = jnp.asarray

    def _L0_attn_setup():
        import jax, jax.numpy as jnp
        import numpy as np
        key = jax.random.key(seed)
        k1, k2, k3 = jax.random.split(key, 3)
        B, S, D, N = (2, 512, 256, 16)
        H = D // N
        x = jax.random.normal(k1, (B, S, D), dtype=jnp.float32)
        W_qkv = jax.random.normal(k2, (N, D, 3 * H), dtype=jnp.float32) / np.sqrt(D).astype(np.float32)
        W_out = jax.random.normal(k3, (N, H, D), dtype=jnp.float32) / np.sqrt(D).astype(np.float32)
        return {'x': x, 'W_qkv': W_qkv, 'W_out': W_out}
    _L0_attn_in = _L0_attn_setup()

    def _L0_ffn_setup():
        import jax, jax.numpy as jnp
        import numpy as np
        TOP_K = 2
        CAPACITY_FACTOR = 1.25

        def _moe_forward(x, gate_w, wi_gate, wi_up, wo):
            B, S, D = x.shape
            E = wi_gate.shape[0]
            N = B * S
            capacity = max(int(N / E * CAPACITY_FACTOR), 1)
            x_flat = x.reshape(N, D)
            router_logits = x_flat @ gate_w.T
            router_probs = jax.nn.softmax(router_logits, axis=-1)
            top_k_probs, top_k_idx = jax.lax.top_k(router_probs, TOP_K)
            top_k_probs = top_k_probs / jnp.sum(top_k_probs, axis=-1, keepdims=True)
            out = jnp.zeros_like(x_flat)
            experts = jnp.arange(E, dtype=jnp.int32)
            for k in range(TOP_K):
                eid = top_k_idx[:, k]
                ew = top_k_probs[:, k]
                onehot = (eid[:, None] == experts[None, :]).astype(jnp.int32)
                pos_all = jnp.cumsum(onehot, axis=0) - 1
                pos = jnp.take_along_axis(pos_all, eid[:, None].astype(jnp.int32), axis=1)[:, 0]
                valid = pos < capacity
                pos_c = jnp.where(valid, pos, 0)
                disp = jnp.zeros((E, capacity, D), x_flat.dtype).at[eid, pos_c].add(jnp.where(valid[:, None], x_flat, 0.0))
                gate = jax.nn.silu(jnp.einsum('ecd,efd->ecf', disp, wi_gate))
                up = jnp.einsum('ecd,efd->ecf', disp, wi_up)
                expert_out = jnp.einsum('ecf,edf->ecd', gate * up, wo)
                tok_out = expert_out[eid, pos_c]
                out = out + jnp.where(valid[:, None], ew[:, None] * tok_out, 0.0)
            return out.reshape(B, S, D)
        key = jax.random.key(seed)
        k1, k2, k3, k4, k5 = jax.random.split(key, 5)
        B, S, D, F, E = (4, 512, 256, 1024, 8)
        return {'x': jax.random.normal(k1, (B, S, D), dtype=jnp.float32), 'gate_w': jax.random.normal(k2, (E, D), dtype=jnp.float32) * 0.02, 'wi_gate': jax.random.normal(k3, (E, F, D), dtype=jnp.float32) * 0.02, 'wi_up': jax.random.normal(k4, (E, F, D), dtype=jnp.float32) * 0.02, 'wo': jax.random.normal(k5, (E, D, F), dtype=jnp.float32) * 0.02}
    _L0_ffn_in = _L0_ffn_setup()
    _d = {'L0_attn_x': _L0_attn_in['x'], 'L0_attn_W_qkv': _L0_attn_in['W_qkv'], 'L0_attn_W_out': _L0_attn_in['W_out'], 'L0_ffn_gate_w': _L0_ffn_in['gate_w'], 'L0_ffn_wi_gate': _L0_ffn_in['wi_gate'], 'L0_ffn_wi_up': _L0_ffn_in['wi_up'], 'L0_ffn_wo': _L0_ffn_in['wo']}
    _x0 = _d['L0_attn_x']
    _d['L0_attn_x'] = jax.random.normal(jax.random.fold_in(jax.random.key(seed), 1), (4, 2048, 256), dtype=_x0.dtype)
    del _x0
    return _d

def reference(L0_attn_x, L0_attn_W_qkv, L0_attn_W_out, L0_ffn_gate_w, L0_ffn_wi_gate, L0_ffn_wi_up, L0_ffn_wo):

    def _L0_attn_ref(x, W_qkv, W_out):
        import jax, jax.numpy as jnp
        import numpy as np
        B, S, D = x.shape
        head_dim = W_qkv.shape[-1] // 3
        qkv = jnp.einsum('bsd,ndh->bnsh', x, W_qkv)
        q, k, v = jnp.split(qkv, 3, axis=-1)
        scale = jnp.asarray(1.0 / np.sqrt(head_dim), dtype=x.dtype)
        attn = jnp.einsum('bnqh,bnkh->bnqk', q, k) * scale
        mask = jnp.asarray(-10000000000.0, dtype=x.dtype) * (1.0 - jnp.tril(jnp.ones((S, S), dtype=x.dtype)))
        attn = jax.nn.softmax(attn + mask, axis=-1)
        out = jnp.einsum('bnqk,bnkh->bnqh', attn, v)
        out = out.reshape(B, -1, S)
        return jnp.einsum('bds,nhd->bsd', out, W_out)

    def _L0_ffn_ref(x, gate_w, wi_gate, wi_up, wo):
        import jax, jax.numpy as jnp
        import numpy as np
        TOP_K = 2
        CAPACITY_FACTOR = 1.25

        def _moe_forward(x, gate_w, wi_gate, wi_up, wo):
            B, S, D = x.shape
            E = wi_gate.shape[0]
            N = B * S
            capacity = max(int(N / E * CAPACITY_FACTOR), 1)
            x_flat = x.reshape(N, D)
            router_logits = x_flat @ gate_w.T
            router_probs = jax.nn.softmax(router_logits, axis=-1)
            top_k_probs, top_k_idx = jax.lax.top_k(router_probs, TOP_K)
            top_k_probs = top_k_probs / jnp.sum(top_k_probs, axis=-1, keepdims=True)
            out = jnp.zeros_like(x_flat)
            experts = jnp.arange(E, dtype=jnp.int32)
            for k in range(TOP_K):
                eid = top_k_idx[:, k]
                ew = top_k_probs[:, k]
                onehot = (eid[:, None] == experts[None, :]).astype(jnp.int32)
                pos_all = jnp.cumsum(onehot, axis=0) - 1
                pos = jnp.take_along_axis(pos_all, eid[:, None].astype(jnp.int32), axis=1)[:, 0]
                valid = pos < capacity
                pos_c = jnp.where(valid, pos, 0)
                disp = jnp.zeros((E, capacity, D), x_flat.dtype).at[eid, pos_c].add(jnp.where(valid[:, None], x_flat, 0.0))
                gate = jax.nn.silu(jnp.einsum('ecd,efd->ecf', disp, wi_gate))
                up = jnp.einsum('ecd,efd->ecf', disp, wi_up)
                expert_out = jnp.einsum('ecf,edf->ecd', gate * up, wo)
                tok_out = expert_out[eid, pos_c]
                out = out + jnp.where(valid[:, None], ew[:, None] * tok_out, 0.0)
            return out.reshape(B, S, D)
        return _moe_forward(x, gate_w, wi_gate, wi_up, wo)
    x = L0_attn_x
    x = x + _L0_attn_ref(_layernorm(x, axis=-1), L0_attn_W_qkv, L0_attn_W_out)
    x = x + _L0_ffn_ref(_layernorm(x, axis=-1), L0_ffn_gate_w, L0_ffn_wi_gate, L0_ffn_wi_up, L0_ffn_wo)
    return x

_drawn_inputs = setup_inputs


def setup_inputs(seed=0):
    import zlib

    import numpy as np

    out = dict(_drawn_inputs(seed))
    spreads = {}
    factors = {'L0_ffn_gate_w': 2.703}
    for name, (base, spread) in spreads.items():
        noise = np.random.default_rng([zlib.crc32(name.encode()), seed]).standard_normal(out[name].shape)
        drawn = base * np.exp(spread * noise) if base else spread * noise
        out[name] = jnp.asarray(drawn.astype(out[name].dtype))
    for name, factor in factors.items():
        out[name] = (out[name] * factor).astype(out[name].dtype)
    return out
```

```python
from contextlib import ExitStack

import numpy as np
import concourse.bass as bass
from concourse import mybir

F32 = mybir.dt.float32
BF16 = mybir.dt.bfloat16
I32 = mybir.dt.int32
U32 = mybir.dt.uint32
ALU = mybir.AluOpType
ACT = mybir.ActivationFunctionType
AXX = mybir.AxisListType.X
ds = bass.ds

P = 128
B, S, D = 4, 2048, 256
NH, HD = 16, 16
J = S // P
KD = D // P
QH = 4
NQ = B * NH // QH
CH = 512
NC = S // CH
EPS = 1e-5
MASKED = -4.0e10
SCALE = HD ** -0.5
E, F, CAP = 8, 1024, 1280
EPS_ROWS = 96
MROWS = 3
KROWS = EPS_ROWS + MROWS
VW = 32


def steps_of_quad():
    return [(qc, kt) for qc in range(NC) for kt in range(4 * qc + 4)]


def max_units():
    units = []
    for g in range(NC):
        for t4 in range(4):
            for part in range(g):
                units += [(g, t4, h, 1, part, CH) for h in range(QH)]
            w = (t4 + 1) * P
            n = {0: 4, 1: 2, 2: 1, 3: 1}[t4]
            units += [(g, t4, h, n, g, w) for h in range(0, QH, n)]
    return units


STEPS = steps_of_quad()
NS = len(STEPS)
UNITS = max_units()
NU = len(UNITS)
FIRST_MAX_STEP = 6
LAST_UNIT_OF_GROUP = [max(i for i, u in enumerate(UNITS) if u[0] == g) for g in range(NC)]


def quad_plan():
    plan = [dict(units=[], finish=[], turn_max=[], turn_out=[]) for _ in range(NS + 2)]
    for i in range(NU):
        s = FIRST_MAX_STEP + i * (NS - FIRST_MAX_STEP) // NU
        plan[s]["units"].append(i)
    for g in range(NC):
        s = next(s for s in range(NS) if LAST_UNIT_OF_GROUP[g] in plan[s]["units"])
        plan[s]["finish"].append(g)
        plan[s + 1]["turn_max"].append(g)
    for qc in range(NC):
        last = max(s for s in range(NS) if STEPS[s][0] == qc)
        plan[min(last + 2, NS)]["turn_out"].append(qc)
    return plan


PLAN = quad_plan()


def looped(eng, n):
    def run(body):
        body(0)
        with eng.Fori(1, n) as i:
            body(i)
    return run


def build_constants(nc, ctx):
    ident = ctx.enter_context(nc.sbuf_tensor("ident", [P, P], F32))
    identb = ctx.enter_context(nc.sbuf_tensor("identb", [P, P], BF16))
    maskb = ctx.enter_context(nc.sbuf_tensor("maskb", [P, P], BF16))
    made = ctx.enter_context(nc.semaphore("constants_made"))
    with nc.Block() as block:
        @block.gpsimd
        def _(pool):
            nc.gpsimd.memset(ident[:], 0.0).then_inc(made, 1)
            nc.gpsimd.memset(maskb[:], 0.0).then_inc(made, 1)
            pool.wait_ge(made, 2)
            nc.gpsimd.affine_select(out=ident[:], in_=ident[:], compare_op=ALU.not_equal, fill=1.0, base=0,
                                    pattern=[[-1, P]], channel_multiplier=1).then_inc(made, 1)
            nc.gpsimd.affine_select(out=maskb[:], in_=maskb[:], compare_op=ALU.is_ge, fill=MASKED, base=0,
                                    pattern=[[-1, P]], channel_multiplier=1).then_inc(made, 1)
            pool.wait_ge(made, 4)
            nc.gpsimd.tensor_copy(identb[:], ident[:]).then_inc(made, 1)
            pool.wait_ge(made, 5)
    return ident, identb, maskb


def build_project(nc, c, x, wq, wk, wv, w_out, qparts, kparts, vstore):
    X, wsum, ident = c["X"], c["wsum"], c["ident"]
    with ExitStack() as ctx:
        def sb(n, s, t): return ctx.enter_context(nc.sbuf_tensor(n, s, t))
        def ps(n, s, t): return ctx.enter_context(nc.psum_tensor(n, s, t))
        def sem(n): return ctx.enter_context(nc.semaphore(n))
        passed = sem("passed0")
        wqk = sb("wqk", [P, 2, KD, D], F32)
        wvs = sb("wvs", [P, KD, D], F32)
        wos = sb("wos", [P, KD, D], F32)
        ones = sb("ones", [P, P], F32)
        stats = sb("stats", [P, J, 6], F32)
        mv = sb("mv", [P, J, 2], F32)
        std = sb("std", [P, J], F32)
        rstd = sb("rstd", [P, J], F32)
        xn = sb("xn", [P, J, D], F32)
        xT = sb("xT", [P, KD, S], F32)
        parts = sb("parts", [P, 2, 3, CH], BF16)
        rest = sb("rest", [P, 2, CH], F32)
        vst = sb("vst", [P, 2, NC, 4, QH * VW], F32)
        tp = ps("tp", [P, 2, CH], F32)
        pj = ps("pj", [P, 3, CH], F32)
        vp = ps("vp", [P, 2, CH], F32)
        wp = ps("wp", [P, CH], F32)
        epst = sb("epst", [P, 1], F32)

        w_loaded, x_loaded = sem("w_loaded"), sem("x_loaded")
        ones_made, v_consts = sem("ones_made"), sem("v_consts")
        stat_done, mv_done, std_done, rstd_done, xn_done = (sem(n) for n in
                                                           ("stat_done", "mv_done", "std_done", "rstd_done", "xn_done"))
        turned, turn_free, xT_done = sem("turned"), sem("turn_free"), sem("xT_done")
        proj_done, proj_free, part1, left1, part2, part3 = (sem(n) for n in
            ("proj_done", "proj_free", "part1", "left1", "part2", "part3"))
        parts_out = [sem(f"parts_out{i}") for i in range(2)]
        v_done, v_free, v_put = sem("v_done"), sem("v_free"), sem("v_put")
        v_out = [sem(f"v_out{i}") for i in range(2)]
        wsum_done, wsum_put = sem("wsum_done"), sem("wsum_put")
        NG = 2 * KD * NC
        groups = [(w, half, ch) for w in range(2) for ch in range(NC) for half in range(2)]

        with nc.Block() as block:
            @block.sync
            def _(sp):
                sp.dma_start(wqk[:, 0], wq).then_inc(w_loaded, 16)
                sp.dma_start(wqk[:, 1], wk).then_inc(w_loaded, 16)
                sp.dma_start(wvs[:], wv).then_inc(w_loaded, 16)
                sp.dma_start(wos[:], w_out).then_inc(w_loaded, 16)
                sp.dma_start(X[:, 0], x[0]).then_inc(x_loaded, 16)
                sp.wait_ge(x_loaded, 16)
                for b in range(1, B):
                    sp.dma_start(X[:, b], x[b]).then_inc(x_loaded, 16)
                    sp.wait_ge(x_loaded, 16 * b + 16)
                @looped(sp, B)
                def _(b):
                    for i, (w, half, ch) in enumerate(groups):
                        dst = (qparts, kparts)[w]
                        sp.wait_ge(part3, b * NG + i + 1)
                        sp.dma_start(dst[:, ds(b * D + half * P, P), ch * CH:(ch + 1) * CH].rearrange("r i s -> i r s"),
                                     parts[:, i % 2]).then_inc(parts_out[i % 2], 16)
                    for g in range(4):
                        sp.wait_ge(v_put, b * J + 4 * g + 4)
                        sp.dma_start(vstore[ds(b * 4, 4), :, 4 * g:4 * g + 4].rearrange("q p k w -> p q (k w)"),
                                     vst[:, g % 2].rearrange("p q k w -> p q (k w)")).then_inc(v_out[g % 2], 16)
                sp.wait_ge(parts_out[0], 16 * B * NG // 2)
                sp.wait_ge(parts_out[1], 16 * B * NG // 2)
                sp.wait_ge(v_out[0], 16 * B * 2)
                sp.wait_ge(v_out[1], 16 * B * 2)

            @block.gpsimd
            def _(pool):
                nc.gpsimd.memset(ones[:], 1.0).then_inc(ones_made, 1)
                nc.gpsimd.memset(epst[:], EPS).then_inc(ones_made, 1)
                v5 = vst.rearrange("p a q k (h w) -> p (a q k h) w", w=VW)
                nc.gpsimd.memset(v5[:, :, HD:VW], 0.0).then_inc(v_consts, 1)
                pool.wait_ge(v_consts, 1)
                nc.gpsimd.memset(v5[:, :, HD:HD + 1], 1.0).then_inc(v_consts, 1)
                @looped(pool, B)
                def _(b):
                    for i in range(NG):
                        pool.wait_ge(left1, b * NG + i + 1).then_inc(passed, 1)
                        nc.gpsimd.tensor_copy(parts[:, i % 2, 1], rest[:, i % 2]).then_inc(part2, 1)
                        pool.wait_ge(part2, b * NG + i + 1)
                        nc.gpsimd.tensor_tensor(parts[:, i % 2, 2], rest[:, i % 2], parts[:, i % 2, 1],
                                                ALU.subtract).then_inc(part3, 1)

            @block.scalar
            def _(act):
                act.wait_ge(ones_made, 2)
                @looped(act, B)
                def _(b):
                    act.wait_ge(mv_done, b * J + J)
                    act.wait_ge(rstd_done, b)
                    nc.scalar.activation(std[:], mv[:, :, 1], ACT.Sqrt, bias=epst[:, 0:1]).then_inc(std_done, 1)
                    for i in range(4):
                        act.wait_ge(turned, b * 8 + 2 * i + 1)
                        act.wait_ge(proj_done, b * NG)
                        act.wait_ge(v_done, b * J)
                        nc.scalar.copy(xT[:, 0].rearrange("d (p j) -> d j p", j=J)[:, 4 * i:4 * i + 4],
                                       tp[:, 0].rearrange("d (j p) -> d j p", p=P)).then_inc(turn_free, 1)
                    for i in range(NG):
                        act.wait_ge(proj_done, b * NG + i + 1)
                        act.wait_ge(parts_out[i % 2], (b * (NG // 2) + i // 2) * 16)
                        nc.scalar.copy(parts[:, i % 2, 0], pj[:, i % 2]).then_inc(part1, 1)

            @block.vector
            def _(dve):
                dve.wait_ge(w_loaded, 64)
                dve.wait_ge(wsum_done, 1)
                for r in range(B):
                    nc.vector.tensor_copy(wsum[:, r * D:(r + 1) * D], wp[:, 0:D]).then_inc(wsum_put, 1)
                @looped(dve, B)
                def _(b):
                    dve.wait_ge(x_loaded, 16 * b + 16)
                    for j in range(J):
                        if j == 0:
                            dve.wait_ge(mv_done, b * J)
                        nc.vector.bn_stats(stats[:, j], X[:, ds(b, 1), j].rearrange("p o d -> p (o d)")).then_inc(stat_done, 1)
                    dve.wait_ge(xn_done, b * J)
                    for j in range(J):
                        dve.wait_ge(stat_done, b * J + j + 1).then_inc(passed, 1)
                        nc.vector.bn_aggr(mv[:, j], stats[:, j]).then_inc(mv_done, 1)
                    dve.wait_ge(std_done, b + 1)
                    nc.vector.reciprocal(rstd[:], std[:]).then_inc(rstd_done, 1)
                    dve.wait_ge(rstd_done, b + 1)
                    dve.wait_ge(turned, b * 8)
                    for j in range(J):
                        nc.vector.tensor_scalar(xn[:, j], X[:, ds(b, 1), j].rearrange("p o d -> p (o d)"),
                                                mv[:, j, 0:1], rstd[:, j:j + 1],
                                                ALU.subtract, ALU.mult).then_inc(xn_done, 1)
                    for i in range(4):
                        dve.wait_ge(turned, b * 8 + 2 * i + 2)
                        dve.wait_ge(proj_done, b * NG)
                        dve.wait_ge(v_done, b * J)
                        nc.vector.tensor_copy(xT[:, 1].rearrange("d (p j) -> d j p", j=J)[:, 4 * i:4 * i + 4],
                                              tp[:, 1].rearrange("d (j p) -> d j p", p=P)).then_inc(xT_done, 1)
                    for i in range(NG):
                        dve.wait_ge(part1, b * NG + i + 1)
                        if i >= 2:
                            dve.wait_ge(part3, b * NG + i - 1)
                        else:
                            dve.wait_ge(part3, b * NG)
                        nc.vector.tensor_tensor(rest[:, i % 2], pj[:, i % 2], parts[:, i % 2, 0],
                                                ALU.subtract).then_inc(left1, 1)
                    dve.wait_ge(v_consts, 2)
                    for kt in range(J):
                        sl = (kt // 4) % 2
                        dve.wait_ge(v_done, b * J + kt + 1)
                        if kt % 4 == 0:
                            dve.wait_ge(v_out[sl], (b * 2 + kt // 8) * 16)
                        nc.vector.tensor_copy(
                            vst[:, sl, :, kt % 4].rearrange("p q (h w) -> p q h w", w=VW)[:, :, :, 0:HD],
                            vp[:, kt % 2, 0:D].rearrange("p (q h w) -> p q h w", q=4, w=HD)).then_inc(v_put, 1)

            @block.tensor
            def _(pe):
                pe.wait_ge(w_loaded, 64)
                pe.wait_ge(ones_made, 2)
                for k in range(KD):
                    last = nc.tensor.matmul(wp[:, 0:D], ones[:], wos[:, k], start=(k == 0), stop=(k == KD - 1))
                last.then_inc(wsum_done, 1)
                @looped(pe, B)
                def _(b):
                    for i in range(4):
                        for half in range(2):
                            pe.wait_ge(xn_done, b * J + 4 * i + 4)
                            if half == 0:
                                pe.wait_ge(turn_free, b * 4 + i)
                            else:
                                pe.wait_ge(xT_done, b * 4 + i)
                            for j in range(4):
                                last = nc.tensor.transpose(tp[:, half, j * P:(j + 1) * P],
                                                           xn[:, 4 * i + j, half * P:(half + 1) * P], ident[:])
                            last.then_inc(turned, 1)
                    pe.wait_ge(turn_free, b * 4 + 4)
                    pe.wait_ge(xT_done, b * 4 + 4)
                    for i, (w, half, ch) in enumerate(groups):
                        if i >= 2:
                            pe.wait_ge(left1, b * NG + i - 1)
                        else:
                            pe.wait_ge(left1, b * NG)
                        for k in range(KD):
                            last = nc.tensor.matmul(pj[:, i % 2], wqk[:, w, k, half * P:(half + 1) * P],
                                                    xT[:, k, ch * CH:(ch + 1) * CH], start=(k == 0), stop=(k == KD - 1))
                        last.then_inc(proj_done, 1)
                    for kt in range(J):
                        pe.wait_ge(v_put, b * J + max(kt - 1, 0))
                        for k in range(KD):
                            last = nc.tensor.matmul(vp[:, kt % 2, 0:D], xT[:, k, kt * P:(kt + 1) * P], wvs[:, k],
                                                    start=(k == 0), stop=(k == KD - 1))
                        last.then_inc(v_done, 1)


def build_attend(nc, c, qparts, kparts, vstore):
    X, wsum, ident, identb, maskb = c["X"], c["wsum"], c["ident"], c["identb"], c["maskb"]
    with ExitStack() as ctx:
        def sb(n, s, t): return ctx.enter_context(nc.sbuf_tensor(n, s, t))
        def ps(n, s, t): return ctx.enter_context(nc.psum_tensor(n, s, t))
        def sem(n): return ctx.enter_context(nc.semaphore(n))
        passed = sem("passed1")
        Q = sb("Q", [P, 2, NC, QH, CH], BF16)
        K = sb("K", [P, 2, QH, S], BF16)
        V = sb("V", [P, 2, J, QH * VW], F32)
        NP = 4
        probs = sb("probs", [P, NP, QH, CH], F32)
        maxima = sb("maxima", [P, NC, QH, 4, 4], F32)
        negmax = sb("negmax", [P, NC, QH * 4], F32)
        mparts = sb("mparts", [QH * 4, NC, MROWS, P], BF16)
        mrest = sb("mrest", [QH * 4, NC, P], F32)
        outs = sb("outs", [P, NC, CH], F32)
        recip = sb("recip", [P, NC, 4, QH], F32)
        weight = sb("weight", [P, NC, 4, QH], F32)
        addend = sb("addend", [P, NC, 4, QH, J], F32)
        scores = ps("scores", [P, 2, 2, CH], F32)
        fill = ps("fill", [P, 2, CH], F32)
        acc = ps("acc", [P, CH], F32)
        turn = ps("turn", [P, CH], F32)

        loaded = [sem(f"loaded{i}") for i in range(2)]
        rows_in = [[sem(f"rows_in{i}{g}") for g in range(NC)] for i in range(2)]
        ones_made = sem("k_ones_made")
        scores_ready, probs_ready, masked, pv_done = (sem(n) for n in ("scores_ready", "probs_ready", "masked", "pv_done"))
        fill_ready, fill_read, negmax_ready = sem("fill_ready"), sem("fill_read"), sem("negmax_ready")
        turned_out, turned_max = sem("turned_out"), sem("turned_max")
        out_read, turn_read, outs_ready = sem("out_read"), sem("turn_read"), sem("outs_ready")
        part1, left1, part2, part3 = sem("m_part1"), sem("m_left1"), sem("m_part2"), sem("m_part3")
        recip_ready, weight_ready, addend_ready, added = (sem(n) for n in
            ("recip_ready", "weight_ready", "addend_ready", "added"))
        NDMA = 6 * NC + 6 + 1

        def turns_before(step, kind, g):
            n = 0
            for s in range(len(PLAN)):
                for k in ("turn_max", "turn_out"):
                    for x in PLAN[s][k]:
                        if (s, k, x) == (step, kind, g):
                            return n
                        n += 1

        def loop_quads(eng, body):
            body(0, 0, True)
            body(0, 1, True)
            with eng.Fori(1, NQ // 2 - 1) as i:
                body(i, 0, True)
                body(i, 1, True)
            body(NQ // 2 - 1, 0, True)
            body(NQ // 2 - 1, 1, False)

        with nc.Block() as block:
            @block.sync
            def _(sp):
                def load(q, par):
                    for r, src in ((0, 0), (1, 0), (2, 0), (3, 1), (4, 1), (5, 2)):
                        for g in range(NC):
                            sp.dma_start(Q[16 * r:16 * r + 16, par, g],
                                         qparts[src, ds(q * QH * HD, QH * HD), g * CH:(g + 1) * CH]
                                         .rearrange("(h i) s -> i h s", i=HD)).then_inc(loaded[par], 16)
                    for r, src in ((0, 0), (1, 1), (2, 2), (3, 0), (4, 1), (5, 0)):
                        sp.dma_start(K[16 * r:16 * r + 16, par], kparts[src, ds(q * QH * HD, QH * HD), :]
                                     .rearrange("(h i) s -> i h s", i=HD)).then_inc(loaded[par], 16)
                    sp.dma_start(V[:, par], vstore[ds(q, 1)].rearrange("o p k w -> p (o k) w")).then_inc(loaded[par], 16)

                def rows(q, par):
                    for g in range(NC):
                        sp.wait_ge(part3, q * NC + g + 1)
                        for r in range(MROWS):
                            sp.dma_start(Q[EPS_ROWS + r:EPS_ROWS + r + 1, par, g].rearrange("o h s -> o (h s)"),
                                         mparts[:, g, r]).then_inc(rows_in[par][g], 16)

                def body(pr, par, more):
                    q = pr * 2 + par
                    if more:
                        sp.wait_ge(pv_done, q * NS)
                        load(q + 1, 1 - par)
                        rows(q + 1, 1 - par)

                load(0, 0)
                rows(0, 0)
                loop_quads(sp, body)

            @block.gpsimd
            def _(pool):
                nc.gpsimd.memset(K[EPS_ROWS:P, :, :, :], 1.0).then_inc(ones_made, 1)

                def max_parts(g, n):
                    pool.wait_ge(left1, n + 1).then_inc(passed, 1)
                    nc.gpsimd.tensor_copy(mparts[:, g, 1], mrest[:, g]).then_inc(part2, 1)
                    pool.wait_ge(part2, n + 1)
                    nc.gpsimd.tensor_tensor(mparts[:, g, 2], mrest[:, g], mparts[:, g, 1],
                                            ALU.subtract).then_inc(part3, 1)

                def quad(b, k, q, more):
                    nmask = 0
                    for s in range(NS + 1):
                        if s < NS:
                            qc, kt = STEPS[s]
                            if kt >= 4 * qc:
                                pool.wait_ge(probs_ready, (q * NS + s + 1) * 2).then_inc(passed, 1)
                                c0 = (kt - 4 * qc) * P
                                diag = probs[:, s % NP, :, c0:c0 + P]
                                nc.gpsimd.affine_select(out=diag, in_=diag, compare_op=ALU.is_ge, fill=0.0, base=0,
                                                        pattern=[[0, QH], [1, P]], channel_multiplier=-1).then_inc(masked, 1)
                        for g in PLAN[s]["turn_max"] if more else []:
                            max_parts(g, (q + 1) * NC + g)
                        for qc in PLAN[s]["turn_out"]:
                            pool.wait_ge(addend_ready, q * NC + qc + 1)
                            dst = X[:, ds(b, 1)].rearrange("p o j (n t) -> p (o n) t j", t=J)[
                                :, k * QH:(k + 1) * QH, 4 * qc:4 * qc + 4].rearrange("p n t j -> p t n j")
                            nc.gpsimd.tensor_tensor(dst, dst, addend[:, qc], ALU.add).then_inc(added, 1)

                for g in range(NC):
                    max_parts(g, g)
                with pool.Fori(0, B - 1) as b:
                    for k in range(4):
                        quad(b, k, b * 4 + k, True)
                for k in range(4):
                    quad(B - 1, k, (B - 1) * 4 + k, k < 3)
                pool.wait_ge(added, NQ * NC)

            @block.scalar
            def _(act):
                def body(pr, par, more):
                    q = pr * 2 + par
                    for s, (qc, kt) in enumerate(STEPS):
                        c0 = max(kt - 4 * qc, 0) * P
                        for pair in range(2):
                            act.wait_ge(scores_ready, (q * NS + s) * 2 + pair + 1)
                            if pair == 0 and (s >= NP or not isinstance(q, int) or q > 0):
                                act.wait_ge(pv_done, q * NS + s - NP + 1)
                            nc.scalar.activation(probs[:, s % NP, 2 * pair:2 * pair + 2, c0:CH], scores[:, pair, :, c0:CH],
                                                 ACT.Exp, scale=SCALE).then_inc(probs_ready, 1)
                loop_quads(act, body)

            @block.vector
            def _(dve):
                def reduce_unit(q, i):
                    g, t4, h, n, part, w = UNITS[i]
                    dve.wait_ge(fill_ready, q * NU + i + 1)
                    nc.vector.tensor_reduce(maxima[:, g, h:h + n, t4, part],
                                            fill[:, i % 2, 0:n * w].rearrange("p (h w) -> p h w", w=w),
                                            AXX, ALU.max).then_inc(fill_read, 1)

                def finish(q, g):
                    dve.wait_ge(fill_read, q * NU + LAST_UNIT_OF_GROUP[g] + 1)
                    dve.wait_ge(turned_max, q * NC)
                    nc.vector.tensor_reduce(negmax[:, g], maxima[:, g, :, :, 0:g + 1].rearrange("p h t r -> p (h t) r"),
                                            AXX, ALU.max, negate=True).then_inc(negmax_ready, 1)

                def take_max(pr, par, g):
                    n = (pr * 2 + par) * NC + g
                    dve.wait_ge(turned_max, n + 1)
                    dve.wait_ge(rows_in[1 - par][g], (pr + par) * 16 * MROWS)
                    nc.vector.tensor_copy(mparts[:, g, 0], turn[0:QH * 4, 0:P]).then_inc(part1, 1)
                    dve.wait_ge(part1, n + 1)
                    nc.vector.tensor_tensor(mrest[:, g], turn[0:QH * 4, 0:P], mparts[:, g, 0],
                                            ALU.subtract).then_inc(left1, 1)

                def read_out(q, qc):
                    dve.wait_ge(pv_done, q * NS + 4 * (qc + 1) * (qc + 2) // 2)
                    dve.wait_ge(turned_out, q * NC)
                    nc.vector.tensor_copy(outs[:, qc], acc[:]).then_inc(outs_ready, 1)

                def take_out(q, qc):
                    n = q * NC + qc
                    dve.wait_ge(turned_out, n + 1)
                    dve.wait_ge(added, q * NC)
                    t = turn.rearrange("p (t h w) -> p t h w", t=4, w=VW)
                    nc.vector.reciprocal(recip[:, qc], t[:, :, :, HD]).then_inc(recip_ready, 1)
                    dve.wait_ge(recip_ready, n + 1)
                    nc.vector.tensor_tensor(weight[:, qc], recip[:, qc],
                                            wsum[:, ds(q * QH * J, QH * J)].rearrange("p (h t) -> p t h", t=J)[:, 4 * qc:4 * qc + 4],
                                            ALU.mult).then_inc(weight_ready, 1)
                    dve.wait_ge(weight_ready, n + 1)
                    nc.vector.tensor_tensor(addend[:, qc], t[:, :, :, 0:HD],
                                            weight[:, qc].unsqueeze(3).to_broadcast([P, 4, QH, HD]),
                                            ALU.mult).then_inc(addend_ready, 1)

                def body(pr, par, more):
                    q = pr * 2 + par
                    for s in range(NS + 1):
                        if more:
                            for i in PLAN[s]["units"]:
                                reduce_unit(q + 1, i)
                            for g in PLAN[s]["finish"]:
                                finish(q + 1, g)
                            for g in PLAN[s]["turn_max"]:
                                take_max(pr + par, 1 - par, g)
                        if s > 0 and (s == NS or STEPS[s][0] != STEPS[s - 1][0]):
                            read_out(q, STEPS[s - 1][0])
                        for qc in PLAN[s]["turn_out"]:
                            take_out(q, qc)

                for g in range(NC):
                    for i in range(NU):
                        if UNITS[i][0] == g:
                            reduce_unit(0, i)
                    finish(0, g)
                    take_max(0, 0, g)
                loop_quads(dve, body)

            @block.tensor
            def _(pe):
                mm = nc.tensor.matmul

                def fill_unit(pr, par, i):
                    q = pr * 2 + par
                    g, t4, h0, n, part, w = UNITS[i]
                    if i >= 2 or not (isinstance(q, int) and q == 0):
                        pe.wait_ge(fill_read, q * NU + i - 1)
                    if i == 0:
                        pe.wait_ge(loaded[par], (pr + 1) * 16 * NDMA)
                    for h in range(h0, h0 + n):
                        at = (h - h0) * w
                        last = mm(fill[:, i % 2, at:at + w], Q[0:EPS_ROWS, par, g, h, t4 * P:(t4 + 1) * P],
                                  K[0:EPS_ROWS, par, h, part * CH:part * CH + w], start=True, stop=True,
                                  skip_group_check=True)
                        if part == g:
                            last = mm(fill[:, i % 2, at + w - P:at + w], identb[:], maskb[:], start=False, stop=True,
                                      skip_group_check=True)
                    last.then_inc(fill_ready, 1)

                def turn_free(q, kind, x, more):
                    uses = [(k, y) for p in PLAN for k in ("turn_max", "turn_out") for y in p[k] if more or k == "turn_out"]
                    at = uses.index((kind, x))
                    if at == 0:
                        pe.wait_ge(left1, (q + 1) * NC)
                        pe.wait_ge(addend_ready, q * NC)
                    elif uses[at - 1][0] == "turn_max":
                        pe.wait_ge(left1, (q + 1) * NC + uses[at - 1][1] + 1)
                    else:
                        pe.wait_ge(addend_ready, q * NC + uses[at - 1][1] + 1)

                def turn_max(q, g):
                    pe.wait_ge(negmax_ready, q * NC + g + 1)
                    nc.tensor.transpose(turn[0:QH * 4, 0:P], negmax[:, g], ident[:]).then_inc(turned_max, 1)

                def turn_out(q, qc):
                    pe.wait_ge(outs_ready, q * NC + qc + 1)
                    for t in range(4):
                        last = nc.tensor.transpose(turn[:, t * P:(t + 1) * P], outs[:, qc, t * P:(t + 1) * P], ident[:])
                    last.then_inc(turned_out, 1)

                def score(q, par, s, pair):
                    qc, kt = STEPS[s]
                    c0 = max(kt - 4 * qc, 0) * P
                    if s > 0 or not (isinstance(q, int) and q == 0):
                        pe.wait_ge(probs_ready, (q * NS + s) * 2 + pair - 1)
                    for hh in range(2):
                        h = 2 * pair + hh
                        last = mm(scores[:, pair, hh, c0:CH], K[0:KROWS, par, h, kt * P:(kt + 1) * P],
                                  Q[0:KROWS, par, qc, h, c0:CH], start=True, stop=True)
                    last.then_inc(scores_ready, 1)

                def weigh(q, par, s):
                    qc, kt = STEPS[s]
                    c0 = max(kt - 4 * qc, 0) * P
                    pe.wait_ge(probs_ready, (q * NS + s + 1) * 2)
                    if kt >= 4 * qc:
                        pe.wait_ge(masked, (q * NC + qc) * 4 + kt - 4 * qc + 1)
                    if kt == 0:
                        pe.wait_ge(outs_ready, q * NC + qc)
                    for h in range(QH):
                        last = mm(acc[VW * h:VW * h + VW, c0:CH], V[:, par, kt, VW * h:VW * h + VW],
                                  probs[:, s % NP, h, c0:CH], start=(kt == 0), stop=(kt == 4 * qc + 3),
                                  skip_group_check=True)
                    last.then_inc(pv_done, 1)

                def body(pr, par, more):
                    q = pr * 2 + par
                    for s in range(NS + 1):
                        units = PLAN[s]["units"] if more else []
                        if s < NS:
                            if STEPS[s][1] == 0:
                                pe.wait_ge(rows_in[par][STEPS[s][0]], (pr + 1) * 16 * MROWS)
                            score(q, par, s, 0)
                        for i in units[:len(units) // 2]:
                            fill_unit(pr + par, 1 - par, i)
                        if s < NS:
                            score(q, par, s, 1)
                        for i in units[len(units) // 2:]:
                            fill_unit(pr + par, 1 - par, i)
                        if s > 0:
                            weigh(q, par, s - 1)
                        for g in PLAN[s]["turn_max"] if more else []:
                            turn_free(q, "turn_max", g, more)
                            turn_max(q + 1, g)
                        for qc in PLAN[s]["turn_out"]:
                            turn_free(q, "turn_out", qc, more)
                            turn_out(q, qc)

                pe.wait_ge(ones_made, 1)
                for g in range(NC):
                    for i in range(NU):
                        if UNITS[i][0] == g:
                            fill_unit(0, 0, i)
                    if g > 0:
                        pe.wait_ge(left1, g)
                    turn_max(0, g)
                loop_quads(pe, body)


SLOTS = E * 2 * CAP
TILES = SLOTS // P
ET = 2 * CAP // P
CT = 4
EC = ET // CT
C64 = B * J


def build_route(nc, c, gate_w, xrows):
    X, ident = c["X"], c["ident"]
    rowof, slotof, W = c["rowof"], c["slotof"], c["W"]
    with ExitStack() as ctx:
        def sb(n, s, t): return ctx.enter_context(nc.sbuf_tensor(n, s, t))
        def ps(n, s, t): return ctx.enter_context(nc.psum_tensor(n, s, t))
        def sem(n): return ctx.enter_context(nc.semaphore(n))
        passed = sem("passed2")
        gw = sb("gw", [P, KD, E], F32)
        epst = sb("r_eps", [P, 1], F32)
        before = sb("before", [P, P], F32)
        ones = sb("r_ones", [P, P], F32)
        zerob = sb("zerob", [P, P], BF16)
        lane = sb("lane", [P, P], BF16)
        tile_no = sb("tile_no", [P, TILES], BF16)
        part_no = sb("part_no", [P, 1], F32)
        col_no = sb("col_no", [P, 2, C64], F32)
        expert_no = sb("expert_no", [P, E], F32)
        rank = sb("rank", [P, E], F32)
        stats = sb("r_stats", [P, J, 6], F32)
        mv = sb("r_mv", [P, J, 2], F32)
        std = sb("r_std", [P, J], F32)
        rstd = sb("r_rstd", [P, J], F32)
        xn = sb("r_xn", [P, J, D], F32)
        xT = sb("r_xT", [P, KD, J, P], F32)
        small = [P, C64, E]
        shifted, ex, pr = sb("shifted", small, F32), sb("ex", small, F32), sb("pr", small, F32)
        eq, cand = sb("eq", small, F32), sb("cand", small, F32)
        top, total, rtotal, best = (sb(n, [P, C64], F32) for n in ("top", "total", "rtotal", "best"))
        hot = sb("hot", [P, 2, C64, E], F32)
        prob = sb("prob", [P, 2, C64], F32)
        count = sb("count", [P, 2, 2 * B, J, E], F32)
        sums = sb("sums", [P, 2, B, E], F32)
        offset = sb("offset", [P, 2, B, E], F32)
        place, eno, valid, slot = (sb(n, [P, 2, C64], F32) for n in ("place", "eno", "valid", "slot"))
        slot_i, hi_i, lo_i = (sb(n, [P, 2, C64], I32) for n in ("slot_i", "hi_i", "lo_i"))
        hi, lo = sb("hi", [P, 2, C64], F32), sb("lo", [P, 2, C64], F32)
        LS = 4
        is_lane = sb("is_lane", [P, LS, P], BF16)
        is_tile = sb("is_tile", [P, LS, 2, TILES], BF16)
        tabc = sb("tabc", [P, TILES], F32)
        tabr = sb("tabr", [P, TILES], F32)
        tp = ps("r_tp", [P, 2, CH], F32)
        logits = ps("logits", [P, C64, E], F32)
        sums_before = ps("sums_before", [P, 2, 64], F32)
        table = ps("table", [P, 2 * TILES], F32)

        gw_loaded, consts, stat_done, mv_done, std_done, rstd_done, xn_done = (sem("r_" + n) for n in
            ("gw_loaded", "consts", "stat_done", "mv_done", "std_done", "rstd_done", "xn_done"))
        turned, turn_free, xT_done, logits_done, rows_out = (sem("r_" + n) for n in
            ("turned", "turn_free", "xT_done", "logits_done", "rows_out"))
        step, exp_done, sums_ready, ranked, hot_tiles, tabled, table_done, shift_ready = (sem("r_" + n) for n in
            ("step", "exp_done", "sums_ready", "ranked", "hot_tiles", "tabled", "table_done", "shift_ready"))

        with nc.Block() as block:
            @block.sync
            def _(sp):
                sp.dma_start(gw[:], gate_w).then_inc(gw_loaded, 16)
                @looped(sp, B)
                def _(b):
                    sp.wait_ge(xn_done, b * J + J)
                    sp.dma_start(xrows.rearrange("(p b j) d -> p b j d", b=B, j=J)[:, ds(b, 1)].rearrange("p o j d -> p (o j) d"),
                                 xn[:]).then_inc(rows_out, 16)
                sp.wait_ge(rows_out, 16 * B)

            @block.gpsimd
            def _(pool):
                nc.gpsimd.memset(epst[:], EPS).then_inc(consts, 1)
                nc.gpsimd.memset(before[:], 0.0).then_inc(consts, 1)
                nc.gpsimd.memset(ones[:], 1.0).then_inc(consts, 1)
                nc.gpsimd.memset(zerob[:], 0.0).then_inc(consts, 1)
                nc.gpsimd.iota(lane[:], pattern=[[1, P]], base=0, channel_multiplier=0,
                               allow_small_or_imprecise_dtypes=True).then_inc(consts, 1)
                nc.gpsimd.iota(tile_no[:], pattern=[[1, TILES]], base=0, channel_multiplier=0,
                               allow_small_or_imprecise_dtypes=True).then_inc(consts, 1)
                nc.gpsimd.iota(part_no[:], pattern=[[1, 1]], base=0, channel_multiplier=1,
                               allow_small_or_imprecise_dtypes=True).then_inc(consts, 1)
                nc.gpsimd.iota(col_no[:], pattern=[[0, 2], [1, C64]], base=0, channel_multiplier=0,
                               allow_small_or_imprecise_dtypes=True).then_inc(consts, 1)
                nc.gpsimd.iota(expert_no[:], pattern=[[1, E]], base=0, channel_multiplier=0,
                               allow_small_or_imprecise_dtypes=True).then_inc(consts, 1)
                nc.gpsimd.iota(rank[:], pattern=[[-1, E]], base=E, channel_multiplier=0,
                               allow_small_or_imprecise_dtypes=True).then_inc(consts, 1)
                pool.wait_ge(consts, 10)
                nc.gpsimd.affine_select(out=before[:], in_=before[:], compare_op=ALU.is_ge, fill=1.0, base=0,
                                        pattern=[[-1, P]], channel_multiplier=1).then_inc(consts, 1)

            @block.scalar
            def _(act):
                act.wait_ge(consts, 11)
                @looped(act, B)
                def _(b):
                    act.wait_ge(mv_done, b * J + J)
                    act.wait_ge(rstd_done, b)
                    nc.scalar.activation(std[:], mv[:, :, 1], ACT.Sqrt, bias=epst[:, 0:1]).then_inc(std_done, 1)
                    for i in range(4):
                        act.wait_ge(turned, b * 8 + 2 * i + 1)
                        act.wait_ge(logits_done, b * J)
                        nc.scalar.copy(xT[:, 0, 4 * i:4 * i + 4], tp[:, 0].rearrange("d (j p) -> d j p", p=P)).then_inc(turn_free, 1)
                act.wait_ge(shift_ready, 1)
                nc.scalar.activation(ex[:], shifted[:], ACT.Exp).then_inc(exp_done, 1)

            @block.tensor
            def _(pe):
                pe.wait_ge(gw_loaded, 16)
                pe.wait_ge(consts, 11)
                @looped(pe, B)
                def _(b):
                    for i in range(4):
                        for half in range(2):
                            pe.wait_ge(xn_done, b * J + 4 * i + 4)
                            pe.wait_ge((turn_free, xT_done)[half], b * 4 + i)
                            for j in range(4):
                                last = nc.tensor.transpose(tp[:, half, j * P:(j + 1) * P],
                                                           xn[:, 4 * i + j, half * P:(half + 1) * P], ident[:])
                            last.then_inc(turned, 1)
                    pe.wait_ge(turn_free, b * 4 + 4)
                    pe.wait_ge(xT_done, b * 4 + 4)
                    for j in range(J):
                        for k in range(KD):
                            last = nc.tensor.matmul(logits[:, ds(b * J + j, 1)].rearrange("p o e -> p (o e)"),
                                                    xT[:, k, j], gw[:, k], start=(k == 0), stop=(k == KD - 1))
                        last.then_inc(logits_done, 1)
                pe.wait_ge(sums_ready, 1)
                cols = sums.rearrange("p k b e -> p (k b e)")
                nc.tensor.matmul(sums_before[:, 0], before[:], cols, start=True, stop=True)
                nc.tensor.matmul(sums_before[:, 1], ones[:], cols, start=True, stop=True).then_inc(ranked, 1)
                nc.tensor.matmul(table[:], zerob[:], zerob[:, 0:1].to_broadcast([P, 2 * TILES]), start=True, stop=False)
                @looped(pe, 2 * B)
                def _(n):
                    for j in range(J):
                        pe.wait_ge(hot_tiles, n * J + j + 1)
                        nc.tensor.matmul(table[:], is_lane[:, j % LS], is_tile[:, j % LS].rearrange("p a t -> p (a t)"),
                                         start=False, stop=False).then_inc(tabled, 1)
                nc.tensor.matmul(table[:], zerob[:], zerob[:, 0:1].to_broadcast([P, 2 * TILES]), start=False, stop=True).then_inc(table_done, 1)

            @block.vector
            def _(dve):
                @looped(dve, B)
                def _(b):
                    dve.wait_ge(mv_done, b * J)
                    for j in range(J):
                        nc.vector.bn_stats(stats[:, j], X[:, ds(b, 1), j].rearrange("p o d -> p (o d)")).then_inc(stat_done, 1)
                    dve.wait_ge(xn_done, b * J)
                    for j in range(J):
                        dve.wait_ge(stat_done, b * J + j + 1).then_inc(passed, 1)
                        nc.vector.bn_aggr(mv[:, j], stats[:, j]).then_inc(mv_done, 1)
                    dve.wait_ge(std_done, b + 1)
                    nc.vector.reciprocal(rstd[:], std[:]).then_inc(rstd_done, 1)
                    dve.wait_ge(rstd_done, b + 1)
                    dve.wait_ge(turned, b * 8)
                    dve.wait_ge(rows_out, b * 16)
                    for j in range(J):
                        nc.vector.tensor_scalar(xn[:, j], X[:, ds(b, 1), j].rearrange("p o d -> p (o d)"),
                                                mv[:, j, 0:1], rstd[:, j:j + 1],
                                                ALU.subtract, ALU.mult).then_inc(xn_done, 1)
                    for i in range(4):
                        dve.wait_ge(turned, b * 8 + 2 * i + 2)
                        dve.wait_ge(logits_done, b * J)
                        nc.vector.tensor_copy(xT[:, 1, 4 * i:4 * i + 4], tp[:, 1].rearrange("d (j p) -> d j p", p=P)).then_inc(xT_done, 1)

                v = nc.vector
                done = [0]

                def then(ins):
                    done[0] += 1
                    ins.then_inc(step, 1)
                    dve.wait_ge(step, done[0])

                def wide(a):
                    return a.unsqueeze(2).to_broadcast(small)

                def over(a):
                    return a.unsqueeze(1).to_broadcast(small)
                dve.wait_ge(logits_done, C64)
                dve.wait_ge(consts, 11)
                then(v.tensor_reduce(top[:], logits[:], AXX, ALU.max))
                v.tensor_tensor(shifted[:], logits[:], wide(top[:]), ALU.subtract).then_inc(shift_ready, 1)
                dve.wait_ge(exp_done, 1)
                then(v.tensor_reduce(total[:], ex[:], AXX, ALU.add))
                then(v.reciprocal(rtotal[:], total[:]))
                then(v.tensor_tensor(pr[:], ex[:], wide(rtotal[:]), ALU.mult))
                for k in range(2):
                    then(v.tensor_reduce(prob[:, k], pr[:], AXX, ALU.max))
                    then(v.tensor_tensor(eq[:], pr[:], wide(prob[:, k]), ALU.is_equal))
                    then(v.tensor_tensor(cand[:], eq[:], over(rank[:]), ALU.mult))
                    then(v.tensor_reduce(best[:], cand[:], AXX, ALU.max))
                    then(v.tensor_tensor(hot[:, k], cand[:], wide(best[:]), ALU.is_equal))
                    if k == 0:
                        then(v.scalar_tensor_tensor(out=pr[:], in0=hot[:, k], scalar=-2.0, in1=pr[:],
                                                    op0=ALU.mult, op1=ALU.add))
                then(v.tensor_tensor(total[:], prob[:, 0], prob[:, 1], ALU.add))
                then(v.reciprocal(rtotal[:], total[:]))
                for k in range(2):
                    then(v.tensor_tensor(W[:, k], prob[:, k], rtotal[:], ALU.mult))
                src = hot.rearrange("p k (b j) e -> p (k b) j e", j=J)
                for n, d in enumerate((1, 2, 4, 8)):
                    dst = count[:, n % 2]
                    then(v.tensor_copy(dst[:, :, 0:d], src[:, :, 0:d]))
                    then(v.tensor_tensor(dst[:, :, d:], src[:, :, d:], src[:, :, 0:J - d], ALU.add))
                    src = dst
                cnt = src
                v.tensor_copy(sums.rearrange("p k b e -> p (k b) e"), cnt[:, :, J - 1]).then_inc(sums_ready, 1)
                dve.wait_ge(ranked, 1)
                before_p = sums_before[:, 0].rearrange("p (k b e) -> p k b e", k=2, b=B)
                whole = sums_before[:, 1].rearrange("p (k b e) -> p k b e", k=2, b=B)
                then(v.memset(offset[:, :, 0], 0.0))
                for b in range(1, B):
                    then(v.tensor_tensor(offset[:, :, b], whole[:, :, b - 1], offset[:, :, b - 1], ALU.add))
                then(v.tensor_tensor(offset[:], before_p, offset[:], ALU.add))
                other = count[:, 0]
                then(v.tensor_tensor(other, cnt, offset.rearrange("p k b e -> p (k b) e").unsqueeze(2)
                                     .to_broadcast([P, 2 * B, J, E]), ALU.add))
                hot8 = hot.rearrange("p k (b j) e -> p (k b) j e", j=J)
                then(v.tensor_tensor(cnt, other, hot8, ALU.mult))
                then(v.tensor_reduce(place.rearrange("p k (b j) -> p (k b) j", j=J), cnt, AXX, ALU.add))
                for k in range(2):
                    then(v.tensor_tensor(cand[:], hot[:, k], over(expert_no[:]), ALU.mult))
                    then(v.tensor_reduce(eno[:, k], cand[:], AXX, ALU.add))
                then(v.tensor_scalar(valid[:], place[:], float(CAP) + 0.5, None, ALU.is_lt))
                then(v.tensor_tensor(W[:], W[:], valid[:], ALU.mult))
                then(v.scalar_tensor_tensor(out=slot[:], in0=eno[:], scalar=2.0 * CAP, in1=place[:],
                                            op0=ALU.mult, op1=ALU.add))
                then(v.tensor_scalar(slot[:, 1], slot[:, 1], float(CAP), None, ALU.add))
                then(v.tensor_tensor(slot[:], slot[:], valid[:], ALU.mult))
                then(v.tensor_scalar(place[:], slot[:], -1.0, None, ALU.add))
                then(v.tensor_copy(slot_i[:], place[:]))
                then(v.tensor_scalar(slot[:], place[:], 0.0, None, ALU.max))
                then(v.tensor_copy(slotof[:], slot[:]))
                then(v.tensor_scalar(hi_i[:], slot_i[:], 7, None, ALU.arith_shift_right))
                then(v.tensor_scalar(lo_i[:], slot_i[:], P - 1, None, ALU.bitwise_and))
                then(v.tensor_copy(hi[:], hi_i[:]))
                then(v.tensor_copy(lo[:], lo_i[:]))
                hi_c, lo_c, no_c = (a.rearrange("p k c -> p (k c)") for a in (hi, lo, col_no))
                @looped(dve, 2 * B)
                def _(n):
                    for j in range(J):
                        if j < LS:
                            dve.wait_ge(tabled, n * J)
                        else:
                            dve.wait_ge(tabled, n * J + j - LS + 1)
                        at = ds(n * J + j, 1)
                        v.tensor_scalar(is_lane[:, j % LS], lane[:], lo_c[:, at], None, ALU.is_equal)
                        v.tensor_scalar(is_tile[:, j % LS, 0], tile_no[:], hi_c[:, at], part_no[:, 0:1],
                                        ALU.is_equal, ALU.mult)
                        v.tensor_scalar(is_tile[:, j % LS, 1], tile_no[:], hi_c[:, at], no_c[:, at],
                                        ALU.is_equal, ALU.mult).then_inc(hot_tiles, 1)
                dve.wait_ge(table_done, 1)
                then(v.tensor_copy(tabc[:], table[:, TILES:2 * TILES]))
                then(v.scalar_tensor_tensor(out=tabr[:], in0=table[:, 0:TILES], scalar=float(C64), in1=tabc[:],
                                            op0=ALU.mult, op1=ALU.add))
                then(v.tensor_copy(rowof[:], tabr[:]))


def build_experts(nc, c, wi_gate, wi_up, wo, xrows, yrows):
    ident, rowof = c["ident"], c["rowof"]
    FT = F // P
    with ExitStack() as ctx:
        def sb(n, s, t): return ctx.enter_context(nc.sbuf_tensor(n, s, t))
        def ps(n, s, t): return ctx.enter_context(nc.psum_tensor(n, s, t))
        def sem(n): return ctx.enter_context(nc.semaphore(n))
        passed = sem("passed3")
        wg, wu = sb("wg", [P, 2, KD, F], F32), sb("wu", [P, 2, KD, F], F32)
        wd = sb("wd", [P, 2, FT, D], F32)
        rows = sb("rows", [P, 2, ET], I32)
        xg = sb("xg", [P, 2, CT, D], F32)
        xgT = sb("xgT", [P, 2, KD, CH], F32)
        act_g = sb("act_g", [P, 2, CH], F32)
        hid = sb("hid", [P, 2, FT, CH], F32)
        ysb = sb("ysb", [P, 2, CT, D], F32)
        xp = ps("xp", [P, KD, CH], F32)
        gu = ps("gu", [P, 2, 2, CH], F32)
        yp = ps("yp", [P, 2, CH], F32)
        w_in = [sem(f"w_in{i}") for i in range(2)]
        x_in = [sem(f"x_in{i}") for i in range(2)]
        y_out = [sem(f"y_out{i}") for i in range(2)]
        rows_ready, x_turned, xT0, xT1, gu_ready, silu_done, hid_ready, y_ready, y_put0, y_put1 = (sem("e_" + n) for n in
            ("rows_ready", "x_turned", "xT0", "xT1", "gu_ready", "silu_done", "hid_ready", "y_ready", "y_put0", "y_put1"))

        def loop_experts(eng, body):
            body(0, 0, True)
            body(0, 1, True)
            with eng.Fori(1, E // 2 - 1) as pr:
                body(pr, 0, True)
                body(pr, 1, True)
            body(E // 2 - 1, 0, True)
            body(E // 2 - 1, 1, False)

        with nc.Block() as block:
            @block.sync
            def _(sp):
                def load(e, par):
                    for dst, src in ((wg, wi_gate), (wu, wi_up), (wd, wo)):
                        sp.dma_start(dst[:, par], src[ds(e, 1)].rearrange("o p k f -> p (o k) f")).then_inc(w_in[par], 16)

                def body(pr, par, more):
                    e = pr * 2 + par
                    if more:
                        sp.wait_ge(y_ready, e * EC * CT)
                        load(e + 1, 1 - par)
                    for ch in range(EC):
                        n = e * EC + ch
                        slot = (par * EC + ch) % 2
                        sp.wait_ge(y_put0, n * 2 + 2)
                        sp.wait_ge(y_put1, n * 2 + 2)
                        sp.dma_start(yrows.rearrange("(n t p) d -> n p t d", t=CT, p=P)[ds(n, 1)].rearrange("o p t d -> p (o t) d"),
                                     ysb[:, slot]).then_inc(y_out[slot], 16)
                load(0, 0)
                loop_experts(sp, body)
                sp.wait_ge(y_out[0], 16 * E * EC // 2)
                sp.wait_ge(y_out[1], 16 * E * EC // 2)

            @block.gpsimd
            def _(pool):
                def body(pr, par, more):
                    e = pr * 2 + par
                    pool.wait_ge(x_turned, e * EC).then_inc(passed, 1)
                    nc.gpsimd.tensor_copy(rows[:, par], rowof[:, ds(e * ET, ET)]).then_inc(rows_ready, 1)
                    pool.wait_ge(rows_ready, e + 1)
                    for ch in range(EC):
                        i = par * EC + ch
                        n = e * EC + ch
                        if i < 2:
                            pool.wait_ge(x_turned, pr * 2 * EC).then_inc(passed, 1)
                        else:
                            pool.wait_ge(x_turned, n - 1).then_inc(passed, 1)
                        for t in range(CT):
                            nc.gpsimd.indirect_dma_start(
                                out=xg[:, i % 2, t], out_offset=None, in_=xrows,
                                in_offset=bass.IndirectOffsetOnAxis(ap=rows[:, par, ch * CT + t:ch * CT + t + 1].bitcast(U32), axis=0),
                            ).then_inc(x_in[i % 2], 16)
                loop_experts(pool, body)

            @block.scalar
            def _(act):
                def turn(pr, i):
                    act.wait_ge(x_turned, pr * 2 * EC + i + 1)
                    nc.scalar.copy(xgT[:, i % 2, 0], xp[:, 0]).then_inc(xT0, 1)

                def body(pr, par, more):
                    for ch in range(EC):
                        i = par * EC + ch
                        n = pr * 2 * EC + i
                        for f in range(FT):
                            act.wait_ge(gu_ready, n * FT + f + 1)
                            act.wait_ge(hid_ready, max(n * FT + f - 1, 0) if isinstance(n, int) else
                                        (n * FT + f - 1 if i or f > 1 else n * FT))
                            nc.scalar.activation(act_g[:, f % 2], gu[:, f % 2, 0], ACT.Silu).then_inc(silu_done, 1)
                        if more or ch < EC - 1:
                            turn(pr, i + 1)
                        for t in (0, 2):
                            act.wait_ge(y_ready, n * CT + t + 1)
                            act.wait_ge(y_out[i % 2], (pr * EC + i // 2) * 16)
                            nc.scalar.copy(ysb[:, i % 2, t], yp[:, 0, 0:D]).then_inc(y_put0, 1)
                turn(0, 0)
                loop_experts(act, body)

            @block.vector
            def _(dve):
                def turn(pr, i):
                    dve.wait_ge(x_turned, pr * 2 * EC + i + 1)
                    nc.vector.tensor_copy(xgT[:, i % 2, 1], xp[:, 1]).then_inc(xT1, 1)

                def body(pr, par, more):
                    for ch in range(EC):
                        i = par * EC + ch
                        n = pr * 2 * EC + i
                        for f in range(FT):
                            dve.wait_ge(silu_done, n * FT + f + 1)
                            if f == 0:
                                dve.wait_ge(y_ready, (n - 1) * CT if i > 1 else pr * 2 * EC * CT)
                            nc.vector.tensor_tensor(hid[:, i % 2, f], act_g[:, f % 2], gu[:, f % 2, 1],
                                                    ALU.mult).then_inc(hid_ready, 1)
                        if more or ch < EC - 1:
                            turn(pr, i + 1)
                        for t in (1, 3):
                            dve.wait_ge(y_ready, n * CT + t + 1)
                            dve.wait_ge(y_out[i % 2], (pr * EC + i // 2) * 16)
                            nc.vector.tensor_copy(ysb[:, i % 2, t], yp[:, 1, 0:D]).then_inc(y_put1, 1)
                turn(0, 0)
                loop_experts(dve, body)

            @block.tensor
            def _(pe):
                mm = nc.tensor.matmul

                def turn(pr, i):
                    n = pr * 2 * EC + i
                    pe.wait_ge(x_in[i % 2], (pr * EC + i // 2 + 1) * 16 * CT)
                    pe.wait_ge(xT0, n)
                    pe.wait_ge(xT1, n)
                    for k in range(KD):
                        for t in range(CT):
                            last = nc.tensor.transpose(xp[:, k, t * P:(t + 1) * P], xg[:, i % 2, t, k * P:(k + 1) * P], ident[:])
                    last.then_inc(x_turned, 1)

                def body(pr, par, more):
                    pe.wait_ge(w_in[par], (pr + 1) * 48)
                    for ch in range(EC):
                        i = par * EC + ch
                        n = pr * 2 * EC + i
                        pe.wait_ge(xT0, n + 1)
                        pe.wait_ge(xT1, n + 1)
                        for f in range(FT):
                            if i or f > 1:
                                pe.wait_ge(hid_ready, n * FT + f - 1)
                            else:
                                pe.wait_ge(hid_ready, n * FT)
                            for a, w in ((0, wg), (1, wu)):
                                for k in range(KD):
                                    last = mm(gu[:, f % 2, a], w[:, par, k, f * P:(f + 1) * P], xgT[:, i % 2, k],
                                              start=(k == 0), stop=(k == KD - 1))
                            last.then_inc(gu_ready, 1)
                        if more or ch < EC - 1:
                            turn(pr, i + 1)
                        pe.wait_ge(hid_ready, (n + 1) * FT)
                        for t in range(CT):
                            pe.wait_ge((y_put0, y_put1)[t % 2], n * 2 + t // 2)
                            for f in range(FT):
                                last = mm(yp[:, t % 2, 0:D], hid[:, i % 2, f, t * P:(t + 1) * P], wd[:, par, f],
                                          start=(f == 0), stop=(f == FT - 1))
                            last.then_inc(y_ready, 1)
                turn(0, 0)
                loop_experts(pe, body)


def build_combine(nc, c, yrows, out):
    X, slotof, W = c["X"], c["slotof"], c["W"]
    with ExitStack() as ctx:
        def sb(n, s, t): return ctx.enter_context(nc.sbuf_tensor(n, s, t))
        def sem(n): return ctx.enter_context(nc.semaphore(n))
        GS = 4
        slots = sb("slots", [P, 2, 2, J], I32)
        yg = sb("yg", [P, GS, 2, D], F32)
        wcol = sb("wcol", [P, 2, 2, J], F32)
        y_in = [sem(f"y_in{i}") for i in range(GS)]
        slots_ready, first_added, added, out_done = sem("slots_ready"), sem("first_added"), sem("c_added"), sem("out_done")
        with nc.Block() as block:
            @block.gpsimd
            def _(pool):
                for b in range(B):
                    for j in range(J):
                        n = b * J + j
                        if n >= GS:
                            pool.wait_ge(added, n - GS + 1)
                        for k in range(2):
                            nc.gpsimd.indirect_dma_start(
                                out=yg[:, n % GS, k], out_offset=None, in_=yrows,
                                in_offset=bass.IndirectOffsetOnAxis(ap=slotof[:, k, n:n + 1].bitcast(U32), axis=0),
                            ).then_inc(y_in[n % GS], 16)

            @block.vector
            def _(dve):
                for b in range(B):
                    for j in range(J):
                        n = b * J + j
                        dve.wait_ge(y_in[n % GS], (n // GS + 1) * 32)
                        for k in range(2):
                            if k:
                                dve.wait_ge(first_added, n + 1)
                            nc.vector.scalar_tensor_tensor(out=X[:, b, j], in0=yg[:, n % GS, k], scalar=W[:, k, n:n + 1],
                                                           in1=X[:, b, j], op0=ALU.mult, op1=ALU.add).then_inc(
                                                               (first_added, added)[k], 1)

            @block.sync
            def _(sp):
                for b in range(B):
                    sp.wait_ge(added, (b + 1) * J)
                    sp.dma_start(out[b], X[:, b]).then_inc(out_done, 16)
                sp.wait_ge(out_done, 16 * B)


def build(nc, t):
    qparts = nc.dram_tensor("qparts", [3, B * D, S], BF16, kind="Internal").ap()
    kparts = nc.dram_tensor("kparts", [3, B * D, S], BF16, kind="Internal").ap()
    vstore = nc.dram_tensor("vstore", [NQ, P, J, QH * VW], F32, kind="Internal").ap()
    xrows = nc.dram_tensor("xrows", [B * S, D], F32, kind="Internal").ap()
    yrows = nc.dram_tensor("yrows", [SLOTS, D], F32, kind="Internal").ap()
    with ExitStack() as ctx:
        def sb(n, s, dt): return ctx.enter_context(nc.sbuf_tensor(n, s, dt))
        c = {"X": sb("X", [P, B, J, D], F32), "wsum": sb("wsum", [P, B * D], F32),
             "rowof": sb("rowof", [P, TILES], I32), "slotof": sb("slotof", [P, 2, C64], I32),
             "W": sb("W", [P, 2, C64], F32)}
        c["ident"], c["identb"], c["maskb"] = build_constants(nc, ctx)
        build_project(nc, c, t["x"], t["wq"], t["wk"], t["wv"], t["w_out"], qparts, kparts, vstore)
        build_attend(nc, c, qparts, kparts, vstore)
        build_route(nc, c, t["gate_w"], xrows)
        build_experts(nc, c, t["wi_gate"], t["wi_up"], t["wo"], xrows, yrows)
        build_combine(nc, c, yrows, t["out"])


def kernel(L0_attn_x, L0_attn_W_qkv, L0_attn_W_out, L0_ffn_gate_w, L0_ffn_wi_gate, L0_ffn_wi_up, L0_ffn_wo):
    import concourse.bacc as bacc
    from concourse.bass_utils import run_bass_kernel_spmd

    def lay(a, *shape_and_order):
        shape, order = shape_and_order
        return np.ascontiguousarray(np.asarray(a).reshape(shape).transpose(order))

    w = np.asarray(L0_attn_W_qkv)
    arrays = {"x": np.asarray(L0_attn_x).reshape(B, P, J, D)}
    for i, n in enumerate(("wq", "wk", "wv")):
        arrays[n] = lay(w[:, :, i * HD:(i + 1) * HD], (NH, KD, P, HD), (2, 1, 0, 3)).reshape(P, KD, D)
    arrays["w_out"] = lay(L0_attn_W_out, (KD, P, D), (1, 0, 2))
    arrays["gate_w"] = lay(L0_ffn_gate_w, (E, KD, P), (2, 1, 0))
    arrays["wi_gate"] = lay(L0_ffn_wi_gate, (E, F, KD, P), (0, 3, 2, 1))
    arrays["wi_up"] = lay(L0_ffn_wi_up, (E, F, KD, P), (0, 3, 2, 1))
    arrays["wo"] = lay(L0_ffn_wo, (E, D, F // P, P), (0, 3, 2, 1))
    nc = bacc.Bacc("TRN2", target_bir_lowering=False, num_devices=1)
    t = {n: nc.dram_tensor(n + "_in", a.shape, mybir.dt.from_np(a.dtype), kind="ExternalInput").ap()
         for n, a in arrays.items()}
    t["out"] = nc.dram_tensor("out", (B, P, J, D), F32, kind="ExternalOutput").ap()
    build(nc, t)
    r = run_bass_kernel_spmd(nc, [{n + "_in": np.ascontiguousarray(a) for n, a in arrays.items()}], core_ids=[0])
    return r.results[0]["out"].reshape(B, S, D)
```

```python
from contextlib import ExitStack

import numpy as np
import concourse.bass as bass
from concourse import mybir

F32 = mybir.dt.float32
BF16 = mybir.dt.bfloat16
F32R = mybir.dt.float32r
I32 = mybir.dt.int32
U32 = mybir.dt.uint32
ALU = mybir.AluOpType
ACT = mybir.ActivationFunctionType
AXX = mybir.AxisListType.X
ds = bass.ds

P = 128
B, S, D = 4, 2048, 256
NH, HD = 16, 16
J = S // P
KD = D // P
QH = 4
NQ = B * NH // QH
CH = 512
NC = S // CH
EPS = 1e-5
MASKED = -4.0e10
SCALE = HD ** -0.5
E, F, CAP = 8, 1024, 1280
EPS_ROWS = 96
MROWS = 3
KROWS = EPS_ROWS + MROWS
VW = 32


def steps_of_quad():
    return [(qc, kt) for qc in range(NC) for kt in range(4 * qc + 4)]


def max_units():
    units = []
    for g in range(NC):
        for t4 in range(4):
            for part in range(g):
                units += [(g, t4, h, 1, part, CH) for h in range(QH)]
            w = (t4 + 1) * P
            n = {0: 4, 1: 2, 2: 1, 3: 1}[t4]
            units += [(g, t4, h, n, g, w) for h in range(0, QH, n)]
    return units


STEPS = steps_of_quad()
NS = len(STEPS)
UNITS = max_units()
NU = len(UNITS)
FIRST_UNITS = sum(u[0] < NC - 1 for u in UNITS)
LAST_UNIT_OF_GROUP = [max(i for i, u in enumerate(UNITS) if u[0] == g) for g in range(NC)]
LAG = 2


FB = SB = 3
LOAD_NS = 12000.0
AHEAD = 1000.0
DEFER = 8


def quad_events():
    ev, later = [], []
    order = [i for i in range(NU) if UNITS[i][0] == NC - 1] + [i for i in range(NU) if UNITS[i][0] < NC - 1]
    t = {"pe": 0.0, "dve": 0.0}

    def fill():
        while order and t["dve"] < t["pe"] + AHEAD and (UNITS[order[0]][0] == NC - 1 or t["pe"] > LOAD_NS):
            i = order.pop(0)
            g, t4, h, n, part, w = UNITS[i]
            ev.append(("unit", i))
            t["pe"] += n * w / 2.4 + (n * 56.0 if part == g else 0.0)
            t["dve"] = max(t["dve"], t["pe"]) + n * w / 0.96 + 66.0
            if i in LAST_UNIT_OF_GROUP:
                ev.append(("finish", g))
                t["dve"] += 250.0
                later.append([DEFER, "turn_max", g])
                later.append([DEFER, "take_max", g])

    def tick():
        for x in later:
            x[0] -= 1
        while later and later[0][0] <= 0:
            _, kind, g = later.pop(0)
            ev.append((kind, g))
            t["dve"] += {"take_max": 700.0, "take_out": 1100.0, "take_out_prev": 1100.0}.get(kind, 0.0)

    def weigh(s, suffix):
        qc, kt = STEPS[s]
        ev.append(("weigh" + suffix, s))
        t["pe"] += 740.0 * (CH - max(kt - 4 * qc, 0) * P) / CH
        if kt == 4 * qc + 3:
            ev.append(("read_out" + suffix, qc))
            later.append([DEFER, "turn_out" + suffix, qc])
            later.append([DEFER, "take_out" + suffix, qc])

    for s in range(NS):
        qc, kt = STEPS[s]
        for h in range(QH):
            ev.append(("score", (s, h)))
            t["pe"] += (CH - max(kt - 4 * qc, 0) * P) / 2.4 + 3
            tick()
            fill()
        weigh(s - LAG if s >= LAG else NS - LAG + s, "" if s >= LAG else "_prev")
        tick()
        fill()
    left = len(order)
    while order:
        t["dve"] = t["pe"]
        fill()
        tick()
    while later:
        tick()
    return ev, left, t


EVENTS, _, _ = quad_events()
TAIL = [e for e in EVENTS if e[0].endswith("_prev")]
TURNS = [e for e in EVENTS if e[0].startswith("turn_")]
assert TURNS[0] == ("turn_out_prev", NC - 1)


def looped(eng, n):
    def run(body):
        body(0)
        with eng.Fori(1, n) as i:
            body(i)
    return run


def build_constants(nc, ctx):
    ident = ctx.enter_context(nc.sbuf_tensor("ident", [P, P], F32))
    identb = ctx.enter_context(nc.sbuf_tensor("identb", [P, P], BF16))
    maskb = ctx.enter_context(nc.sbuf_tensor("maskb", [P, P], BF16))
    made = ctx.enter_context(nc.semaphore("constants_made"))
    with nc.Block() as block:
        @block.gpsimd
        def _(pool):
            nc.gpsimd.memset(ident[:], 0.0).then_inc(made, 1)
            nc.gpsimd.memset(maskb[:], 0.0).then_inc(made, 1)
            pool.wait_ge(made, 2)
            nc.gpsimd.affine_select(out=ident[:], in_=ident[:], compare_op=ALU.not_equal, fill=1.0, base=0,
                                    pattern=[[-1, P]], channel_multiplier=1).then_inc(made, 1)
            nc.gpsimd.affine_select(out=maskb[:], in_=maskb[:], compare_op=ALU.is_ge, fill=MASKED, base=0,
                                    pattern=[[-1, P]], channel_multiplier=1).then_inc(made, 1)
            pool.wait_ge(made, 4)
            nc.gpsimd.tensor_copy(identb[:], ident[:]).then_inc(made, 1)
            pool.wait_ge(made, 5)
    return ident, identb, maskb


def build_project(nc, c, x, wq, wk, wv, w_out, qparts, kparts, vstore):
    X, wsum, ident = c["X"], c["wsum"], c["ident"]
    with ExitStack() as ctx:
        def sb(n, s, t): return ctx.enter_context(nc.sbuf_tensor(n, s, t))
        def ps(n, s, t): return ctx.enter_context(nc.psum_tensor(n, s, t))
        def sem(n): return ctx.enter_context(nc.semaphore(n))
        passed = sem("passed0")
        wqk = sb("wqk", [P, 2, KD, D], F32)
        wvs = sb("wvs", [P, KD, D], F32)
        wos = sb("wos", [P, KD, D], F32)
        ones = sb("ones", [P, P], F32)
        stats = sb("stats", [P, J, 6], F32)
        mv = sb("mv", [P, J, 2], F32)
        std = sb("std", [P, J], F32)
        rstd = sb("rstd", [P, J], F32)
        xn = sb("xn", [P, J, D], F32)
        xT = sb("xT", [P, KD, S], F32)
        parts = sb("parts", [P, 2, 3, CH], BF16)
        rest = sb("rest", [P, 2, CH], F32)
        vst = sb("vst", [P, 2, NC, 4, QH * VW], F32)
        tp = ps("tp", [P, 2, CH], F32)
        pj = ps("pj", [P, 3, CH], F32)
        vp = ps("vp", [P, 2, CH], F32)
        wp = ps("wp", [P, CH], F32)
        epst = sb("epst", [P, 1], F32)

        w_loaded, x_loaded = sem("w_loaded"), sem("x_loaded")
        ones_made, v_consts = sem("ones_made"), sem("v_consts")
        stat_done, mv_done, std_done, rstd_done, xn_done = (sem(n) for n in
                                                           ("stat_done", "mv_done", "std_done", "rstd_done", "xn_done"))
        turned, turn_free, xT_done = sem("turned"), sem("turn_free"), sem("xT_done")
        proj_done, proj_free, part1, left1, part2, part3 = (sem(n) for n in
            ("proj_done", "proj_free", "part1", "left1", "part2", "part3"))
        parts_out = [sem(f"parts_out{i}") for i in range(2)]
        v_done, v_free, v_put = sem("v_done"), sem("v_free"), sem("v_put")
        v_out = [sem(f"v_out{i}") for i in range(2)]
        wsum_done, wsum_put = sem("wsum_done"), sem("wsum_put")
        NG = 2 * KD * NC
        groups = [(w, half, ch) for w in range(2) for ch in range(NC) for half in range(2)]

        with nc.Block() as block:
            @block.sync
            def _(sp):
                sp.dma_start(wqk[:, 0], wq).then_inc(w_loaded, 16)
                sp.dma_start(wqk[:, 1], wk).then_inc(w_loaded, 16)
                sp.dma_start(wvs[:], wv).then_inc(w_loaded, 16)
                sp.dma_start(wos[:], w_out).then_inc(w_loaded, 16)
                sp.dma_start(X[:, 0], x[0]).then_inc(x_loaded, 16)
                sp.wait_ge(x_loaded, 16)
                for b in range(1, B):
                    sp.dma_start(X[:, b], x[b]).then_inc(x_loaded, 16)
                    sp.wait_ge(x_loaded, 16 * b + 16)
                @looped(sp, B)
                def _(b):
                    for i, (w, half, ch) in enumerate(groups):
                        dst = (qparts, kparts)[w]
                        sp.wait_ge(part3, b * NG + i + 1)
                        for qd in range(2):
                            sp.dma_start(dst[ds(b * 4 + half * 2 + qd, 1), ch].rearrange("o r i (h s) -> (o i h) r s", h=QH),
                                         parts[64 * qd:64 * qd + 64, i % 2]).then_inc(parts_out[i % 2], 16)
                    for g in range(4):
                        sp.wait_ge(v_put, b * J + 4 * g + 4)
                        sp.dma_start(vstore[ds(b * 4, 4), :, 4 * g:4 * g + 4].rearrange("q p k w -> p q (k w)"),
                                     vst[:, g % 2].rearrange("p q k w -> p q (k w)")).then_inc(v_out[g % 2], 16)
                sp.wait_ge(parts_out[0], 32 * B * NG // 2)
                sp.wait_ge(parts_out[1], 32 * B * NG // 2)
                sp.wait_ge(v_out[0], 16 * B * 2)
                sp.wait_ge(v_out[1], 16 * B * 2)

            @block.gpsimd
            def _(pool):
                nc.gpsimd.memset(ones[:], 1.0).then_inc(ones_made, 1)
                nc.gpsimd.memset(epst[:], EPS).then_inc(ones_made, 1)
                v5 = vst.rearrange("p a q k (h w) -> p (a q k h) w", w=VW)
                nc.gpsimd.memset(v5[:, :, HD:VW], 0.0).then_inc(v_consts, 1)
                pool.wait_ge(v_consts, 1)
                nc.gpsimd.memset(v5[:, :, HD:HD + 1], 1.0).then_inc(v_consts, 1)
                @looped(pool, B)
                def _(b):
                    for i in range(NG):
                        pool.wait_ge(left1, b * NG + i + 1).then_inc(passed, 1)
                        nc.gpsimd.tensor_copy(parts[:, i % 2, 1], rest[:, i % 2]).then_inc(part2, 1)
                        pool.wait_ge(part2, b * NG + i + 1)
                        nc.gpsimd.tensor_tensor(parts[:, i % 2, 2], rest[:, i % 2], parts[:, i % 2, 1],
                                                ALU.subtract).then_inc(part3, 1)

            @block.scalar
            def _(act):
                act.wait_ge(ones_made, 2)
                @looped(act, B)
                def _(b):
                    act.wait_ge(mv_done, b * J + J)
                    act.wait_ge(rstd_done, b)
                    nc.scalar.activation(std[:], mv[:, :, 1], ACT.Sqrt, bias=epst[:, 0:1]).then_inc(std_done, 1)
                    for i in range(4):
                        act.wait_ge(turned, b * 8 + 2 * i + 1)
                        act.wait_ge(proj_done, b * NG)
                        act.wait_ge(v_done, b * J)
                        nc.scalar.copy(xT[:, 0].rearrange("d (p j) -> d j p", j=J)[:, 4 * i:4 * i + 4],
                                       tp[:, 0].rearrange("d (j p) -> d j p", p=P)).then_inc(turn_free, 1)
                    for i in range(NG):
                        act.wait_ge(proj_done, b * NG + i + 1)
                        act.wait_ge(parts_out[i % 2], (b * (NG // 2) + i // 2) * 32)
                        nc.scalar.copy(parts[:, i % 2, 0], pj[:, i % 2]).then_inc(part1, 1)

            @block.vector
            def _(dve):
                dve.wait_ge(w_loaded, 64)
                dve.wait_ge(wsum_done, 1)
                for r in range(B):
                    nc.vector.tensor_copy(wsum[:, r * D:(r + 1) * D], wp[:, 0:D]).then_inc(wsum_put, 1)
                @looped(dve, B)
                def _(b):
                    dve.wait_ge(x_loaded, 16 * b + 16)
                    for j in range(J):
                        if j == 0:
                            dve.wait_ge(mv_done, b * J)
                        nc.vector.bn_stats(stats[:, j], X[:, ds(b, 1), j].rearrange("p o d -> p (o d)")).then_inc(stat_done, 1)
                    dve.wait_ge(xn_done, b * J)
                    for j in range(J):
                        dve.wait_ge(stat_done, b * J + j + 1).then_inc(passed, 1)
                        nc.vector.bn_aggr(mv[:, j], stats[:, j]).then_inc(mv_done, 1)
                    dve.wait_ge(std_done, b + 1)
                    nc.vector.reciprocal(rstd[:], std[:]).then_inc(rstd_done, 1)
                    dve.wait_ge(rstd_done, b + 1)
                    dve.wait_ge(turned, b * 8)
                    for j in range(J):
                        nc.vector.tensor_scalar(xn[:, j], X[:, ds(b, 1), j].rearrange("p o d -> p (o d)"),
                                                mv[:, j, 0:1], rstd[:, j:j + 1],
                                                ALU.subtract, ALU.mult).then_inc(xn_done, 1)
                    for i in range(4):
                        dve.wait_ge(turned, b * 8 + 2 * i + 2)
                        dve.wait_ge(proj_done, b * NG)
                        dve.wait_ge(v_done, b * J)
                        nc.vector.tensor_copy(xT[:, 1].rearrange("d (p j) -> d j p", j=J)[:, 4 * i:4 * i + 4],
                                              tp[:, 1].rearrange("d (j p) -> d j p", p=P)).then_inc(xT_done, 1)
                    for i in range(NG):
                        dve.wait_ge(part1, b * NG + i + 1)
                        if i >= 2:
                            dve.wait_ge(part3, b * NG + i - 1)
                        else:
                            dve.wait_ge(part3, b * NG)
                        nc.vector.tensor_tensor(rest[:, i % 2], pj[:, i % 2], parts[:, i % 2, 0],
                                                ALU.subtract).then_inc(left1, 1)
                    dve.wait_ge(v_consts, 2)
                    for kt in range(J):
                        sl = (kt // 4) % 2
                        dve.wait_ge(v_done, b * J + kt + 1)
                        if kt % 4 == 0:
                            dve.wait_ge(v_out[sl], (b * 2 + kt // 8) * 16)
                        nc.vector.tensor_copy(
                            vst[:, sl, :, kt % 4].rearrange("p q (h w) -> p q h w", w=VW)[:, :, :, 0:HD],
                            vp[:, kt % 2, 0:D].rearrange("p (q h w) -> p q h w", q=4, w=HD)).then_inc(v_put, 1)

            @block.tensor
            def _(pe):
                pe.wait_ge(w_loaded, 64)
                pe.wait_ge(ones_made, 2)
                for k in range(KD):
                    last = nc.tensor.matmul(wp[:, 0:D], ones[:], wos[:, k], start=(k == 0), stop=(k == KD - 1))
                last.then_inc(wsum_done, 1)
                @looped(pe, B)
                def _(b):
                    for i in range(4):
                        for half in range(2):
                            pe.wait_ge(xn_done, b * J + 4 * i + 4)
                            if half == 0:
                                pe.wait_ge(turn_free, b * 4 + i)
                            else:
                                pe.wait_ge(xT_done, b * 4 + i)
                            for j in range(4):
                                last = nc.tensor.transpose(tp[:, half, j * P:(j + 1) * P],
                                                           xn[:, 4 * i + j, half * P:(half + 1) * P], ident[:])
                            last.then_inc(turned, 1)
                    pe.wait_ge(turn_free, b * 4 + 4)
                    pe.wait_ge(xT_done, b * 4 + 4)
                    for i, (w, half, ch) in enumerate(groups):
                        if i >= 2:
                            pe.wait_ge(left1, b * NG + i - 1)
                        else:
                            pe.wait_ge(left1, b * NG)
                        for k in range(KD):
                            last = nc.tensor.matmul(pj[:, i % 2], wqk[:, w, k, half * P:(half + 1) * P],
                                                    xT[:, k, ch * CH:(ch + 1) * CH], start=(k == 0), stop=(k == KD - 1))
                        last.then_inc(proj_done, 1)
                    for kt in range(J):
                        pe.wait_ge(v_put, b * J + max(kt - 1, 0))
                        for k in range(KD):
                            last = nc.tensor.matmul(vp[:, kt % 2, 0:D], xT[:, k, kt * P:(kt + 1) * P], wvs[:, k],
                                                    start=(k == 0), stop=(k == KD - 1))
                        last.then_inc(v_done, 1)


def build_attend(nc, c, qparts, kparts, vstore):
    X, wsum, ident, identb, maskb = c["X"], c["wsum"], c["ident"], c["identb"], c["maskb"]
    with ExitStack() as ctx:
        def sb(n, s, t): return ctx.enter_context(nc.sbuf_tensor(n, s, t))
        def ps(n, s, t): return ctx.enter_context(nc.psum_tensor(n, s, t))
        def sem(n): return ctx.enter_context(nc.semaphore(n))
        passed = sem("passed1")
        Q = sb("Q", [P, 2, NC, QH, CH], BF16)
        K = sb("K", [P, 2, NC, QH, CH], BF16)
        V = sb("V", [P, 2, J, QH * VW], F32)
        NP = 4
        probs = sb("probs", [P, NP, QH, CH], F32)
        maxima = sb("maxima", [P, NC, QH, 4, 4], F32)
        negmax = sb("negmax", [P, NC, QH * 4], F32)
        mparts = sb("mparts", [QH * 4, NC, MROWS, P], BF16)
        mrest = sb("mrest", [QH * 4, NC, P], F32)
        outs = sb("outs", [P, NC, CH], F32)
        recip = sb("recip", [P, NC, 4, QH], F32)
        weight = sb("weight", [P, NC, 4, QH], F32)
        addend = sb("addend", [P, NC, 4, QH, J], F32)
        scores = ps("scores", [P, SB, CH], F32)
        fill = ps("fill", [P, FB, CH], F32)
        acc = ps("acc", [P, CH], F32)
        turn = ps("turn", [P, CH], F32)

        loaded = [[sem(f"loaded{i}{g}") for g in range(NC)] for i in range(2)]
        v_loaded = [sem(f"v_loaded{i}") for i in range(2)]
        rows_in = [[sem(f"rows_in{i}{g}") for g in range(NC)] for i in range(2)]
        ones_made = sem("k_ones_made")
        scores_ready, probs_ready, masked, pv_done = (sem(n) for n in ("scores_ready", "probs_ready", "masked", "pv_done"))
        fill_ready, fill_read, negmax_ready = sem("fill_ready"), sem("fill_read"), sem("negmax_ready")
        turned_out, turned_max, outs_ready = sem("turned_out"), sem("turned_max"), sem("outs_ready")
        part1, left1, part2, part3 = sem("m_part1"), sem("m_left1"), sem("m_part2"), sem("m_part3")
        recip_ready, weight_ready, addend_ready, added = (sem(n) for n in
            ("recip_ready", "weight_ready", "addend_ready", "added"))
        ROWS_SENT = 16 * MROWS
        QK_SENT = 16 * 6

        def loop_quads(eng, body):
            body(0, 0, True)
            body(0, 1, True)
            with eng.Fori(1, NQ // 2 - 1) as i:
                body(i, 0, True)
                body(i, 1, True)
            body(NQ // 2 - 1, 0, True)
            body(NQ // 2 - 1, 1, False)

        def events_of(q, more):
            first = isinstance(q, int) and q == 0
            return [e for e in EVENTS if not (first and e[0].endswith("_prev"))
                    and (more or not for_next(e))]

        def for_next(e):
            kind, x = e
            return (kind == "unit" and UNITS[x][0] < NC - 1) or (kind in ("finish", "turn_max", "take_max") and x < NC - 1)

        def split(kind):
            return (kind[:-5], 1) if kind.endswith("_prev") else (kind, 0)

        def columns(s):
            qc, kt = STEPS[s]
            return max(kt - 4 * qc, 0) * P

        def at_least(eng, sem_, n):
            if not isinstance(n, int) or n > 0:
                eng.wait_ge(sem_, n)

        with nc.Block() as block:
            @block.sync
            def _(sp):
                def load(q, par):
                    for g in range(NC):
                        for r, src, copies, dst, store in ((0, 0, 3, Q, qparts), (3, 1, 2, Q, qparts), (5, 2, 1, Q, qparts)):
                            sp.dma_start(dst[16 * r:16 * (r + copies), par, g],
                                         store[ds(q, 1), g, src:src + 1].rearrange("o r i x -> (o r) i x")
                                         .to_broadcast([copies, HD, QH * CH])).then_inc(loaded[par][g], 16)
                        for r, parts in ((0, 3), (3, 2), (5, 1)):
                            sp.dma_start(K[16 * r:16 * (r + parts), par, g],
                                         kparts[ds(q, 1), g, 0:parts].rearrange("o r i x -> (o r i) x")).then_inc(loaded[par][g], 16)

                def load_v(q, par):
                    sp.dma_start(V[:, par], vstore[ds(q, 1)].rearrange("o p k w -> p (o k) w")).then_inc(v_loaded[par], 16)

                def rows(q, par, chunks):
                    for g in chunks:
                        sp.wait_ge(part3, q * NC + g + 1)
                        for r in range(MROWS):
                            sp.dma_start(Q[EPS_ROWS + r:EPS_ROWS + r + 1, par, g].rearrange("o h s -> o (h s)"),
                                         mparts[:, g, r]).then_inc(rows_in[par][g], 16)

                def body(pr, par, more):
                    q = pr * 2 + par
                    if more:
                        at_least(sp, scores_ready, q * NS * QH)
                        load(q + 1, 1 - par)
                        at_least(sp, pv_done, q * NS)
                        load_v(q + 1, 1 - par)
                    rows(q, par, [NC - 1])
                    if more:
                        rows(q + 1, 1 - par, range(NC - 1))

                load(0, 0)
                load_v(0, 0)
                rows(0, 0, range(NC - 1))
                loop_quads(sp, body)

            @block.gpsimd
            def _(pool):
                nc.gpsimd.memset(K[EPS_ROWS:P, :, :, :], 1.0).then_inc(ones_made, 1)

                def max_parts(g, n):
                    pool.wait_ge(left1, n + 1).then_inc(passed, 1)
                    nc.gpsimd.tensor_copy(mparts[:, g, 1], mrest[:, g]).then_inc(part2, 1)
                    pool.wait_ge(part2, n + 1)
                    nc.gpsimd.tensor_tensor(mparts[:, g, 2], mrest[:, g], mparts[:, g, 1],
                                            ALU.subtract).then_inc(part3, 1)

                def mask(q, s):
                    pool.wait_ge(probs_ready, (q * NS + s + 1) * QH).then_inc(passed, 1)
                    c0 = columns(s)
                    diag = probs[:, s % NP, :, c0:c0 + P]
                    nc.gpsimd.affine_select(out=diag, in_=diag, compare_op=ALU.is_ge, fill=0.0, base=0,
                                            pattern=[[0, QH], [1, P]], channel_multiplier=-1).then_inc(masked, 1)

                def add(b, k, q, qc):
                    pool.wait_ge(addend_ready, q * NC + qc + 1)
                    dst = X[:, ds(b, 1)].rearrange("p o j (n t) -> p (o n) t j", t=J)[
                        :, k * QH:(k + 1) * QH, 4 * qc:4 * qc + 4].rearrange("p n t j -> p t n j")
                    nc.gpsimd.tensor_tensor(dst, dst, addend[:, qc], ALU.add).then_inc(added, 1)

                def quad(b, k, more, events=None):
                    q = b * 4 + k
                    for kind, x in events or events_of(q, more):
                        kind, back = split(kind)
                        if kind == "score" and x[1] == QH - 1 and STEPS[x[0]][1] >= 4 * STEPS[x[0]][0]:
                            mask(q, x[0])
                        elif kind == "take_max":
                            max_parts(x, (q + (x < NC - 1)) * NC + x)
                        elif kind == "take_out":
                            if back:
                                add(b - (k == 0), (k - 1) % 4, q - 1, x)
                            else:
                                add(b, k, q, x)

                for g in range(NC - 1):
                    max_parts(g, g)
                for k in range(4):
                    quad(0, k, True)
                with pool.Fori(1, B - 1) as b:
                    for k in range(4):
                        quad(b, k, True)
                for k in range(4):
                    quad(B - 1, k, k < 3)
                quad(B, 0, False, TAIL)
                pool.wait_ge(added, NQ * NC)

            @block.scalar
            def _(act):
                def read_out(q, qc):
                    act.wait_ge(pv_done, q * NS + 2 * (qc + 1) * (qc + 2))
                    at_least(act, turned_out, (q - 1) * NC + qc + 1)
                    nc.scalar.copy(outs[:, qc], acc[:]).then_inc(outs_ready, 1)

                def body(pr, par, more, events=None):
                    q = pr * 2 + par
                    for kind, x in events or events_of(q, more):
                        kind, back = split(kind)
                        if kind == "score":
                            s, h = x
                            act.wait_ge(scores_ready, (q * NS + s) * QH + h + 1)
                            if h == 0:
                                at_least(act, pv_done, q * NS + s - NP + 1)
                            c0 = columns(s)
                            nc.scalar.activation(probs[:, s % NP, h, c0:CH], scores[:, (s * QH + h) % SB, c0:CH],
                                                 ACT.Exp, scale=SCALE).then_inc(probs_ready, 1)
                        elif kind == "read_out":
                            read_out(q - back, x)
                loop_quads(act, body)
                body(NQ // 2, 0, False, TAIL)

            @block.vector
            def _(dve):
                def reduce_unit(q, i):
                    g, t4, h, n, part, w = UNITS[i]
                    dve.wait_ge(fill_ready, q * NU + i + 1)
                    nc.vector.tensor_reduce(maxima[:, g, h:h + n, t4, part],
                                            fill[:, i % FB, 0:n * w].rearrange("p (h w) -> p h w", w=w),
                                            AXX, ALU.max).then_inc(fill_read, 1)

                def finish(q, g):
                    dve.wait_ge(fill_read, q * NU + LAST_UNIT_OF_GROUP[g] + 1)
                    at_least(dve, turned_max, (q - 1) * NC + g + 1)
                    nc.vector.tensor_reduce(negmax[:, g], maxima[:, g, :, :, 0:g + 1].rearrange("p h t r -> p (h t) r"),
                                            AXX, ALU.max, negate=True).then_inc(negmax_ready, 1)

                def take_max(pr, par, g):
                    n = (pr * 2 + par) * NC + g
                    dve.wait_ge(turned_max, n + 1)
                    at_least(dve, rows_in[1 - par][g], (pr + par) * ROWS_SENT)
                    nc.vector.tensor_copy(mparts[:, g, 0], turn[0:QH * 4, 0:P]).then_inc(part1, 1)
                    dve.wait_ge(part1, n + 1)
                    nc.vector.tensor_tensor(mrest[:, g], turn[0:QH * 4, 0:P], mparts[:, g, 0],
                                            ALU.subtract).then_inc(left1, 1)

                def take_out(q, qc):
                    n = q * NC + qc
                    dve.wait_ge(turned_out, n + 1)
                    at_least(dve, added, (q - 1) * NC + qc + 1)
                    t = turn.rearrange("p (t h w) -> p t h w", t=4, w=VW)
                    nc.vector.reciprocal(recip[:, qc], t[:, :, :, HD]).then_inc(recip_ready, 1)
                    dve.wait_ge(recip_ready, n + 1)
                    nc.vector.tensor_tensor(weight[:, qc], recip[:, qc],
                                            wsum[:, ds(q * QH * J, QH * J)].rearrange("p (h t) -> p t h", t=J)[:, 4 * qc:4 * qc + 4],
                                            ALU.mult).then_inc(weight_ready, 1)
                    dve.wait_ge(weight_ready, n + 1)
                    nc.vector.tensor_tensor(addend[:, qc], t[:, :, :, 0:HD],
                                            weight[:, qc].unsqueeze(3).to_broadcast([P, 4, QH, HD]),
                                            ALU.mult).then_inc(addend_ready, 1)

                def body(pr, par, more, events=None):
                    q = pr * 2 + par
                    for kind, x in events or events_of(q, more):
                        kind, back = split(kind)
                        if kind == "unit":
                            reduce_unit(q + for_next((kind, x)), x)
                        elif kind == "finish":
                            finish(q + for_next((kind, x)), x)
                        elif kind == "take_max":
                            take_max(*((pr + par, 1 - par) if for_next((kind, x)) else (pr, par)), x)
                        elif kind == "take_out":
                            take_out(q - back, x)

                for i in range(FIRST_UNITS):
                    reduce_unit(0, i)
                    if i in LAST_UNIT_OF_GROUP:
                        finish(0, UNITS[i][0])
                        take_max(0, 0, UNITS[i][0])
                loop_quads(dve, body)
                body(NQ // 2, 0, False, TAIL)

            @block.tensor
            def _(pe):
                mm = nc.tensor.matmul

                def fill_unit(pr, par, i):
                    q = pr * 2 + par
                    g, t4, h0, n, part, w = UNITS[i]
                    at_least(pe, fill_read, q * NU + (i - FB + 1 if i >= FB else 0))
                    if i == 0 or g != UNITS[i - 1][0]:
                        pe.wait_ge(loaded[par][g], (pr + 1) * QK_SENT)
                    for h in range(h0, h0 + n):
                        at = (h - h0) * w
                        last = mm(fill[:, i % FB, at:at + w], Q[0:EPS_ROWS, par, g, h, t4 * P:(t4 + 1) * P],
                                  K[0:EPS_ROWS, par, part, h, 0:w], start=True, stop=True, skip_group_check=True)
                        if part == g:
                            last = mm(fill[:, i % FB, at + w - P:at + w], identb[:], maskb[:], start=False, stop=True,
                                      skip_group_check=True)
                    last.then_inc(fill_ready, 1)

                def turn_max(q, g):
                    pe.wait_ge(negmax_ready, q * NC + g + 1)
                    nc.tensor.transpose(turn[0:QH * 4, 0:P], negmax[:, g], ident[:]).then_inc(turned_max, 1)

                def turn_out(q, qc):
                    pe.wait_ge(outs_ready, q * NC + qc + 1)
                    for t in range(4):
                        last = nc.tensor.transpose(turn[:, t * P:(t + 1) * P], outs[:, qc, t * P:(t + 1) * P], ident[:])
                    last.then_inc(turned_out, 1)

                def read_of_turn(q, use):
                    kind, back = split(use[0])
                    if kind == "turn_max":
                        return left1, (q + for_next(use)) * NC + use[1] + 1
                    return addend_ready, (q - back) * NC + use[1] + 1

                def turn_free(q, event, uses):
                    at = uses.index(event)
                    if at > 0:
                        pe.wait_ge(*read_of_turn(q, uses[at - 1]))
                    elif isinstance(q, int) and q == 0:
                        pe.wait_ge(left1, NC - 1)
                    elif isinstance(q, int) and q == NQ:
                        pe.wait_ge(*read_of_turn(q - 1, [e for e in TURNS if not for_next(e)][-1]))
                    else:
                        pe.wait_ge(*read_of_turn(q - 1, TURNS[-1]))

                def score(q, pr, par, s, h):
                    qc, kt = STEPS[s]
                    c0 = columns(s)
                    if kt == 0 and h == 0:
                        pe.wait_ge(rows_in[par][qc], (pr + 1) * ROWS_SENT)
                    n = s * QH + h
                    at_least(pe, probs_ready, q * NS * QH + (n - SB + 1 if n >= SB else 0))
                    mm(scores[:, n % SB, c0:CH], K[0:KROWS, par, kt // 4, h, kt % 4 * P:(kt % 4 + 1) * P],
                       Q[0:KROWS, par, qc, h, c0:CH], start=True, stop=True).then_inc(scores_ready, 1)

                def weigh(q, pr, par, s):
                    qc, kt = STEPS[s]
                    c0 = columns(s)
                    if s == 0:
                        pe.wait_ge(v_loaded[par], (pr + 1) * 16)
                    pe.wait_ge(probs_ready, (q * NS + s + 1) * QH)
                    if kt >= 4 * qc:
                        pe.wait_ge(masked, (q * NC + qc) * 4 + kt - 4 * qc + 1)
                    if kt == 0:
                        at_least(pe, outs_ready, q * NC + qc)
                    for h in range(QH):
                        last = mm(acc[VW * h:VW * h + VW, c0:CH], V[:, par, kt, VW * h:VW * h + VW],
                                  probs[:, s % NP, h, c0:CH], start=(kt == 0), stop=(kt == 4 * qc + 3),
                                  skip_group_check=True)
                    last.then_inc(pv_done, 1)

                def body(pr, par, more, events=None):
                    q = pr * 2 + par
                    todo = events or events_of(q, more)
                    uses = [e for e in todo if e[0].startswith("turn_")]
                    for kind, x in todo:
                        event = (kind, x)
                        kind, back = split(kind)
                        if kind == "score":
                            score(q, pr, par, *x)
                        elif kind == "weigh":
                            weigh(q - back, pr - (1 - par) if back else pr, 1 - par if back else par, x)
                        elif kind == "unit":
                            fill_unit(*((pr + par, 1 - par) if for_next(event) else (pr, par)), x)
                        elif kind == "turn_max":
                            turn_free(q, event, uses)
                            turn_max(q + for_next(event), x)
                        elif kind == "turn_out":
                            turn_free(q, event, uses)
                            turn_out(q - back, x)

                pe.wait_ge(ones_made, 1)
                for i in range(FIRST_UNITS):
                    fill_unit(0, 0, i)
                    if i in LAST_UNIT_OF_GROUP:
                        if i != LAST_UNIT_OF_GROUP[0]:
                            pe.wait_ge(left1, UNITS[i][0])
                        turn_max(0, UNITS[i][0])
                loop_quads(pe, body)
                body(NQ // 2, 0, False, TAIL)


SLOTS = E * 2 * CAP
TILES = SLOTS // P
ET = 2 * CAP // P
CT = 4
EC = ET // CT
C64 = B * J


def build_route(nc, c, gate_w, xrows, x1rows):
    X, ident = c["X"], c["ident"]
    rowof, slotof, W = c["rowof"], c["slotof"], c["W"]
    with ExitStack() as ctx:
        def sb(n, s, t): return ctx.enter_context(nc.sbuf_tensor(n, s, t))
        def ps(n, s, t): return ctx.enter_context(nc.psum_tensor(n, s, t))
        def sem(n): return ctx.enter_context(nc.semaphore(n))
        passed = sem("passed2")
        gw = sb("gw", [P, KD, E], F32)
        epst = sb("r_eps", [P, 1], F32)
        before = sb("before", [P, P], F32)
        ones = sb("r_ones", [P, P], F32)
        zerob = sb("zerob", [P, P], BF16)
        lane = sb("lane", [P, P], BF16)
        tile_no = sb("tile_no", [P, TILES], BF16)
        part_no = sb("part_no", [P, 1], F32)
        col_no = sb("col_no", [P, 2, C64], F32)
        expert_no = sb("expert_no", [P, E], F32)
        rank = sb("rank", [P, E], F32)
        stats = sb("r_stats", [P, J, 6], F32)
        mv = sb("r_mv", [P, J, 2], F32)
        std = sb("r_std", [P, J], F32)
        rstd = sb("r_rstd", [P, J], F32)
        xn = sb("r_xn", [P, J, D], F32)
        xT = sb("r_xT", [P, KD, J, P], F32)
        small = [P, C64, E]
        shifted, ex, pr = sb("shifted", small, F32), sb("ex", small, F32), sb("pr", small, F32)
        eq, cand = sb("eq", small, F32), sb("cand", small, F32)
        top, total, rtotal, best = (sb(n, [P, C64], F32) for n in ("top", "total", "rtotal", "best"))
        hot = sb("hot", [P, 2, C64, E], F32)
        prob = sb("prob", [P, 2, C64], F32)
        count = sb("count", [P, 2, 2 * B, J, E], F32)
        sums = sb("sums", [P, 2, B, E], F32)
        offset = sb("offset", [P, 2, B, E], F32)
        place, eno, valid, slot = (sb(n, [P, 2, C64], F32) for n in ("place", "eno", "valid", "slot"))
        slot_i, hi_i, lo_i = (sb(n, [P, 2, C64], I32) for n in ("slot_i", "hi_i", "lo_i"))
        hi, lo = sb("hi", [P, 2, C64], F32), sb("lo", [P, 2, C64], F32)
        LS = 4
        is_lane = sb("is_lane", [P, LS, P], BF16)
        is_tile = sb("is_tile", [P, LS, 2, TILES], BF16)
        tabc = sb("tabc", [P, TILES], F32)
        tabr = sb("tabr", [P, TILES], F32)
        tp = ps("r_tp", [P, 2, CH], F32)
        logits = ps("logits", [P, C64, E], F32)
        sums_before = ps("sums_before", [P, 2, 64], F32)
        table = ps("table", [P, 2 * TILES], F32)

        x1_out = sem("x1_out")
        gw_loaded, consts, stat_done, mv_done, std_done, rstd_done, xn_done = (sem("r_" + n) for n in
            ("gw_loaded", "consts", "stat_done", "mv_done", "std_done", "rstd_done", "xn_done"))
        turned, turn_free, xT_done, logits_done, rows_out = (sem("r_" + n) for n in
            ("turned", "turn_free", "xT_done", "logits_done", "rows_out"))
        step, exp_done, sums_ready, ranked, hot_tiles, tabled, table_done, shift_ready = (sem("r_" + n) for n in
            ("step", "exp_done", "sums_ready", "ranked", "hot_tiles", "tabled", "table_done", "shift_ready"))

        with nc.Block() as block:
            @block.sync
            def _(sp):
                sp.dma_start(gw[:], gate_w).then_inc(gw_loaded, 16)
                for b in range(B):
                    sp.dma_start(x1rows[b], X[:, b]).then_inc(x1_out, 16)
                @looped(sp, B)
                def _(b):
                    sp.wait_ge(xn_done, b * J + J)
                    sp.dma_start(xrows.rearrange("(p b j) d -> p b j d", b=B, j=J)[:, ds(b, 1)].rearrange("p o j d -> p (o j) d"),
                                 xn[:]).then_inc(rows_out, 16)
                sp.wait_ge(rows_out, 16 * B)
                sp.wait_ge(x1_out, 16 * B)

            @block.gpsimd
            def _(pool):
                nc.gpsimd.memset(epst[:], EPS).then_inc(consts, 1)
                nc.gpsimd.memset(before[:], 0.0).then_inc(consts, 1)
                nc.gpsimd.memset(ones[:], 1.0).then_inc(consts, 1)
                nc.gpsimd.memset(zerob[:], 0.0).then_inc(consts, 1)
                nc.gpsimd.iota(lane[:], pattern=[[1, P]], base=0, channel_multiplier=0,
                               allow_small_or_imprecise_dtypes=True).then_inc(consts, 1)
                nc.gpsimd.iota(tile_no[:], pattern=[[1, TILES]], base=0, channel_multiplier=0,
                               allow_small_or_imprecise_dtypes=True).then_inc(consts, 1)
                nc.gpsimd.iota(part_no[:], pattern=[[1, 1]], base=0, channel_multiplier=1,
                               allow_small_or_imprecise_dtypes=True).then_inc(consts, 1)
                nc.gpsimd.iota(col_no[:], pattern=[[0, 2], [1, C64]], base=0, channel_multiplier=0,
                               allow_small_or_imprecise_dtypes=True).then_inc(consts, 1)
                nc.gpsimd.iota(expert_no[:], pattern=[[1, E]], base=0, channel_multiplier=0,
                               allow_small_or_imprecise_dtypes=True).then_inc(consts, 1)
                nc.gpsimd.iota(rank[:], pattern=[[-1, E]], base=E, channel_multiplier=0,
                               allow_small_or_imprecise_dtypes=True).then_inc(consts, 1)
                pool.wait_ge(consts, 10)
                nc.gpsimd.affine_select(out=before[:], in_=before[:], compare_op=ALU.is_ge, fill=1.0, base=0,
                                        pattern=[[-1, P]], channel_multiplier=1).then_inc(consts, 1)

            @block.scalar
            def _(act):
                act.wait_ge(consts, 11)
                @looped(act, B)
                def _(b):
                    act.wait_ge(mv_done, b * J + J)
                    act.wait_ge(rstd_done, b)
                    nc.scalar.activation(std[:], mv[:, :, 1], ACT.Sqrt, bias=epst[:, 0:1]).then_inc(std_done, 1)
                    for i in range(4):
                        act.wait_ge(turned, b * 8 + 2 * i + 1)
                        act.wait_ge(logits_done, b * J)
                        nc.scalar.copy(xT[:, 0, 4 * i:4 * i + 4], tp[:, 0].rearrange("d (j p) -> d j p", p=P)).then_inc(turn_free, 1)
                act.wait_ge(shift_ready, 1)
                nc.scalar.activation(ex[:], shifted[:], ACT.Exp).then_inc(exp_done, 1)

            @block.tensor
            def _(pe):
                pe.wait_ge(gw_loaded, 16)
                pe.wait_ge(consts, 11)
                @looped(pe, B)
                def _(b):
                    for i in range(4):
                        for half in range(2):
                            pe.wait_ge(xn_done, b * J + 4 * i + 4)
                            pe.wait_ge((turn_free, xT_done)[half], b * 4 + i)
                            for j in range(4):
                                last = nc.tensor.transpose(tp[:, half, j * P:(j + 1) * P],
                                                           xn[:, 4 * i + j, half * P:(half + 1) * P], ident[:])
                            last.then_inc(turned, 1)
                    pe.wait_ge(turn_free, b * 4 + 4)
                    pe.wait_ge(xT_done, b * 4 + 4)
                    for j in range(J):
                        for k in range(KD):
                            last = nc.tensor.matmul(logits[:, ds(b * J + j, 1)].rearrange("p o e -> p (o e)"),
                                                    xT[:, k, j], gw[:, k], start=(k == 0), stop=(k == KD - 1))
                        last.then_inc(logits_done, 1)
                pe.wait_ge(sums_ready, 1)
                cols = sums.rearrange("p k b e -> p (k b e)")
                nc.tensor.matmul(sums_before[:, 0], before[:], cols, start=True, stop=True)
                nc.tensor.matmul(sums_before[:, 1], ones[:], cols, start=True, stop=True).then_inc(ranked, 1)
                nc.tensor.matmul(table[:], zerob[:], zerob[:, 0:1].to_broadcast([P, 2 * TILES]), start=True, stop=False)
                @looped(pe, 2 * B)
                def _(n):
                    for j in range(J):
                        pe.wait_ge(hot_tiles, n * J + j + 1)
                        nc.tensor.matmul(table[:], is_lane[:, j % LS], is_tile[:, j % LS].rearrange("p a t -> p (a t)"),
                                         start=False, stop=False).then_inc(tabled, 1)
                nc.tensor.matmul(table[:], zerob[:], zerob[:, 0:1].to_broadcast([P, 2 * TILES]), start=False, stop=True).then_inc(table_done, 1)

            @block.vector
            def _(dve):
                @looped(dve, B)
                def _(b):
                    dve.wait_ge(mv_done, b * J)
                    for j in range(J):
                        nc.vector.bn_stats(stats[:, j], X[:, ds(b, 1), j].rearrange("p o d -> p (o d)")).then_inc(stat_done, 1)
                    dve.wait_ge(xn_done, b * J)
                    for j in range(J):
                        dve.wait_ge(stat_done, b * J + j + 1).then_inc(passed, 1)
                        nc.vector.bn_aggr(mv[:, j], stats[:, j]).then_inc(mv_done, 1)
                    dve.wait_ge(std_done, b + 1)
                    nc.vector.reciprocal(rstd[:], std[:]).then_inc(rstd_done, 1)
                    dve.wait_ge(rstd_done, b + 1)
                    dve.wait_ge(turned, b * 8)
                    dve.wait_ge(rows_out, b * 16)
                    for j in range(J):
                        nc.vector.tensor_scalar(xn[:, j], X[:, ds(b, 1), j].rearrange("p o d -> p (o d)"),
                                                mv[:, j, 0:1], rstd[:, j:j + 1],
                                                ALU.subtract, ALU.mult).then_inc(xn_done, 1)
                    for i in range(4):
                        dve.wait_ge(turned, b * 8 + 2 * i + 2)
                        dve.wait_ge(logits_done, b * J)
                        nc.vector.tensor_copy(xT[:, 1, 4 * i:4 * i + 4], tp[:, 1].rearrange("d (j p) -> d j p", p=P)).then_inc(xT_done, 1)

                v = nc.vector
                done = [0]

                def then(ins):
                    done[0] += 1
                    ins.then_inc(step, 1)
                    dve.wait_ge(step, done[0])

                def wide(a):
                    return a.unsqueeze(2).to_broadcast(small)

                def over(a):
                    return a.unsqueeze(1).to_broadcast(small)
                dve.wait_ge(logits_done, C64)
                dve.wait_ge(consts, 11)
                then(v.tensor_reduce(top[:], logits[:], AXX, ALU.max))
                v.tensor_tensor(shifted[:], logits[:], wide(top[:]), ALU.subtract).then_inc(shift_ready, 1)
                dve.wait_ge(exp_done, 1)
                then(v.tensor_reduce(total[:], ex[:], AXX, ALU.add))
                then(v.reciprocal(rtotal[:], total[:]))
                then(v.tensor_tensor(pr[:], ex[:], wide(rtotal[:]), ALU.mult))
                for k in range(2):
                    then(v.tensor_reduce(prob[:, k], pr[:], AXX, ALU.max))
                    then(v.tensor_tensor(eq[:], pr[:], wide(prob[:, k]), ALU.is_equal))
                    then(v.tensor_tensor(cand[:], eq[:], over(rank[:]), ALU.mult))
                    then(v.tensor_reduce(best[:], cand[:], AXX, ALU.max))
                    then(v.tensor_tensor(hot[:, k], cand[:], wide(best[:]), ALU.is_equal))
                    if k == 0:
                        then(v.scalar_tensor_tensor(out=pr[:], in0=hot[:, k], scalar=-2.0, in1=pr[:],
                                                    op0=ALU.mult, op1=ALU.add))
                then(v.tensor_tensor(total[:], prob[:, 0], prob[:, 1], ALU.add))
                then(v.reciprocal(rtotal[:], total[:]))
                for k in range(2):
                    then(v.tensor_tensor(W[:, k], prob[:, k], rtotal[:], ALU.mult))
                src = hot.rearrange("p k (b j) e -> p (k b) j e", j=J)
                for n, d in enumerate((1, 2, 4, 8)):
                    dst = count[:, n % 2]
                    then(v.tensor_copy(dst[:, :, 0:d], src[:, :, 0:d]))
                    then(v.tensor_tensor(dst[:, :, d:], src[:, :, d:], src[:, :, 0:J - d], ALU.add))
                    src = dst
                cnt = src
                v.tensor_copy(sums.rearrange("p k b e -> p (k b) e"), cnt[:, :, J - 1]).then_inc(sums_ready, 1)
                dve.wait_ge(ranked, 1)
                before_p = sums_before[:, 0].rearrange("p (k b e) -> p k b e", k=2, b=B)
                whole = sums_before[:, 1].rearrange("p (k b e) -> p k b e", k=2, b=B)
                then(v.memset(offset[:, :, 0], 0.0))
                for b in range(1, B):
                    then(v.tensor_tensor(offset[:, :, b], whole[:, :, b - 1], offset[:, :, b - 1], ALU.add))
                then(v.tensor_tensor(offset[:], before_p, offset[:], ALU.add))
                other = count[:, 0]
                then(v.tensor_tensor(other, cnt, offset.rearrange("p k b e -> p (k b) e").unsqueeze(2)
                                     .to_broadcast([P, 2 * B, J, E]), ALU.add))
                hot8 = hot.rearrange("p k (b j) e -> p (k b) j e", j=J)
                then(v.tensor_tensor(cnt, other, hot8, ALU.mult))
                then(v.tensor_reduce(place.rearrange("p k (b j) -> p (k b) j", j=J), cnt, AXX, ALU.add))
                for k in range(2):
                    then(v.tensor_tensor(cand[:], hot[:, k], over(expert_no[:]), ALU.mult))
                    then(v.tensor_reduce(eno[:, k], cand[:], AXX, ALU.add))
                then(v.tensor_scalar(valid[:], place[:], float(CAP) + 0.5, None, ALU.is_lt))
                then(v.tensor_tensor(W[:], W[:], valid[:], ALU.mult))
                then(v.scalar_tensor_tensor(out=slot[:], in0=eno[:], scalar=2.0 * CAP, in1=place[:],
                                            op0=ALU.mult, op1=ALU.add))
                then(v.tensor_scalar(slot[:, 1], slot[:, 1], float(CAP), None, ALU.add))
                then(v.tensor_tensor(slot[:], slot[:], valid[:], ALU.mult))
                then(v.tensor_scalar(place[:], slot[:], -1.0, None, ALU.add))
                then(v.tensor_copy(slot_i[:], place[:]))
                then(v.tensor_scalar(slot[:], place[:], 0.0, None, ALU.max))
                then(v.tensor_copy(slotof[:], slot[:]))
                then(v.tensor_scalar(hi_i[:], slot_i[:], 7, None, ALU.arith_shift_right))
                then(v.tensor_scalar(lo_i[:], slot_i[:], P - 1, None, ALU.bitwise_and))
                then(v.tensor_copy(hi[:], hi_i[:]))
                then(v.tensor_copy(lo[:], lo_i[:]))
                hi_c, lo_c, no_c = (a.rearrange("p k c -> p (k c)") for a in (hi, lo, col_no))
                @looped(dve, 2 * B)
                def _(n):
                    for j in range(J):
                        if j < LS:
                            dve.wait_ge(tabled, n * J)
                        else:
                            dve.wait_ge(tabled, n * J + j - LS + 1)
                        at = ds(n * J + j, 1)
                        v.tensor_scalar(is_lane[:, j % LS], lane[:], lo_c[:, at], None, ALU.is_equal)
                        v.tensor_scalar(is_tile[:, j % LS, 0], tile_no[:], hi_c[:, at], part_no[:, 0:1],
                                        ALU.is_equal, ALU.mult)
                        v.tensor_scalar(is_tile[:, j % LS, 1], tile_no[:], hi_c[:, at], no_c[:, at],
                                        ALU.is_equal, ALU.mult).then_inc(hot_tiles, 1)
                dve.wait_ge(table_done, 1)
                then(v.tensor_copy(tabc[:], table[:, TILES:2 * TILES]))
                then(v.scalar_tensor_tensor(out=tabr[:], in0=table[:, 0:TILES], scalar=float(C64), in1=tabc[:],
                                            op0=ALU.mult, op1=ALU.add))
                then(v.tensor_copy(rowof[:], tabr[:]))


def build_experts(nc, c, wi_gate, wi_up, wo, xrows, yrows):
    ident, rowof = c["ident"], c["rowof"]
    FT = F // P
    HI, LO = 0, 1
    PIECES = 3
    PAIRS = ((HI, HI), (HI, LO), (LO, HI))
    with ExitStack() as ctx:
        def sb(n, s, t): return ctx.enter_context(nc.sbuf_tensor(n, s, t))
        def ps(n, s, t): return ctx.enter_context(nc.psum_tensor(n, s, t))
        def sem(n): return ctx.enter_context(nc.semaphore(n))
        passed = sem("passed3")
        raw = sb("raw", [P, PIECES, KD * F], F32)
        w_hi = sb("w_hi", [P, 2, PIECES, KD * F], F32R)
        w_lo = sb("w_lo", [P, 2, PIECES, KD * F], F32R)
        rows = sb("rows", [P, 2, ET], I32)
        xg = sb("xg", [P, 2, CT, D], F32)
        x_hi = sb("x_hi", [P, 2, KD, CH], F32R)
        x_lo = sb("x_lo", [P, 2, KD, CH], F32R)
        act_g = sb("act_g", [P, 2, CH], F32)
        prod = sb("prod", [P, 2, CH], F32)
        h_hi = sb("h_hi", [P, FT, CH], F32R)
        h_lo = sb("h_lo", [P, FT, CH], F32R)
        ysb = sb("ysb", [P, 2, CT, D], F32)
        xp = ps("xp", [P, KD, CH], F32)
        gu = ps("gu", [P, 2, 2, CH], F32)
        yp = ps("yp", [P, 2, CH], F32)
        w_in = [sem(f"w_in{i}") for i in range(PIECES)]
        x_in = [sem(f"x_in{i}") for i in range(2)]
        y_out = [sem(f"y_out{i}") for i in range(2)]
        names = ("w_hi_done", "w_lo_done", "rows_ready", "x_turned", "x_hi_done", "x_lo_done", "gu_ready", "silu_done",
                 "prod_ready", "h_hi_done", "h_lo_done", "y_ready", "y_put0", "y_put1")
        (w_hi_done, w_lo_done, rows_ready, x_turned, x_hi_done, x_lo_done, gu_ready, silu_done,
         prod_ready, h_hi_done, h_lo_done, y_ready, y_put0, y_put1) = (sem("e_" + n) for n in names)
        NCH = E * EC

        def at_least(eng, sem_, n):
            if not isinstance(n, int) or n > 0:
                eng.wait_ge(sem_, n)

        def loop_experts(eng, body):
            body(0, 0, True)
            body(0, 1, True)
            with eng.Fori(1, E // 2 - 1) as pr:
                body(pr, 0, True)
                body(pr, 1, True)
            body(E // 2 - 1, 0, True)
            body(E // 2 - 1, 1, False)

        with nc.Block() as block:
            @block.sync
            def _(sp):
                def load(e):
                    for i, src in enumerate((wi_gate, wi_up, wo)):
                        at_least(sp, w_lo_done, (e - 1) * PIECES + i + 1)
                        sp.dma_start(raw[:, i], src[ds(e, 1)].rearrange("o p k f -> p (o k f)")).then_inc(w_in[i], 16)

                def body(pr, par, more):
                    e = pr * 2 + par
                    if more:
                        load(e + 1)
                    for ch in range(EC):
                        n = e * EC + ch
                        slot = (par * EC + ch) % 2
                        sp.wait_ge(y_put0, n * 2 + 2)
                        sp.wait_ge(y_put1, n * 2 + 2)
                        sp.dma_start(yrows.rearrange("(n t p) d -> n p t d", t=CT, p=P)[ds(n, 1)].rearrange("o p t d -> p (o t) d"),
                                     ysb[:, slot]).then_inc(y_out[slot], 16)
                load(0)
                loop_experts(sp, body)
                sp.wait_ge(y_out[0], 16 * NCH // 2)
                sp.wait_ge(y_out[1], 16 * NCH // 2)

            @block.gpsimd
            def _(pool):
                def split_lo(e, par, i):
                    pool.wait_ge(w_hi_done, e * PIECES + i + 1)
                    nc.gpsimd.tensor_tensor(w_lo[:, par, i], raw[:, i], w_hi[:, par, i].bitcast(F32),
                                            ALU.subtract).then_inc(w_lo_done, 1)

                def gather(pr, par, ch):
                    i = par * EC + ch
                    n = pr * 2 * EC + i
                    if i > 1 or not isinstance(n, int):
                        pool.wait_ge(x_turned, n - 1 if i > 1 else pr * 2 * EC).then_inc(passed, 1)
                    for t in range(CT):
                        nc.gpsimd.indirect_dma_start(
                            out=xg[:, i % 2, t], out_offset=None, in_=xrows,
                            in_offset=bass.IndirectOffsetOnAxis(ap=rows[:, par, ch * CT + t:ch * CT + t + 1].bitcast(U32), axis=0),
                        ).then_inc(x_in[i % 2], 16)

                def body(pr, par, more):
                    e = pr * 2 + par
                    pool.wait_ge(x_turned, e * EC).then_inc(passed, 1)
                    nc.gpsimd.tensor_copy(rows[:, par], rowof[:, ds(e * ET, ET)]).then_inc(rows_ready, 1)
                    pool.wait_ge(rows_ready, e + 1)
                    for ch in range(EC):
                        gather(pr, par, ch)
                        if e_is_first(pr, par) and ch == 1:
                            for i in range(PIECES):
                                split_lo(0, 0, i)
                        if more and ch >= 2:
                            split_lo(e + 1, 1 - par, ch - 2)

                def e_is_first(pr, par):
                    return isinstance(pr, int) and pr == 0 and par == 0
                loop_experts(pool, body)

            @block.scalar
            def _(act):
                def split_hi(pr, par, i):
                    e = pr * 2 + par
                    act.wait_ge(w_in[i], 16 * (e + 1))
                    at_least(act, y_ready, (e - 1) * EC * CT)
                    nc.scalar.copy(w_hi[:, par, i], raw[:, i]).then_inc(w_hi_done, 1)

                def turn(pr, i):
                    n = pr * 2 * EC + i
                    act.wait_ge(x_turned, n + 1)
                    at_least(act, y_ready, (n - 1) * CT)
                    for k in range(KD):
                        nc.scalar.copy(x_hi[:, i % 2, k], xp[:, k]).then_inc(x_hi_done, 1)

                def round_h(n, f):
                    act.wait_ge(prod_ready, n * FT + f + 1)
                    at_least(act, y_ready, n * CT)
                    nc.scalar.copy(h_hi[:, f], prod[:, f % 2]).then_inc(h_hi_done, 1)

                def body(pr, par, more):
                    for ch in range(EC):
                        i = par * EC + ch
                        n = pr * 2 * EC + i
                        for f in range(FT):
                            act.wait_ge(gu_ready, n * FT + f + 1)
                            at_least(act, prod_ready, n * FT + f - 1)
                            nc.scalar.activation(act_g[:, f % 2], gu[:, f % 2, 0], ACT.Silu).then_inc(silu_done, 1)
                            if f > 0:
                                round_h(n, f - 1)
                        round_h(n, FT - 1)
                        if more or ch < EC - 1:
                            turn(pr, i + 1)
                        for t in (0, 2):
                            act.wait_ge(y_ready, n * CT + t + 1)
                            at_least(act, y_out[i % 2], (pr * EC + i // 2) * 16)
                            nc.scalar.copy(ysb[:, i % 2, t], yp[:, 0, 0:D]).then_inc(y_put0, 1)
                        if more and ch in (1, 2, 3):
                            split_hi(pr + par, 1 - par, ch - 1)
                turn(0, 0)
                for i in range(PIECES):
                    split_hi(0, 0, i)
                loop_experts(act, body)

            @block.vector
            def _(dve):
                def turn(pr, i):
                    n = pr * 2 * EC + i
                    for k in range(KD):
                        dve.wait_ge(x_hi_done, n * KD + k + 1)
                        nc.vector.tensor_tensor(x_lo[:, i % 2, k], xp[:, k], x_hi[:, i % 2, k].bitcast(F32),
                                                ALU.subtract).then_inc(x_lo_done, 1)

                def rest_h(n, f):
                    dve.wait_ge(h_hi_done, n * FT + f + 1)
                    nc.vector.tensor_tensor(h_lo[:, f], prod[:, f % 2], h_hi[:, f].bitcast(F32),
                                            ALU.subtract).then_inc(h_lo_done, 1)

                def body(pr, par, more):
                    for ch in range(EC):
                        i = par * EC + ch
                        n = pr * 2 * EC + i
                        for f in range(FT):
                            dve.wait_ge(silu_done, n * FT + f + 1)
                            at_least(dve, h_lo_done, n * FT + f - 1)
                            nc.vector.tensor_tensor(prod[:, f % 2], act_g[:, f % 2], gu[:, f % 2, 1],
                                                    ALU.mult).then_inc(prod_ready, 1)
                            if f > 0:
                                rest_h(n, f - 1)
                        rest_h(n, FT - 1)
                        if more or ch < EC - 1:
                            turn(pr, i + 1)
                        for t in (1, 3):
                            dve.wait_ge(y_ready, n * CT + t + 1)
                            at_least(dve, y_out[i % 2], (pr * EC + i // 2) * 16)
                            nc.vector.tensor_copy(ysb[:, i % 2, t], yp[:, 1, 0:D]).then_inc(y_put1, 1)
                turn(0, 0)
                loop_experts(dve, body)

            @block.tensor
            def _(pe):
                mm = nc.tensor.matmul
                w = [x.rearrange("p a i (k f) -> p a i k f", k=KD) for x in (w_hi, w_lo)]
                wd = [x.rearrange("p a i (f d) -> p a i f d", f=FT)[:, :, 2] for x in (w_hi, w_lo)]
                x, h = (x_hi, x_lo), (h_hi, h_lo)

                def turn(pr, i):
                    n = pr * 2 * EC + i
                    pe.wait_ge(x_in[i % 2], (pr * EC + i // 2 + 1) * 16 * CT)
                    at_least(pe, x_lo_done, n * KD)
                    for k in range(KD):
                        for t in range(CT):
                            last = nc.tensor.transpose(xp[:, k, t * P:(t + 1) * P], xg[:, i % 2, t, k * P:(k + 1) * P], ident[:])
                    last.then_inc(x_turned, 1)

                def body(pr, par, more):
                    pe.wait_ge(w_lo_done, (pr * 2 + par + 1) * PIECES)
                    for ch in range(EC):
                        i = par * EC + ch
                        n = pr * 2 * EC + i
                        pe.wait_ge(x_lo_done, (n + 1) * KD)
                        for f in range(FT):
                            at_least(pe, prod_ready, n * FT + f - 1)
                            for a in range(2):
                                todo = [(k, sw, sx) for k in range(KD) for sw, sx in PAIRS]
                                for j, (k, sw, sx) in enumerate(todo):
                                    last = mm(gu[:, f % 2, a], w[sw][:, par, a, k, f * P:(f + 1) * P], x[sx][:, i % 2, k],
                                              start=(j == 0), stop=(j == len(todo) - 1))
                            last.then_inc(gu_ready, 1)
                        if more or ch < EC - 1:
                            turn(pr, i + 1)
                        for t in range(CT):
                            at_least(pe, (y_put0, y_put1)[t % 2], n * 2 + t // 2)
                            todo = [(f, sh, sw) for f in range(FT) for sh, sw in PAIRS]
                            for j, (f, sh, sw) in enumerate(todo):
                                if t == 0 and j % len(PAIRS) == 0:
                                    pe.wait_ge(h_lo_done, n * FT + f + 1)
                                last = mm(yp[:, t % 2, 0:D], h[sh][:, f, t * P:(t + 1) * P], wd[sw][:, par, f],
                                          start=(j == 0), stop=(j == len(todo) - 1))
                            last.then_inc(y_ready, 1)
                turn(0, 0)
                loop_experts(pe, body)


def build_combine(nc, c, x1rows, yrows, out):
    slotof, W = c["slotof"], c["W"]
    with ExitStack() as ctx:
        def sb(n, s, t): return ctx.enter_context(nc.sbuf_tensor(n, s, t))
        def sem(n): return ctx.enter_context(nc.semaphore(n))
        GS = 8
        X = sb("x_again", [P, B, J, D], F32)
        yg = sb("yg", [P, GS, 2, D], F32)
        x_in = [sem(f"x1_in{b}") for b in range(B)]
        y_in = [sem(f"y_in{i}") for i in range(GS)]
        first_added, added, out_done = sem("first_added"), sem("c_added"), sem("out_done")
        with nc.Block() as block:
            @block.gpsimd
            def _(pool):
                for n in range(C64):
                    if n >= GS:
                        pool.wait_ge(added, n - GS + 1)
                    for k in range(2):
                        nc.gpsimd.indirect_dma_start(
                            out=yg[:, n % GS, k], out_offset=None, in_=yrows,
                            in_offset=bass.IndirectOffsetOnAxis(ap=slotof[:, k, n:n + 1].bitcast(U32), axis=0),
                        ).then_inc(y_in[n % GS], 16)

            @block.vector
            def _(dve):
                for n in range(C64):
                    b, j = n // J, n % J
                    if j == 0:
                        dve.wait_ge(x_in[b], 16)
                    dve.wait_ge(y_in[n % GS], (n // GS + 1) * 32)
                    for k in range(2):
                        if k:
                            dve.wait_ge(first_added, n + 1)
                        nc.vector.scalar_tensor_tensor(out=X[:, b, j], in0=yg[:, n % GS, k], scalar=W[:, k, n:n + 1],
                                                       in1=X[:, b, j], op0=ALU.mult, op1=ALU.add).then_inc(
                                                           (first_added, added)[k], 1)

            @block.sync
            def _(sp):
                for b in range(B):
                    sp.dma_start(X[:, b], x1rows[b]).then_inc(x_in[b], 16)
                for n in range(0, C64, J // 4):
                    sp.wait_ge(added, n + J // 4)
                    b, j = n // J, n % J
                    sp.dma_start(out[b, :, j:j + J // 4], X[:, b, j:j + J // 4]).then_inc(out_done, 16)
                sp.wait_ge(out_done, 16 * C64 // (J // 4))


def build(nc, t):
    def dram(n, shape, dt): return nc.dram_tensor(n, shape, dt, kind="Internal").ap()
    qparts = dram("qparts", [NQ, NC, 3, HD, QH * CH], BF16)
    kparts = dram("kparts", [NQ, NC, 3, HD, QH * CH], BF16)
    vstore = dram("vstore", [NQ, P, J, QH * VW], F32)
    x1rows = dram("x1rows", [B, P, J, D], F32)
    xrows = dram("xrows", [B * S, D], F32)
    yrows = dram("yrows", [SLOTS, D], F32)
    with ExitStack() as ctx:
        def sb(n, s, dt): return ctx.enter_context(nc.sbuf_tensor(n, s, dt))
        c = {"rowof": sb("rowof", [P, TILES], I32), "slotof": sb("slotof", [P, 2, C64], I32),
             "W": sb("W", [P, 2, C64], F32)}
        c["ident"], c["identb"], c["maskb"] = build_constants(nc, ctx)
        with nc.sbuf_tensor("X", [P, B, J, D], F32) as c["X"], nc.sbuf_tensor("wsum", [P, B * D], F32) as c["wsum"]:
            build_project(nc, c, t["x"], t["wq"], t["wk"], t["wv"], t["w_out"], qparts, kparts, vstore)
            build_attend(nc, c, qparts, kparts, vstore)
            build_route(nc, c, t["gate_w"], xrows, x1rows)
        build_experts(nc, c, t["wi_gate"], t["wi_up"], t["wo"], xrows, yrows)
        build_combine(nc, c, x1rows, yrows, t["out"])


def kernel(L0_attn_x, L0_attn_W_qkv, L0_attn_W_out, L0_ffn_gate_w, L0_ffn_wi_gate, L0_ffn_wi_up, L0_ffn_wo):
    import concourse.bacc as bacc
    from concourse.bass_utils import run_bass_kernel_spmd

    def lay(a, *shape_and_order):
        shape, order = shape_and_order
        return np.ascontiguousarray(np.asarray(a).reshape(shape).transpose(order))

    w = np.asarray(L0_attn_W_qkv)
    arrays = {"x": np.asarray(L0_attn_x).reshape(B, P, J, D)}
    for i, n in enumerate(("wq", "wk")):
        arrays[n] = lay(w[:, :, i * HD:(i + 1) * HD], (4, QH, KD, P, HD), (3, 2, 0, 4, 1)).reshape(P, KD, D)
    arrays["wv"] = lay(w[:, :, 2 * HD:], (NH, KD, P, HD), (2, 1, 0, 3)).reshape(P, KD, D)
    arrays["w_out"] = lay(L0_attn_W_out, (KD, P, D), (1, 0, 2))
    arrays["gate_w"] = lay(L0_ffn_gate_w, (E, KD, P), (2, 1, 0))
    arrays["wi_gate"] = lay(L0_ffn_wi_gate, (E, F, KD, P), (0, 3, 2, 1))
    arrays["wi_up"] = lay(L0_ffn_wi_up, (E, F, KD, P), (0, 3, 2, 1))
    arrays["wo"] = lay(L0_ffn_wo, (E, D, F // P, P), (0, 3, 2, 1))
    nc = bacc.Bacc("TRN2", target_bir_lowering=False, num_devices=1)
    t = {n: nc.dram_tensor(n + "_in", a.shape, mybir.dt.from_np(a.dtype), kind="ExternalInput").ap()
         for n, a in arrays.items()}
    t["out"] = nc.dram_tensor("out", (B, P, J, D), F32, kind="ExternalOutput").ap()
    build(nc, t)
    r = run_bass_kernel_spmd(nc, [{n + "_in": np.ascontiguousarray(a) for n, a in arrays.items()}], core_ids=[0])
    return r.results[0]["out"].reshape(B, S, D)
```

```python
from contextlib import ExitStack

import numpy as np
import concourse.bass as bass
from concourse import mybir

F32 = mybir.dt.float32
BF16 = mybir.dt.bfloat16
F32R = mybir.dt.float32r
I32 = mybir.dt.int32
U32 = mybir.dt.uint32
ALU = mybir.AluOpType
ACT = mybir.ActivationFunctionType
AXX = mybir.AxisListType.X
ds = bass.ds

P = 128
B, S, D = 4, 2048, 256
NH, HD = 16, 16
J = S // P
KD = D // P
QH = 4
NQ = B * NH // QH
CH = 512
NC = S // CH
EPS = 1e-5
MASKED = -4.0e10
SCALE = HD ** -0.5
E, F, CAP = 8, 1024, 1280
PIECES = 3
EPS_ROWS = 96
MROWS = 3
KROWS = EPS_ROWS + MROWS
VW = 32
SLOTS = E * 2 * CAP
TILES = SLOTS // P
ET = 2 * CAP // P
KT = E * CAP // P
CT = 4
EC = ET // CT
C64 = B * J
HALF = B * S // 2


def steps_of_quad():
    return [(qc, kt) for qc in range(NC) for kt in range(4 * qc + 4)]


def max_units():
    units = []
    for g in range(NC):
        for t4 in range(4):
            for part in range(g):
                units += [(g, t4, h, 1, part, CH) for h in range(QH)]
            w = (t4 + 1) * P
            n = {0: 4, 1: 2, 2: 1, 3: 1}[t4]
            units += [(g, t4, h, n, g, w) for h in range(0, QH, n)]
    return units


STEPS = steps_of_quad()
NS = len(STEPS)
UNITS = max_units()
NU = len(UNITS)
FIRST_UNITS = sum(u[0] < NC - 1 for u in UNITS)
LAST_UNIT_OF_GROUP = [max(i for i, u in enumerate(UNITS) if u[0] == g) for g in range(NC)]
LAG = 2


FB = SB = 3
LOAD_NS = 12000.0
AHEAD = 500.0
OUT_NS = 2500.0
MAX_NS = 300.0
TAKE_NS = 300.0
HANDOFF = 190.0


def quad_events():
    ev, later = [], []
    order = [i for i in range(NU) if UNITS[i][0] == NC - 1] + [i for i in range(NU) if UNITS[i][0] < NC - 1]
    t = {"pe": 0.0, "dve": 0.0, "act": 0.0, "turn": 0.0}
    fill_read, score_read = [0.0] * 16, [0.0] * 16

    def fill():
        while order and (UNITS[order[0]][0] == NC - 1 or t["pe"] > LOAD_NS):
            free = fill_read[-FB] + HANDOFF <= t["pe"]
            if not (t["dve"] < t["pe"] + AHEAD or score_read[-SB] + HANDOFF > t["pe"]) or not free:
                break
            i = order.pop(0)
            g, t4, h, n, part, w = UNITS[i]
            ev.append(("unit", i))
            t["pe"] = max(t["pe"], fill_read[-FB] + HANDOFF) + n * (w / 2.4 + 3) + (n * 56.0 if part == g else 0.0)
            t["dve"] = max(t["dve"], t["pe"] + HANDOFF) + n * w / 0.96 + 66.0
            fill_read.append(t["dve"])
            if i in LAST_UNIT_OF_GROUP:
                ev.append(("finish", g))
                t["dve"] += 250.0
                later.append((t["dve"] + MAX_NS, "turn_max", g))
                later.append((TAKE_NS, "take_max", g))

    def tick():
        while later and t["pe"] >= later[0][0] + (t["turn"] if later[0][1].startswith("take") else 0.0):
            _, kind, g = later.pop(0)
            ev.append((kind, g))
            if kind.startswith("turn"):
                t["pe"] += 107.0 if kind == "turn_max" else 430.0
                t["turn"] = t["pe"]
            t["dve"] += {"take_max": 700.0, "take_out": 1100.0, "take_out_prev": 1100.0}.get(kind, 0.0)

    def weigh(s, suffix):
        qc, kt = STEPS[s]
        ev.append(("weigh" + suffix, s))
        t["pe"] = max(t["pe"], score_read[-QH * LAG - 1] + HANDOFF) + 930.0 * (CH - max(kt - 4 * qc, 0) * P) / CH
        if kt == 4 * qc + 3:
            ev.append(("read_out" + suffix, qc))
            later.append((t["pe"] + OUT_NS, "turn_out" + suffix, qc))
            later.append((TAKE_NS, "take_out" + suffix, qc))

    for s in range(NS):
        qc, kt = STEPS[s]
        for h in range(QH):
            ev.append(("score", (s, h)))
            w = CH - max(kt - 4 * qc, 0) * P
            t["pe"] = max(t["pe"], score_read[-SB] + HANDOFF) + w / 2.4 + 3
            t["act"] = max(t["act"], t["pe"] + HANDOFF) + w / 1.2 + 50.0
            score_read.append(t["act"])
            tick()
            fill()
        weigh(s - LAG if s >= LAG else NS - LAG + s, "" if s >= LAG else "_prev")
        tick()
        fill()
    left = len(order)
    while order:
        t["pe"] = max(t["pe"], t["dve"])
        fill()
        tick()
    while later:
        t["pe"] += 100.0
        tick()
    return ev, left, t


EVENTS, _, _ = quad_events()
TAIL = [e for e in EVENTS if e[0].endswith("_prev")]
TURNS = [e for e in EVENTS if e[0].startswith("turn_")]
assert TURNS[0] == ("turn_out_prev", NC - 1)


def bank(i, par, banks, per):
    return (i + par * per) % banks


def read_before(q, par, i, banks, per):
    if i >= banks:
        return q * per + i - banks + 1
    last = max(m for m in range(per) if bank(m, 1 - par, banks, per) == bank(i, par, banks, per))
    return (q - 1) * per + last + 1


def looped(eng, n):
    def run(body):
        body(0)
        with eng.Fori(1, n) as i:
            body(i)
    return run


def over_batches(eng, body):
    body(0, True)
    with eng.Fori(1, B - 1) as b:
        body(b, True)
    body(B - 1, False)


def at_least(eng, sem, n):
    if not isinstance(n, int) or n > 0:
        eng.wait_ge(sem, n)


def build_constants(nc, ctx):
    ident = ctx.enter_context(nc.sbuf_tensor("ident", [P, P], F32))
    identb = ctx.enter_context(nc.sbuf_tensor("identb", [P, P], BF16))
    maskb = ctx.enter_context(nc.sbuf_tensor("maskb", [P, P], BF16))
    made = ctx.enter_context(nc.semaphore("constants_made"))
    with nc.Block() as block:
        @block.gpsimd
        def _(pool):
            nc.gpsimd.memset(ident[:], 0.0).then_inc(made, 1)
            nc.gpsimd.memset(maskb[:], 0.0).then_inc(made, 1)
            pool.wait_ge(made, 2)
            nc.gpsimd.affine_select(out=ident[:], in_=ident[:], compare_op=ALU.not_equal, fill=1.0, base=0,
                                    pattern=[[-1, P]], channel_multiplier=1).then_inc(made, 1)
            nc.gpsimd.affine_select(out=maskb[:], in_=maskb[:], compare_op=ALU.is_ge, fill=MASKED, base=0,
                                    pattern=[[-1, P]], channel_multiplier=1).then_inc(made, 1)
            pool.wait_ge(made, 4)
            nc.gpsimd.tensor_copy(identb[:], ident[:]).then_inc(made, 1)
            pool.wait_ge(made, 5)
    return ident, identb, maskb


def build_project(nc, c, x, wq, wk, wv, w_out, qparts, kparts, vstore):
    X, wsum, ident = c["X"], c["wsum"], c["ident"]
    with ExitStack() as ctx:
        def sb(n, s, t): return ctx.enter_context(nc.sbuf_tensor(n, s, t))
        def ps(n, s, t): return ctx.enter_context(nc.psum_tensor(n, s, t))
        def sem(n): return ctx.enter_context(nc.semaphore(n))
        passed = sem("passed0")
        wqk = sb("wqk", [P, 2, KD, D], F32)
        wvs = sb("wvs", [P, KD, D], F32)
        wos = sb("wos", [P, KD, D], F32)
        ones = sb("ones", [P, P], F32)
        stats = sb("stats", [P, J, 6], F32)
        mv = sb("mv", [P, J, 2], F32)
        std = sb("std", [P, J], F32)
        rstd = sb("rstd", [P, J], F32)
        xn = sb("xn", [P, J, D], F32)
        xT = sb("xT", [P, KD, S], F32)
        RS = 4
        parts = sb("parts", [P, RS, 3, CH], BF16)
        rest = sb("rest", [P, RS, CH], F32)
        vst = sb("vst", [P, 2, NC, 4, QH * VW], F32)
        tp = ps("tp", [P, 2, CH], F32)
        pj = ps("pj", [P, RS, CH], F32)
        vp = ps("vp", [P, 2, CH], F32)
        epst = sb("epst", [P, 1], F32)

        w_loaded, x_loaded = sem("w_loaded"), sem("x_loaded")
        x0_in = [sem(f"x0_in{i}") for i in range(4)]
        ones_made, v_consts = sem("ones_made"), sem("v_consts")
        stat_done, mv_done, std_done, rstd_done, xn_done = (sem(n) for n in
                                                           ("stat_done", "mv_done", "std_done", "rstd_done", "xn_done"))
        turned, turn_free, xT_done = sem("turned"), sem("turn_free"), sem("xT_done")
        proj_done, part1, left1, part2, part3 = (sem(n) for n in
            ("proj_done", "part1", "left1", "part2", "part3"))
        parts_out = [sem(f"parts_out{i}") for i in range(RS)]
        v_done, v_put = sem("v_done"), sem("v_put")
        v_out = [sem(f"v_out{i}") for i in range(2)]
        wsum_done, wsum_put = sem("wsum_done"), sem("wsum_put")
        DEVIATION_AT = 10
        NG = 2 * KD * NC
        groups = [(w, half, ch) for w in range(2) for ch in range(NC) for half in range(2)]

        with nc.Block() as block:
            @block.sync
            def _(sp):
                for i in range(4):
                    sp.dma_start(X[:, 0, 4 * i:4 * i + 4], x[0, :, 4 * i:4 * i + 4]).then_inc(x0_in[i], 16)
                for b in range(1, B):
                    sp.dma_start(X[:, b], x[b]).then_inc(x_loaded, 16)
                    sp.wait_ge(x_loaded, 16 * b)

                def body(b, more):
                    for i, (w, half, ch) in enumerate(groups):
                        dst = (qparts, kparts)[w]
                        sp.wait_ge(part3, b * NG + i + 1)
                        for qd in range(2):
                            sp.dma_start(dst[ds(b * 4 + half * 2 + qd, 1), ch].rearrange("o r i (h s) -> (o i h) r s", h=QH),
                                         parts[64 * qd:64 * qd + 64, i % RS]).then_inc(parts_out[i % RS], 16)
                    for g in range(4):
                        sp.wait_ge(v_put, b * J + 4 * g + 4)
                        sp.dma_start(vstore[ds(b * 4, 4), :, 4 * g:4 * g + 4].rearrange("q p k w -> p q (k w)"),
                                     vst[:, g % 2].rearrange("p q k w -> p q (k w)")).then_inc(v_out[g % 2], 16)
                over_batches(sp, body)
                for i in range(RS):
                    sp.wait_ge(parts_out[i], 32 * B * NG // RS)
                sp.wait_ge(v_out[0], 16 * B * 2)
                sp.wait_ge(v_out[1], 16 * B * 2)

            @block.gpsimd
            def _(pool):
                nc.gpsimd.memset(epst[:], EPS).then_inc(ones_made, 1)
                nc.gpsimd.memset(ones[:], 1.0).then_inc(ones_made, 1)
                v5 = vst.rearrange("p a q k (h w) -> p (a q k h) w", w=VW)
                nc.gpsimd.memset(v5[:, :, HD:VW], 0.0).then_inc(v_consts, 1)
                pool.wait_ge(v_consts, 1)
                nc.gpsimd.memset(v5[:, :, HD:HD + 1], 1.0).then_inc(v_consts, 1)

            @block.scalar
            def _(act):
                for dst, src in ((wqk[:, 0], wq), (wqk[:, 1], wk), (wvs[:], wv), (wos[:], w_out)):
                    nc.scalar.dma_start(dst, src).then_inc(w_loaded, 16)
                act.wait_ge(ones_made, 2)

                def deviation(b):
                    act.wait_ge(mv_done, b * J + J)
                    at_least(act, rstd_done, b)
                    nc.scalar.activation(std[:], mv[:, :, 1], ACT.Sqrt, bias=epst[:, 0:1]).then_inc(std_done, 1)

                def copy_part2(b, i):
                    act.wait_ge(left1, b * NG + i + 1)
                    nc.scalar.copy(parts[:, i % RS, 1], rest[:, i % RS]).then_inc(part2, 1)

                def body(b, more):
                    for i in range(4):
                        act.wait_ge(turned, b * 8 + 2 * i + 1)
                        if i == 0:
                            at_least(act, proj_done, b * NG)
                            at_least(act, v_done, b * J)
                        nc.scalar.copy(xT[:, 0].rearrange("d (p j) -> d j p", j=J)[:, 4 * i:4 * i + 4],
                                       tp[:, 0].rearrange("d (j p) -> d j p", p=P)).then_inc(turn_free, 1)
                    for i in range(NG):
                        act.wait_ge(proj_done, b * NG + i + 1)
                        at_least(act, parts_out[i % RS], (b * (NG // RS) + i // RS) * 32)
                        nc.scalar.copy(parts[:, i % RS, 0], pj[:, i % RS]).then_inc(part1, 1)
                        if i:
                            copy_part2(b, i - 1)
                    copy_part2(b, NG - 1)
                    for kt in range(J):
                        sl = (kt // 4) % 2
                        act.wait_ge(v_done, b * J + kt + 1)
                        if kt == 0 and isinstance(b, int) and b == 0:
                            act.wait_ge(v_consts, 2)
                        if kt % 4 == 0:
                            at_least(act, v_out[sl], (b * 2 + kt // 8) * 16)
                        nc.scalar.copy(
                            vst[:, sl, :, kt % 4].rearrange("p q (h w) -> p q h w", w=VW)[:, :, :, 0:HD],
                            vp[:, kt % 2, 0:D].rearrange("p (q h w) -> p q h w", q=4, w=HD)).then_inc(v_put, 1)
                        if kt == DEVIATION_AT and more:
                            deviation(b + 1)
                deviation(0)
                over_batches(act, body)

            @block.vector
            def _(dve):
                def row_stats(b, j, n):
                    if j == 0:
                        at_least(dve, mv_done, b * J)
                    for i in range(j, j + n):
                        nc.vector.bn_stats(stats[:, i], X[:, ds(b, 1), i].rearrange("p o d -> p (o d)")).then_inc(stat_done, 1)

                def gather_stats(b):
                    at_least(dve, xn_done, b * J)
                    for j in range(J):
                        dve.wait_ge(stat_done, b * J + j + 1).then_inc(passed, 1)
                        nc.vector.bn_aggr(mv[:, j], stats[:, j]).then_inc(mv_done, 1)

                def normalise(b):
                    dve.wait_ge(std_done, b + 1)
                    nc.vector.reciprocal(rstd[:], std[:]).then_inc(rstd_done, 1)
                    dve.wait_ge(rstd_done, b + 1)
                    at_least(dve, turned, b * 8)
                    for j in range(J):
                        nc.vector.tensor_scalar(xn[:, j], X[:, ds(b, 1), j].rearrange("p o d -> p (o d)"),
                                                mv[:, j, 0:1], rstd[:, j:j + 1],
                                                ALU.subtract, ALU.mult).then_inc(xn_done, 1)

                def subtract_part2(b, i):
                    dve.wait_ge(part2, b * NG + i + 1)
                    nc.vector.tensor_tensor(parts[:, i % RS, 2], rest[:, i % RS], parts[:, i % RS, 1],
                                            ALU.subtract).then_inc(part3, 1)

                def body(b, more):
                    for i in range(4):
                        dve.wait_ge(turned, b * 8 + 2 * i + 2)
                        if i == 0:
                            at_least(dve, proj_done, b * NG)
                            at_least(dve, v_done, b * J)
                        nc.vector.tensor_copy(xT[:, 1].rearrange("d (p j) -> d j p", j=J)[:, 4 * i:4 * i + 4],
                                              tp[:, 1].rearrange("d (j p) -> d j p", p=P)).then_inc(xT_done, 1)
                    for i in range(NG):
                        dve.wait_ge(part1, b * NG + i + 1)
                        at_least(dve, part3, b * NG + i - RS + 1)
                        nc.vector.tensor_tensor(rest[:, i % RS], pj[:, i % RS], parts[:, i % RS, 0],
                                                ALU.subtract).then_inc(left1, 1)
                        if i:
                            subtract_part2(b, i - 1)
                        if i == 0 and more:
                            dve.wait_ge(x_loaded, 16 * (b + 1))
                        if i % 2 and more:
                            row_stats(b + 1, i // 2, 1)
                    subtract_part2(b, NG - 1)
                    if more:
                        row_stats(b + 1, NG // 2, J - NG // 2)
                        gather_stats(b + 1)
                        normalise(b + 1)
                for i in range(4):
                    dve.wait_ge(x0_in[i], 16)
                    row_stats(0, 4 * i, 4)
                gather_stats(0)
                normalise(0)
                dve.wait_ge(wsum_done, 1)
                for r in range(B):
                    nc.vector.tensor_copy(wsum[:, r * D:(r + 1) * D], vp[:, 0, 0:D]).then_inc(wsum_put, 1)
                over_batches(dve, body)

            @block.tensor
            def _(pe):
                def body(b, more):
                    for i in range(4):
                        for half in range(2):
                            pe.wait_ge(xn_done, b * J + 4 * i + 4)
                            at_least(pe, (turn_free, xT_done)[half], b * 4 + i)
                            for j in range(4):
                                last = nc.tensor.transpose(tp[:, half, j * P:(j + 1) * P],
                                                           xn[:, 4 * i + j, half * P:(half + 1) * P], ident[:])
                            last.then_inc(turned, 1)
                    pe.wait_ge(turn_free, b * 4 + 4)
                    pe.wait_ge(xT_done, b * 4 + 4)
                    for i, (w, half, ch) in enumerate(groups):
                        at_least(pe, left1, b * NG + i - RS + 1)
                        for k in range(KD):
                            last = nc.tensor.matmul(pj[:, i % RS], wqk[:, w, k, half * P:(half + 1) * P],
                                                    xT[:, k, ch * CH:(ch + 1) * CH], start=(k == 0), stop=(k == KD - 1))
                        last.then_inc(proj_done, 1)
                    for kt in range(J):
                        if kt == 0 and isinstance(b, int) and b == 0:
                            pe.wait_ge(wsum_put, B)
                        at_least(pe, v_put, b * J + kt - 1)
                        for k in range(KD):
                            last = nc.tensor.matmul(vp[:, kt % 2, 0:D], xT[:, k, kt * P:(kt + 1) * P], wvs[:, k],
                                                    start=(k == 0), stop=(k == KD - 1))
                        last.then_inc(v_done, 1)
                pe.wait_ge(w_loaded, 64)
                pe.wait_ge(ones_made, 2)
                for k in range(KD):
                    last = nc.tensor.matmul(vp[:, 0, 0:D], ones[:], wos[:, k], start=(k == 0), stop=(k == KD - 1))
                last.then_inc(wsum_done, 1)
                over_batches(pe, body)


def build_attend(nc, c, qparts, kparts, vstore, yrows):
    X, wsum, ident, identb, maskb = c["X"], c["wsum"], c["ident"], c["identb"], c["maskb"]
    with ExitStack() as ctx:
        def sb(n, s, t): return ctx.enter_context(nc.sbuf_tensor(n, s, t))
        def ps(n, s, t): return ctx.enter_context(nc.psum_tensor(n, s, t))
        def sem(n): return ctx.enter_context(nc.semaphore(n))
        passed = sem("passed1")
        Q = sb("Q", [P, 2, NC, QH, CH], BF16)
        K = sb("K", [P, 2, NC, QH, CH], BF16)
        V = sb("V", [P, 2, J, QH * VW], F32)
        NP = 4
        probs = sb("probs", [P, NP, QH, CH], F32)
        maxima = sb("maxima", [P, NC, QH, 4, 4], F32)
        negmax = sb("negmax", [P, NC, QH * 4], F32)
        mparts = sb("mparts", [QH * 4, NC, MROWS, P], BF16)
        mrest = sb("mrest", [QH * 4, NC, P], F32)
        outs = sb("outs", [P, NC, CH], F32)
        recip = sb("recip", [P, NC, 4, QH], F32)
        weight = sb("weight", [P, NC, 4, QH], F32)
        addend = sb("addend", [P, NC, 4, QH, J], F32)
        ZC = C64 * 2 * D // (2 * NQ)
        zeros = sb("zeros", [P, ZC], F32)
        zeros_made, y_zeroed = sem("zeros_made"), sem("y_zeroed")
        scores = ps("scores", [P, SB, CH], F32)
        fill = ps("fill", [P, FB, CH], F32)
        acc = ps("acc", [P, CH], F32)
        turn = ps("turn", [P, CH], F32)

        loaded = [[sem(f"loaded{i}{g}") for g in range(NC)] for i in range(2)]
        v_loaded = [sem(f"v_loaded{i}") for i in range(2)]
        rows_in = [[sem(f"rows_in{i}{g}") for g in range(NC)] for i in range(2)]
        ones_made = sem("k_ones_made")
        scores_ready, probs_ready, masked, pv_done = (sem(n) for n in ("scores_ready", "probs_ready", "masked", "pv_done"))
        fill_ready, fill_read, negmax_ready = sem("fill_ready"), sem("fill_read"), sem("negmax_ready")
        turned_out, turned_max, outs_ready = sem("turned_out"), sem("turned_max"), sem("outs_ready")
        part1, left1, part2, part3 = sem("m_part1"), sem("m_left1"), sem("m_part2"), sem("m_part3")
        recip_ready, weight_ready, addend_ready, added = (sem(n) for n in
            ("recip_ready", "weight_ready", "addend_ready", "added"))
        ROWS_SENT = 16 * MROWS
        QK_SENT = 16 * 6

        def loop_quads(eng, body):
            body(0, 0, True)
            body(0, 1, True)
            with eng.Fori(1, NQ // 2 - 1) as i:
                body(i, 0, True)
                body(i, 1, True)
            body(NQ // 2 - 1, 0, True)
            body(NQ // 2 - 1, 1, False)

        def events_of(q, more):
            first = isinstance(q, int) and q == 0
            return [e for e in EVENTS if not (first and e[0].endswith("_prev"))
                    and (more or not for_next(e))]

        def for_next(e):
            kind, x = e
            return (kind == "unit" and UNITS[x][0] < NC - 1) or (kind in ("finish", "turn_max", "take_max") and x < NC - 1)

        def split(kind):
            return (kind[:-5], 1) if kind.endswith("_prev") else (kind, 0)

        def columns(s):
            qc, kt = STEPS[s]
            return max(kt - 4 * qc, 0) * P

        with nc.Block() as block:
            @block.sync
            def _(sp):
                def load(q, par):
                    for g in range(NC):
                        for r, src, copies, dst, store in ((0, 0, 3, Q, qparts), (3, 1, 2, Q, qparts), (5, 2, 1, Q, qparts)):
                            sp.dma_start(dst[16 * r:16 * (r + copies), par, g],
                                         store[ds(q, 1), g, src:src + 1].rearrange("o r i x -> (o r) i x")
                                         .to_broadcast([copies, HD, QH * CH])).then_inc(loaded[par][g], 16)
                        for r, parts in ((0, 3), (3, 2), (5, 1)):
                            sp.dma_start(K[16 * r:16 * (r + parts), par, g],
                                         kparts[ds(q, 1), g, 0:parts].rearrange("o r i x -> (o r i) x")).then_inc(loaded[par][g], 16)

                def load_v(q, par):
                    sp.dma_start(V[:, par], vstore[ds(q, 1)].rearrange("o p k w -> p (o k) w")).then_inc(v_loaded[par], 16)

                def rows(q, par, chunks):
                    for g in chunks:
                        sp.wait_ge(part3, q * NC + g + 1)
                        for r in range(MROWS):
                            sp.dma_start(Q[EPS_ROWS + r:EPS_ROWS + r + 1, par, g].rearrange("o h s -> o (h s)"),
                                         mparts[:, g, r]).then_inc(rows_in[par][g], 16)

                def body(pr, par, more):
                    q = pr * 2 + par
                    if more:
                        at_least(sp, scores_ready, q * NS * QH)
                        load(q + 1, 1 - par)
                        at_least(sp, pv_done, q * NS)
                        load_v(q + 1, 1 - par)
                    rows(q, par, [NC - 1])
                    sp.dma_start(yrows[0:B * S * 2].rearrange("(p g r) d -> g p (r d)", p=P, g=2 * NQ)[ds(q * 2, 2)]
                                 .rearrange("g p x -> p g x"), zeros[:].unsqueeze(1).to_broadcast([P, 2, ZC])).then_inc(y_zeroed, 16)
                    if more:
                        rows(q + 1, 1 - par, range(NC - 1))

                load(0, 0)
                load_v(0, 0)
                rows(0, 0, range(NC - 1))
                sp.wait_ge(zeros_made, 1)
                loop_quads(sp, body)
                sp.wait_ge(y_zeroed, 16 * NQ)

            @block.gpsimd
            def _(pool):
                nc.gpsimd.memset(zeros[:], 0.0).then_inc(zeros_made, 1)
                pool.wait_ge(zeros_made, 1)
                nc.gpsimd.memset(K[EPS_ROWS:P, :, :, :], 1.0).then_inc(ones_made, 1)

                def max_parts(g, n):
                    pool.wait_ge(left1, n + 1).then_inc(passed, 1)
                    nc.gpsimd.tensor_copy(mparts[:, g, 1], mrest[:, g]).then_inc(part2, 1)
                    pool.wait_ge(part2, n + 1)
                    nc.gpsimd.tensor_tensor(mparts[:, g, 2], mrest[:, g], mparts[:, g, 1],
                                            ALU.subtract).then_inc(part3, 1)

                def mask(q, s):
                    pool.wait_ge(probs_ready, (q * NS + s + 1) * QH).then_inc(passed, 1)
                    c0 = columns(s)
                    diag = probs[:, s % NP, :, c0:c0 + P]
                    nc.gpsimd.affine_select(out=diag, in_=diag, compare_op=ALU.is_ge, fill=0.0, base=0,
                                            pattern=[[0, QH], [1, P]], channel_multiplier=-1).then_inc(masked, 1)

                def add(b, k, q, qc):
                    pool.wait_ge(addend_ready, q * NC + qc + 1)
                    dst = X[:, ds(b, 1)].rearrange("p o j (n t) -> p (o n) t j", t=J)[
                        :, k * QH:(k + 1) * QH, 4 * qc:4 * qc + 4].rearrange("p n t j -> p t n j")
                    nc.gpsimd.tensor_tensor(dst, dst, addend[:, qc], ALU.add).then_inc(added, 1)

                def quad(b, k, more, events=None):
                    q = b * 4 + k
                    for kind, x in events or events_of(q, more):
                        kind, back = split(kind)
                        if kind == "score" and x[1] == QH - 1 and STEPS[x[0]][1] >= 4 * STEPS[x[0]][0]:
                            mask(q, x[0])
                        elif kind == "take_max":
                            max_parts(x, (q + (x < NC - 1)) * NC + x)
                        elif kind == "take_out":
                            if back:
                                add(b - (k == 0), (k - 1) % 4, q - 1, x)
                            else:
                                add(b, k, q, x)

                for g in range(NC - 1):
                    max_parts(g, g)
                for k in range(4):
                    quad(0, k, True)
                with pool.Fori(1, B - 1) as b:
                    for k in range(4):
                        quad(b, k, True)
                for k in range(4):
                    quad(B - 1, k, k < 3)
                quad(B, 0, False, TAIL)
                pool.wait_ge(added, NQ * NC)

            @block.scalar
            def _(act):
                def read_out(q, qc):
                    act.wait_ge(pv_done, q * NS + 2 * (qc + 1) * (qc + 2))
                    at_least(act, turned_out, (q - 1) * NC + qc + 1)
                    nc.scalar.copy(outs[:, qc], acc[:]).then_inc(outs_ready, 1)

                def body(pr, par, more, events=None):
                    q = pr * 2 + par
                    for kind, x in events or events_of(q, more):
                        kind, back = split(kind)
                        if kind == "score":
                            s, h = x
                            act.wait_ge(scores_ready, (q * NS + s) * QH + h + 1)
                            if h == 0:
                                at_least(act, pv_done, q * NS + s - NP + 1)
                            c0 = columns(s)
                            nc.scalar.activation(probs[:, s % NP, h, c0:CH], scores[:, bank(s * QH + h, par, SB, NS * QH), c0:CH],
                                                 ACT.Exp, scale=SCALE).then_inc(probs_ready, 1)
                        elif kind == "read_out":
                            read_out(q - back, x)
                loop_quads(act, body)
                body(NQ // 2, 0, False, TAIL)

            @block.vector
            def _(dve):
                def reduce_unit(q, par, i):
                    g, t4, h, n, part, w = UNITS[i]
                    dve.wait_ge(fill_ready, q * NU + i + 1)
                    nc.vector.tensor_reduce(maxima[:, g, h:h + n, t4, part],
                                            fill[:, bank(i, par, FB, NU), 0:n * w].rearrange("p (h w) -> p h w", w=w),
                                            AXX, ALU.max).then_inc(fill_read, 1)

                def finish(q, g):
                    dve.wait_ge(fill_read, q * NU + LAST_UNIT_OF_GROUP[g] + 1)
                    at_least(dve, turned_max, (q - 1) * NC + g + 1)
                    nc.vector.tensor_reduce(negmax[:, g], maxima[:, g, :, :, 0:g + 1].rearrange("p h t r -> p (h t) r"),
                                            AXX, ALU.max, negate=True).then_inc(negmax_ready, 1)

                def take_max(pr, par, g):
                    n = (pr * 2 + par) * NC + g
                    dve.wait_ge(turned_max, n + 1)
                    at_least(dve, rows_in[1 - par][g], (pr + par) * ROWS_SENT)
                    nc.vector.tensor_copy(mparts[:, g, 0], turn[0:QH * 4, 0:P]).then_inc(part1, 1)
                    dve.wait_ge(part1, n + 1)
                    nc.vector.tensor_tensor(mrest[:, g], turn[0:QH * 4, 0:P], mparts[:, g, 0],
                                            ALU.subtract).then_inc(left1, 1)

                def take_out(q, qc):
                    n = q * NC + qc
                    dve.wait_ge(turned_out, n + 1)
                    at_least(dve, added, (q - 1) * NC + qc + 1)
                    t = turn.rearrange("p (t h w) -> p t h w", t=4, w=VW)
                    nc.vector.reciprocal(recip[:, qc], t[:, :, :, HD]).then_inc(recip_ready, 1)
                    dve.wait_ge(recip_ready, n + 1)
                    nc.vector.tensor_tensor(weight[:, qc], recip[:, qc],
                                            wsum[:, ds(q * QH * J, QH * J)].rearrange("p (h t) -> p t h", t=J)[:, 4 * qc:4 * qc + 4],
                                            ALU.mult).then_inc(weight_ready, 1)
                    dve.wait_ge(weight_ready, n + 1)
                    nc.vector.tensor_tensor(addend[:, qc], t[:, :, :, 0:HD],
                                            weight[:, qc].unsqueeze(3).to_broadcast([P, 4, QH, HD]),
                                            ALU.mult).then_inc(addend_ready, 1)

                def body(pr, par, more, events=None):
                    q = pr * 2 + par
                    for kind, x in events or events_of(q, more):
                        kind, back = split(kind)
                        if kind == "unit":
                            reduce_unit(q + for_next((kind, x)), 1 - par if for_next((kind, x)) else par, x)
                        elif kind == "finish":
                            finish(q + for_next((kind, x)), x)
                        elif kind == "take_max":
                            take_max(*((pr + par, 1 - par) if for_next((kind, x)) else (pr, par)), x)
                        elif kind == "take_out":
                            take_out(q - back, x)

                for i in range(FIRST_UNITS):
                    reduce_unit(0, 0, i)
                    if i in LAST_UNIT_OF_GROUP:
                        finish(0, UNITS[i][0])
                        take_max(0, 0, UNITS[i][0])
                loop_quads(dve, body)
                body(NQ // 2, 0, False, TAIL)

            @block.tensor
            def _(pe):
                mm = nc.tensor.matmul

                def fill_unit(pr, par, i):
                    q = pr * 2 + par
                    g, t4, h0, n, part, w = UNITS[i]
                    at_least(pe, fill_read, read_before(q, par, i, FB, NU))
                    if i == 0 or g != UNITS[i - 1][0]:
                        pe.wait_ge(loaded[par][g], (pr + 1) * QK_SENT)
                    for h in range(h0, h0 + n):
                        at = (h - h0) * w
                        last = mm(fill[:, bank(i, par, FB, NU), at:at + w], Q[0:EPS_ROWS, par, g, h, t4 * P:(t4 + 1) * P],
                                  K[0:EPS_ROWS, par, part, h, 0:w], start=True, stop=True, skip_group_check=True)
                        if part == g:
                            last = mm(fill[:, bank(i, par, FB, NU), at + w - P:at + w], identb[:], maskb[:], start=False, stop=True,
                                      skip_group_check=True)
                    last.then_inc(fill_ready, 1)

                def turn_max(q, g):
                    pe.wait_ge(negmax_ready, q * NC + g + 1)
                    nc.tensor.transpose(turn[0:QH * 4, 0:P], negmax[:, g], ident[:]).then_inc(turned_max, 1)

                def turn_out(q, qc):
                    pe.wait_ge(outs_ready, q * NC + qc + 1)
                    for t in range(4):
                        last = nc.tensor.transpose(turn[:, t * P:(t + 1) * P], outs[:, qc, t * P:(t + 1) * P], ident[:])
                    last.then_inc(turned_out, 1)

                def read_of_turn(q, use):
                    kind, back = split(use[0])
                    if kind == "turn_max":
                        return left1, (q + for_next(use)) * NC + use[1] + 1
                    return addend_ready, (q - back) * NC + use[1] + 1

                def turn_free(q, event, uses):
                    at = uses.index(event)
                    if at > 0:
                        pe.wait_ge(*read_of_turn(q, uses[at - 1]))
                    elif isinstance(q, int) and q == 0:
                        pe.wait_ge(left1, NC - 1)
                    elif isinstance(q, int) and q == NQ:
                        pe.wait_ge(*read_of_turn(q - 1, [e for e in TURNS if not for_next(e)][-1]))
                    else:
                        pe.wait_ge(*read_of_turn(q - 1, TURNS[-1]))

                def score(q, pr, par, s, h):
                    qc, kt = STEPS[s]
                    c0 = columns(s)
                    if kt == 0 and h == 0:
                        pe.wait_ge(rows_in[par][qc], (pr + 1) * ROWS_SENT)
                    n = s * QH + h
                    at_least(pe, probs_ready, read_before(q, par, n, SB, NS * QH))
                    mm(scores[:, bank(n, par, SB, NS * QH), c0:CH], K[0:KROWS, par, kt // 4, h, kt % 4 * P:(kt % 4 + 1) * P],
                       Q[0:KROWS, par, qc, h, c0:CH], start=True, stop=True).then_inc(scores_ready, 1)

                def weigh(q, pr, par, s):
                    qc, kt = STEPS[s]
                    c0 = columns(s)
                    if s == 0:
                        pe.wait_ge(v_loaded[par], (pr + 1) * 16)
                    pe.wait_ge(probs_ready, (q * NS + s + 1) * QH)
                    if kt >= 4 * qc:
                        pe.wait_ge(masked, (q * NC + qc) * 4 + kt - 4 * qc + 1)
                    if kt == 0:
                        at_least(pe, outs_ready, q * NC + qc)
                    for h in range(QH):
                        last = mm(acc[VW * h:VW * h + VW, c0:CH], V[:, par, kt, VW * h:VW * h + VW],
                                  probs[:, s % NP, h, c0:CH], start=(kt == 0), stop=(kt == 4 * qc + 3),
                                  skip_group_check=True)
                    last.then_inc(pv_done, 1)

                def body(pr, par, more, events=None):
                    q = pr * 2 + par
                    todo = events or events_of(q, more)
                    uses = [e for e in todo if e[0].startswith("turn_")]
                    for kind, x in todo:
                        event = (kind, x)
                        kind, back = split(kind)
                        if kind == "score":
                            score(q, pr, par, *x)
                        elif kind == "weigh":
                            weigh(q - back, pr - (1 - par) if back else pr, 1 - par if back else par, x)
                        elif kind == "unit":
                            fill_unit(*((pr + par, 1 - par) if for_next(event) else (pr, par)), x)
                        elif kind == "turn_max":
                            turn_free(q, event, uses)
                            turn_max(q + for_next(event), x)
                        elif kind == "turn_out":
                            turn_free(q, event, uses)
                            turn_out(q - back, x)

                pe.wait_ge(ones_made, 1)
                for i in range(FIRST_UNITS):
                    fill_unit(0, 0, i)
                    if i in LAST_UNIT_OF_GROUP:
                        if i != LAST_UNIT_OF_GROUP[0]:
                            pe.wait_ge(left1, UNITS[i][0])
                        turn_max(0, UNITS[i][0])
                loop_quads(pe, body)
                body(NQ // 2, 0, False, TAIL)


def first_floats(X, n):
    return X.rearrange("p b j d -> p (b j d)")[:, 0:n]


def build_route(nc, c, gate_w, wi_gate, wi_up, wo, xrows, x1rows):
    X, ident = c["X"], c["ident"]
    rowof, dest, W = c["rowof"], c["dest"], c["W"]
    with ExitStack() as ctx:
        def sb(n, s, t): return ctx.enter_context(nc.sbuf_tensor(n, s, t))
        def ps(n, s, t): return ctx.enter_context(nc.psum_tensor(n, s, t))
        def sem(n): return ctx.enter_context(nc.semaphore(n))
        passed = sem("passed2")
        EW = 32
        gw = sb("gw", [P, KD, EW], F32)
        epst = sb("r_eps", [P, 1], F32)
        before = sb("before", [P, P], F32)
        ones = sb("r_ones", [P, P], F32)
        zero_r = sb("zero_r", [P, 2 * KT], F32R)
        lane = sb("lane", [P, P], BF16)
        tile_no = sb("tile_no", [P, 2, KT], BF16)
        row_no = sb("row_no", [P, C64], F32)
        row_code = sb("row_code", [P, C64], F32)
        spare = sb("spare", [P, 2, KT], F32)
        expert_no = sb("expert_no", [P, E], F32)
        rank = sb("rank", [P, E], F32)
        stats = sb("r_stats", [P, J, 6], F32)
        mv = sb("r_mv", [P, J, 2], F32)
        std = sb("r_std", [P, J], F32)
        rstd = sb("r_rstd", [P, J], F32)
        xn = sb("r_xn", [P, B, J, D], F32)
        lgT = sb("lgT", [P, CH], F32)
        logits = sb("logits", [P, B, 4, 4, E], F32)
        xT = sb("r_xT", [P, KD, J, P], F32)
        small = [P, C64, E]
        shifted, ex, pr = sb("shifted", small, F32), sb("ex", small, F32), sb("pr", small, F32)
        eq, cand = sb("eq", small, F32), sb("cand", small, F32)
        top, total, rtotal, best = (sb(n, [P, C64], F32) for n in ("top", "total", "rtotal", "best"))
        hot = sb("hot", [P, 2, C64, E], F32)
        prob = sb("prob", [P, 2, C64], F32)
        count = sb("count", [P, 2, 2 * B, J, E], F32)
        sums = sb("sums", [P, 2, B, E], F32)
        offset = sb("offset", [P, 2, B, E], F32)
        place, eno, valid, slot = (sb(n, [P, 2, C64], F32) for n in ("place", "eno", "valid", "slot"))
        slot_i, hi_i, lo_i = (sb(n, [P, 2, C64], I32) for n in ("slot_i", "hi_i", "lo_i"))
        hi, lo = sb("hi", [P, 2, C64], F32), sb("lo", [P, 2, C64], F32)
        LS = 8
        is_lane = sb("is_lane", [P, LS, P], F32R)
        is_tile = sb("is_tile", [P, LS, KT], BF16)
        value = sb("value", [P, LS, KT], F32R)
        tabr, tabd, used = (sb(n, [P, 2, KT], F32) for n in ("tabr", "tabd", "used"))
        tp = ps("r_tp", [P, 2, CH], F32)
        lgp = ps("lgp", [P, CH], F32)
        lgb = ps("lgb", [P, 4, 4, EW], F32)
        sums_before = ps("sums_before", [P, 2, 64], F32)
        table = ps("table", [P, 2, KT], F32)

        raw = first_floats(X, PIECES * KD * F).rearrange("p (i f) -> p i f", i=PIECES)
        x1_out, w0_in = sem("x1_out"), sem("w0_in")
        gw_loaded, consts, stat_done, mv_done, std_done, rstd_done, xn_done = (sem("r_" + n) for n in
            ("gw_loaded", "consts", "stat_done", "mv_done", "std_done", "rstd_done", "xn_done"))
        turned, turn_free, logits_done, rows_out = (sem("r_" + n) for n in
            ("turned", "turn_free", "logits_done", "rows_out"))
        lg_made, lg_copied, lg_back, gw_zeroed = (sem("r_" + n) for n in ("lg_made", "lg_copied", "lg_back", "gw_zeroed"))
        step, exp_done, sums_ready, ranked, hot_tiles, valued, tabled, table_done, shift_ready = (sem("r_" + n) for n in
            ("step", "exp_done", "sums_ready", "ranked", "hot_tiles", "valued", "tabled", "table_done", "shift_ready"))

        with nc.Block() as block:
            @block.sync
            def _(sp):
                sp.wait_ge(gw_zeroed, 1)
                sp.dma_start(gw[:, :, 0:E], gate_w).then_inc(gw_loaded, 16)
                for b in range(B):
                    sp.dma_start(x1rows[b], X[:, b]).then_inc(x1_out, 16)
                for b in range(B):
                    sp.wait_ge(xn_done, b * J + J)
                    sp.dma_start(xrows.rearrange("(p b j) d -> p b j d", b=B, j=J)[:, b],
                                 xn[:, b]).then_inc(rows_out, 16)
                sp.wait_ge(x1_out, 16 * B)
                for i, src in enumerate((wi_gate, wi_up, wo)):
                    sp.dma_start(raw[:, i], src[0].rearrange("p k f -> p (k f)")).then_inc(w0_in, 16)
                sp.wait_ge(rows_out, 16 * B)
                sp.wait_ge(w0_in, 16 * PIECES)

            @block.gpsimd
            def _(pool):
                nc.gpsimd.memset(epst[:], EPS).then_inc(consts, 1)
                nc.gpsimd.memset(gw[:], 0.0).then_inc(gw_zeroed, 1)
                nc.gpsimd.memset(before[:], 0.0).then_inc(consts, 1)
                nc.gpsimd.memset(ones[:], 1.0).then_inc(consts, 1)
                nc.gpsimd.memset(zero_r[:].bitcast(F32), 0.0).then_inc(consts, 1)
                nc.gpsimd.iota(lane[:], pattern=[[1, P]], base=0, channel_multiplier=0,
                               allow_small_or_imprecise_dtypes=True).then_inc(consts, 1)
                for k in range(2):
                    nc.gpsimd.iota(tile_no[:, k], pattern=[[ET, E], [1, ET // 2]], base=k * ET // 2, channel_multiplier=0,
                                   allow_small_or_imprecise_dtypes=True).then_inc(consts, 1)
                nc.gpsimd.iota(row_no[:], pattern=[[1, C64]], base=-HALF, channel_multiplier=C64,
                               allow_small_or_imprecise_dtypes=True).then_inc(consts, 1)
                for k in range(2):
                    nc.gpsimd.iota(spare[:, k], pattern=[[P * ET, E], [P, ET // 2]], base=2 * B * S - k + k * P * ET // 2,
                                   channel_multiplier=1, allow_small_or_imprecise_dtypes=True).then_inc(consts, 1)
                nc.gpsimd.iota(expert_no[:], pattern=[[1, E]], base=0, channel_multiplier=0,
                               allow_small_or_imprecise_dtypes=True).then_inc(consts, 1)
                nc.gpsimd.iota(rank[:], pattern=[[-1, E]], base=E, channel_multiplier=0,
                               allow_small_or_imprecise_dtypes=True).then_inc(consts, 1)
                pool.wait_ge(consts, 12)
                nc.gpsimd.affine_select(out=before[:], in_=before[:], compare_op=ALU.is_ge, fill=1.0, base=0,
                                        pattern=[[-1, P]], channel_multiplier=1).then_inc(consts, 1)

            @block.scalar
            def _(act):
                act.wait_ge(consts, 13)

                def deviation(b):
                    act.wait_ge(mv_done, b * J + J)
                    at_least(act, rstd_done, b)
                    nc.scalar.activation(std[:], mv[:, :, 1], ACT.Sqrt, bias=epst[:, 0:1]).then_inc(std_done, 1)

                def body(b, more):
                    for i in range(4):
                        for half in range(2):
                            act.wait_ge(turned, b * 8 + 2 * i + half + 1)
                            at_least(act, lg_made, b)
                            nc.scalar.copy(xT[:, half, 4 * i:4 * i + 4],
                                           tp[:, half].rearrange("d (j p) -> d j p", p=P)).then_inc(turn_free, 1)
                        if i == 1 and more:
                            deviation(b + 1)
                    act.wait_ge(lg_made, b + 1)
                    at_least(act, lg_back, b)
                    nc.scalar.copy(lgT[:], lgp[:]).then_inc(lg_copied, 1)
                    act.wait_ge(lg_back, b + 1)
                    nc.scalar.copy(logits[:, b],
                                   lgb[:, :, :, 0:E].rearrange("p j i e -> p i j e")).then_inc(logits_done, 1)
                deviation(0)
                for b in range(B):
                    body(b, b + 1 < B)
                act.wait_ge(shift_ready, 1)
                nc.scalar.activation(ex[:], shifted[:], ACT.Exp).then_inc(exp_done, 1)
                @looped(act, B)
                def _(b):
                    for m in range(2 * J):
                        n, at = b * 2 * J + m, ds(b * J + m // 2, 1)
                        at_least(act, tabled, n - LS + 1)
                        act.wait_ge(hot_tiles, n + 1).then_inc(passed, 1)
                        nc.scalar.mul(value[:, m % LS], is_tile[:, m % LS], row_code[:, at]).then_inc(valued, 1)

            @block.tensor
            def _(pe):
                pe.wait_ge(gw_loaded, 16)
                pe.wait_ge(consts, 13)

                def body(b, more):
                    for i in range(4):
                        for half in range(2):
                            pe.wait_ge(xn_done, b * J + 4 * i + 4)
                            at_least(pe, turn_free, b * 8 + 2 * i + half - 1)
                            for j in range(4):
                                last = nc.tensor.transpose(tp[:, half, j * P:(j + 1) * P],
                                                           xn[:, b, 4 * i + j, half * P:(half + 1) * P], ident[:])
                            last.then_inc(turned, 1)
                    pe.wait_ge(turn_free, b * 8 + 8)
                    at_least(pe, lg_copied, b)
                    for k in range(KD):
                        for i in range(4):
                            last = nc.tensor.matmul(lgp[EW * i:EW * i + EW], gw[:, k], xT[:, k, 4 * i:4 * i + 4],
                                                    start=(k == 0), stop=(k == KD - 1), skip_group_check=True)
                    last.then_inc(lg_made, 1)
                    pe.wait_ge(lg_copied, b + 1)
                    at_least(pe, logits_done, b)
                    for j in range(4):
                        last = nc.tensor.transpose(lgb[:, j].rearrange("p i e -> p (i e)"), lgT[:, j * P:(j + 1) * P], ident[:])
                    last.then_inc(lg_back, 1)
                for b in range(B):
                    body(b, b + 1 < B)
                pe.wait_ge(sums_ready, 1)
                cols = sums.rearrange("p k b e -> p (k b e)")
                nc.tensor.matmul(sums_before[:, 0], before[:], cols, start=True, stop=True)
                nc.tensor.matmul(sums_before[:, 1], ones[:], cols, start=True, stop=True).then_inc(ranked, 1)
                whole = table.rearrange("p k t -> p (k t)")
                nc.tensor.matmul(whole, zero_r[:, 0:P], zero_r[:], start=True, stop=False)
                @looped(pe, B)
                def _(b):
                    for m in range(2 * J):
                        pe.wait_ge(valued, b * 2 * J + m + 1)
                        nc.tensor.matmul(table[:, m % 2], is_lane[:, m % LS], value[:, m % LS],
                                         start=False, stop=False).then_inc(tabled, 1)
                nc.tensor.matmul(whole, zero_r[:, 0:P], zero_r[:], start=False, stop=True).then_inc(table_done, 1)

            @block.vector
            def _(dve):
                def row_stats(b):
                    at_least(dve, mv_done, b * J)
                    for j in range(J):
                        nc.vector.bn_stats(stats[:, j], X[:, b, j]).then_inc(stat_done, 1)

                def gather_stats(b):
                    at_least(dve, xn_done, b * J)
                    for j in range(J):
                        dve.wait_ge(stat_done, b * J + j + 1).then_inc(passed, 1)
                        nc.vector.bn_aggr(mv[:, j], stats[:, j]).then_inc(mv_done, 1)

                def body(b, more):
                    if more:
                        row_stats(b + 1)
                    dve.wait_ge(std_done, b + 1)
                    nc.vector.reciprocal(rstd[:], std[:]).then_inc(rstd_done, 1)
                    dve.wait_ge(rstd_done, b + 1)
                    for j in range(J):
                        nc.vector.tensor_scalar(xn[:, b, j],
                                                X[:, b, j],
                                                mv[:, j, 0:1], rstd[:, j:j + 1],
                                                ALU.subtract, ALU.mult).then_inc(xn_done, 1)
                    if more:
                        gather_stats(b + 1)
                row_stats(0)
                gather_stats(0)
                for b in range(B):
                    body(b, b + 1 < B)

                v = nc.vector
                done = [0]

                def then(ins):
                    done[0] += 1
                    ins.then_inc(step, 1)
                    dve.wait_ge(step, done[0])

                def wide(a):
                    return a.unsqueeze(2).to_broadcast(small)

                def over(a):
                    return a.unsqueeze(1).to_broadcast(small)
                dve.wait_ge(logits_done, B)
                dve.wait_ge(consts, 13)
                lg = logits.rearrange("p b i j e -> p (b i j) e")
                then(v.tensor_reduce(top[:], lg, AXX, ALU.max))
                v.tensor_tensor(shifted[:], lg, wide(top[:]), ALU.subtract).then_inc(shift_ready, 1)
                dve.wait_ge(exp_done, 1)
                then(v.tensor_reduce(total[:], ex[:], AXX, ALU.add))
                then(v.reciprocal(rtotal[:], total[:]))
                then(v.tensor_tensor(pr[:], ex[:], wide(rtotal[:]), ALU.mult))
                for k in range(2):
                    then(v.tensor_reduce(prob[:, k], pr[:], AXX, ALU.max))
                    then(v.tensor_tensor(eq[:], pr[:], wide(prob[:, k]), ALU.is_equal))
                    then(v.tensor_tensor(cand[:], eq[:], over(rank[:]), ALU.mult))
                    then(v.tensor_reduce(best[:], cand[:], AXX, ALU.max))
                    then(v.tensor_tensor(hot[:, k], cand[:], wide(best[:]), ALU.is_equal))
                    if k == 0:
                        then(v.scalar_tensor_tensor(out=pr[:], in0=hot[:, k], scalar=-2.0, in1=pr[:],
                                                    op0=ALU.mult, op1=ALU.add))
                then(v.tensor_tensor(total[:], prob[:, 0], prob[:, 1], ALU.add))
                then(v.reciprocal(rtotal[:], total[:]))
                for k in range(2):
                    then(v.tensor_tensor(W[:, k], prob[:, k], rtotal[:], ALU.mult))
                src = hot.rearrange("p k (b j) e -> p (k b) j e", j=J)
                for n, d in enumerate((1, 2, 4, 8)):
                    dst = count[:, n % 2]
                    then(v.tensor_copy(dst[:, :, 0:d], src[:, :, 0:d]))
                    then(v.tensor_tensor(dst[:, :, d:], src[:, :, d:], src[:, :, 0:J - d], ALU.add))
                    src = dst
                cnt = src
                v.tensor_copy(sums.rearrange("p k b e -> p (k b) e"), cnt[:, :, J - 1]).then_inc(sums_ready, 1)
                dve.wait_ge(ranked, 1)
                before_p = sums_before[:, 0].rearrange("p (k b e) -> p k b e", k=2, b=B)
                whole = sums_before[:, 1].rearrange("p (k b e) -> p k b e", k=2, b=B)
                then(v.memset(offset[:, :, 0], 0.0))
                for b in range(1, B):
                    then(v.tensor_tensor(offset[:, :, b], whole[:, :, b - 1], offset[:, :, b - 1], ALU.add))
                then(v.tensor_tensor(offset[:], before_p, offset[:], ALU.add))
                other = count[:, 0]
                then(v.tensor_tensor(other, cnt, offset.rearrange("p k b e -> p (k b) e").unsqueeze(2)
                                     .to_broadcast([P, 2 * B, J, E]), ALU.add))
                hot8 = hot.rearrange("p k (b j) e -> p (k b) j e", j=J)
                then(v.tensor_tensor(cnt, other, hot8, ALU.mult))
                then(v.tensor_reduce(place.rearrange("p k (b j) -> p (k b) j", j=J), cnt, AXX, ALU.add))
                for k in range(2):
                    then(v.tensor_tensor(cand[:], hot[:, k], over(expert_no[:]), ALU.mult))
                    then(v.tensor_reduce(eno[:, k], cand[:], AXX, ALU.add))
                then(v.tensor_scalar(valid[:], place[:], float(CAP) + 0.5, None, ALU.is_lt))
                then(v.tensor_tensor(W[:], W[:], valid[:], ALU.mult))
                then(v.scalar_tensor_tensor(out=slot[:], in0=eno[:], scalar=2.0 * CAP, in1=place[:],
                                            op0=ALU.mult, op1=ALU.add))
                then(v.tensor_scalar(slot[:, 1], slot[:, 1], float(CAP), None, ALU.add))
                then(v.tensor_tensor(slot[:], slot[:], valid[:], ALU.mult))
                then(v.tensor_scalar(place[:], slot[:], -1.0, None, ALU.add))
                then(v.tensor_copy(slot_i[:], place[:]))
                then(v.tensor_scalar(row_code[:], row_no[:], 0.0, None, ALU.is_ge))
                then(v.tensor_tensor(row_code[:], row_code[:], row_no[:], ALU.add))
                then(v.tensor_scalar(hi_i[:], slot_i[:], 7, None, ALU.arith_shift_right))
                then(v.tensor_scalar(lo_i[:], slot_i[:], P - 1, None, ALU.bitwise_and))
                then(v.tensor_copy(hi[:], hi_i[:]))
                then(v.tensor_copy(lo[:], lo_i[:]))
                @looped(dve, B)
                def _(b):
                    for m in range(2 * J):
                        n, at, k = b * 2 * J + m, ds(b * J + m // 2, 1), m % 2
                        at_least(dve, tabled, n - LS + 1)
                        v.tensor_scalar(is_lane[:, m % LS], lane[:], lo[:, k, at], None, ALU.is_equal)
                        v.tensor_scalar(is_tile[:, m % LS], tile_no[:, k], hi[:, k, at], None,
                                        ALU.is_equal).then_inc(hot_tiles, 1)
                dve.wait_ge(table_done, 1)
                then(v.tensor_scalar(tabr[:], table[:], float(HALF), None, ALU.add))
                then(v.tensor_scalar(used[:], table[:], 0.0, None, ALU.is_gt))
                then(v.tensor_tensor(tabr[:], tabr[:], used[:], ALU.subtract))
                then(v.tensor_scalar(used[:], table[:], 0.0, None, ALU.not_equal))
                then(v.scalar_tensor_tensor(out=tabd[:], in0=tabr[:], scalar=2.0, in1=spare[:], op0=ALU.mult, op1=ALU.subtract))
                then(v.tensor_tensor(tabd[:], tabd[:], used[:], ALU.mult))
                then(v.tensor_tensor(tabd[:], tabd[:], spare[:], ALU.add))
                then(v.tensor_scalar(tabd[:, 1], tabd[:, 1], 1.0, None, ALU.add))
                for ints, floats in ((rowof, tabr), (dest, tabd)):
                    for k in range(2):
                        then(v.tensor_copy(ints.rearrange("p (e k t) -> p k e t", e=E, k=2)[:, k],
                                           floats[:, k].rearrange("p (e t) -> p e t", e=E)))


def build_experts(nc, c, wi_gate, wi_up, wo, xrows, yrows):
    ident, rowof, dest = c["ident"], c["rowof"], c["dest"]
    FT = F // P
    HI, LO = 0, 1
    PAIRS = ((HI, HI), (HI, LO), (LO, HI))
    with ExitStack() as ctx:
        def sb(n, s, t): return ctx.enter_context(nc.sbuf_tensor(n, s, t))
        def ps(n, s, t): return ctx.enter_context(nc.psum_tensor(n, s, t))
        def sem(n): return ctx.enter_context(nc.semaphore(n))
        passed = sem("passed3")
        pieces = {"raw": PIECES * KD * F, "xg": 2 * CT * D, "act_g": 2 * CH, "prod": 2 * CH, "ysb": 2 * CT * D}
        at, sizes = {}, 0
        for name, size in pieces.items():
            at[name] = first_floats(c["X"], sizes + size)[:, sizes:]
            sizes += size
        raw = at["raw"].rearrange("p (i f) -> p i f", i=PIECES)
        xg = at["xg"].rearrange("p (a t d) -> p a t d", a=2, t=CT)
        act_g = at["act_g"].rearrange("p (a c) -> p a c", a=2)
        prod = at["prod"].rearrange("p (a c) -> p a c", a=2)
        ysb = at["ysb"].rearrange("p (a t d) -> p a t d", a=2, t=CT)
        w_hi = sb("w_hi", [P, 2, PIECES, KD * F], F32R)
        w_lo = sb("w_lo", [P, 2, PIECES, KD * F], F32R)
        rows = sb("rows", [P, 2, ET], I32)
        dests = sb("dests", [P, 2, ET], I32)
        x_hi = sb("x_hi", [P, KD, CH], F32R)
        x_lo = sb("x_lo", [P, KD, CH], F32R)
        h_hi = sb("h_hi", [P, FT, CH], F32R)
        h_lo = sb("h_lo", [P, FT, CH], F32R)
        xp = ps("xp", [P, KD, CH], F32)
        gu = ps("gu", [P, 2, 2, CH], F32)
        yp = ps("yp", [P, 2, CH], F32)
        w_in = [sem(f"w_in{i}") for i in range(PIECES)]
        x_in = [sem(f"x_in{i}") for i in range(2)]
        y_out = [sem(f"y_out{i}") for i in range(2)]
        names = ("w_hi_done", "w_lo_done", "rows_ready", "x_turned", "x_hi_done", "x_lo_done", "gu_ready", "silu_done",
                 "prod_ready", "h_hi_done", "h_lo_done", "y_ready", "y_put0", "y_put1")
        (w_hi_done, w_lo_done, rows_ready, x_turned, x_hi_done, x_lo_done, gu_ready, silu_done,
         prod_ready, h_hi_done, h_lo_done, y_ready, y_put0, y_put1) = (sem("e_" + n) for n in names)
        NCH = E * EC
        SCATTER_LAG = 3

        def loop_experts(eng, body):
            body(0, 0, True)
            body(0, 1, True)
            with eng.Fori(1, E // 2 - 1) as pr:
                body(pr, 0, True)
                body(pr, 1, True)
            body(E // 2 - 1, 0, True)
            body(E // 2 - 1, 1, False)

        with nc.Block() as block:
            @block.sync
            def _(sp):
                def load(e):
                    for i, src in enumerate((wi_gate, wi_up, wo)):
                        at_least(sp, w_lo_done, (e - 1) * PIECES + i + 1)
                        sp.dma_start(raw[:, i], src[ds(e, 1)].rearrange("o p k f -> p (o k f)")).then_inc(w_in[i], 16)

                def body(pr, par, more):
                    e = pr * 2 + par
                    if more:
                        load(e + 1)
                loop_experts(sp, body)

            @block.gpsimd
            def _(pool):
                def split_lo(e, par, i):
                    pool.wait_ge(w_hi_done, e * PIECES + i + 1)
                    nc.gpsimd.tensor_tensor(w_lo[:, par, i], raw[:, i], w_hi[:, par, i].bitcast(F32),
                                            ALU.subtract).then_inc(w_lo_done, 1)

                def gather(pr, par, ch):
                    i = par * EC + ch
                    n = pr * 2 * EC + i
                    if i > 1 or not isinstance(n, int):
                        pool.wait_ge(x_turned, n - 1 if i > 1 else pr * 2 * EC).then_inc(passed, 1)
                    for t in range(CT):
                        nc.gpsimd.indirect_dma_start(
                            out=xg[:, i % 2, t], out_offset=None, in_=xrows,
                            in_offset=bass.IndirectOffsetOnAxis(ap=rows[:, par, ch * CT + t:ch * CT + t + 1].bitcast(U32), axis=0),
                        ).then_inc(x_in[i % 2], 16)

                def scatter(pr, par, ch):
                    i = par * EC + ch
                    n = pr * 2 * EC + i
                    pool.wait_ge(y_put0, n * 2 + 2).then_inc(passed, 1)
                    pool.wait_ge(y_put1, n * 2 + 2).then_inc(passed, 1)
                    for t in range(CT):
                        nc.gpsimd.indirect_dma_start(
                            out=yrows, in_=ysb[:, i % 2, t], in_offset=None,
                            out_offset=bass.IndirectOffsetOnAxis(ap=dests[:, par, ch * CT + t:ch * CT + t + 1].bitcast(U32), axis=0),
                        ).then_inc(y_out[i % 2], 16)

                def body(pr, par, more):
                    e = pr * 2 + par
                    pool.wait_ge(x_turned, e * EC).then_inc(passed, 1)
                    if not isinstance(pr, int) or pr > 0:
                        for i in range(2):
                            pool.wait_ge(y_out[i], (pr * EC if par else pr * EC - 2 - i) * 16 * CT).then_inc(passed, 1)
                    nc.gpsimd.tensor_copy(rows[:, par], rowof[:, ds(e * ET, ET)]).then_inc(rows_ready, 1)
                    nc.gpsimd.tensor_copy(dests[:, par], dest[:, ds(e * ET, ET)]).then_inc(rows_ready, 1)
                    pool.wait_ge(rows_ready, 2 * e + 2)
                    for ch in range(EC):
                        gather(pr, par, ch)
                        if ch >= SCATTER_LAG:
                            scatter(pr, par, ch - SCATTER_LAG)
                        elif par:
                            scatter(pr, 0, ch - SCATTER_LAG + EC)
                        elif not isinstance(pr, int) or pr > 0:
                            scatter(pr - 1, 1, ch - SCATTER_LAG + EC)
                        if more and ch >= 2:
                            split_lo(e + 1, 1 - par, ch - 2)

                loop_experts(pool, body)
                for ch in range(EC - SCATTER_LAG, EC):
                    scatter(E // 2 - 1, 1, ch)
                for i in range(2):
                    pool.wait_ge(y_out[i], 16 * CT * NCH // 2)

            @block.scalar
            def _(act):
                def split_hi(pr, par, i):
                    e = pr * 2 + par
                    at_least(act, w_in[i], 16 * e)
                    at_least(act, y_ready, (e - 1) * EC * CT)
                    nc.scalar.copy(w_hi[:, par, i], raw[:, i]).then_inc(w_hi_done, 1)

                def turn(pr, i):
                    n = pr * 2 * EC + i
                    act.wait_ge(x_turned, n + 1)
                    at_least(act, gu_ready, n * FT)
                    for k in range(KD):
                        nc.scalar.copy(x_hi[:, k], xp[:, k]).then_inc(x_hi_done, 1)

                def round_h(n, f):
                    act.wait_ge(prod_ready, n * FT + f + 1)
                    at_least(act, y_ready, n * CT)
                    nc.scalar.copy(h_hi[:, f], prod[:, f % 2]).then_inc(h_hi_done, 1)

                def body(pr, par, more):
                    for ch in range(EC):
                        i = par * EC + ch
                        n = pr * 2 * EC + i
                        for f in range(FT):
                            act.wait_ge(gu_ready, n * FT + f + 1)
                            at_least(act, prod_ready, n * FT + f - 1)
                            nc.scalar.activation(act_g[:, f % 2], gu[:, f % 2, 0], ACT.Silu).then_inc(silu_done, 1)
                            if f > 0:
                                round_h(n, f - 1)
                        round_h(n, FT - 1)
                        if more or ch < EC - 1:
                            turn(pr, i + 1)
                        for t in (0, 2):
                            act.wait_ge(y_ready, n * CT + t + 1)
                            at_least(act, y_out[i % 2], (pr * EC + i // 2) * 16 * CT)
                            nc.scalar.copy(ysb[:, i % 2, t], yp[:, 0, 0:D]).then_inc(y_put0, 1)
                        if more and ch in (1, 2, 3):
                            split_hi(pr + par, 1 - par, ch - 1)
                for i in range(PIECES):
                    split_hi(0, 0, i)
                turn(0, 0)
                loop_experts(act, body)

            @block.vector
            def _(dve):
                def turn(pr, i):
                    n = pr * 2 * EC + i
                    for k in range(KD):
                        dve.wait_ge(x_hi_done, n * KD + k + 1)
                        nc.vector.tensor_tensor(x_lo[:, k], xp[:, k], x_hi[:, k].bitcast(F32),
                                                ALU.subtract).then_inc(x_lo_done, 1)

                def rest_h(n, f):
                    dve.wait_ge(h_hi_done, n * FT + f + 1)
                    nc.vector.tensor_tensor(h_lo[:, f], prod[:, f % 2], h_hi[:, f].bitcast(F32),
                                            ALU.subtract).then_inc(h_lo_done, 1)

                def body(pr, par, more):
                    for ch in range(EC):
                        i = par * EC + ch
                        n = pr * 2 * EC + i
                        for f in range(FT):
                            dve.wait_ge(silu_done, n * FT + f + 1)
                            at_least(dve, h_lo_done, n * FT + f - 1)
                            nc.vector.tensor_tensor(prod[:, f % 2], act_g[:, f % 2], gu[:, f % 2, 1],
                                                    ALU.mult).then_inc(prod_ready, 1)
                            if f > 0:
                                rest_h(n, f - 1)
                        rest_h(n, FT - 1)
                        if more or ch < EC - 1:
                            turn(pr, i + 1)
                        for t in (1, 3):
                            dve.wait_ge(y_ready, n * CT + t + 1)
                            at_least(dve, y_out[i % 2], (pr * EC + i // 2) * 16 * CT)
                            nc.vector.tensor_copy(ysb[:, i % 2, t], yp[:, 1, 0:D]).then_inc(y_put1, 1)
                for i in range(PIECES):
                    dve.wait_ge(w_hi_done, i + 1)
                    nc.vector.tensor_tensor(w_lo[:, 0, i], raw[:, i], w_hi[:, 0, i].bitcast(F32),
                                            ALU.subtract).then_inc(w_lo_done, 1)
                turn(0, 0)
                loop_experts(dve, body)

            @block.tensor
            def _(pe):
                mm = nc.tensor.matmul
                w = [x.rearrange("p a i (k f) -> p a i k f", k=KD) for x in (w_hi, w_lo)]
                wd = [x.rearrange("p a i (f d) -> p a i f d", f=FT)[:, :, 2] for x in (w_hi, w_lo)]
                x, h = (x_hi, x_lo), (h_hi, h_lo)

                def turn(pr, i):
                    n = pr * 2 * EC + i
                    pe.wait_ge(x_in[i % 2], (pr * EC + i // 2 + 1) * 16 * CT)
                    at_least(pe, x_lo_done, n * KD)
                    for k in range(KD):
                        for t in range(CT):
                            last = nc.tensor.transpose(xp[:, k, t * P:(t + 1) * P], xg[:, i % 2, t, k * P:(k + 1) * P], ident[:])
                    last.then_inc(x_turned, 1)

                def body(pr, par, more):
                    pe.wait_ge(w_lo_done, (pr * 2 + par + 1) * PIECES)
                    for ch in range(EC):
                        i = par * EC + ch
                        n = pr * 2 * EC + i
                        pe.wait_ge(x_lo_done, (n + 1) * KD)
                        for f in range(FT):
                            at_least(pe, prod_ready, n * FT + f - 1)
                            for a in range(2):
                                todo = [(k, sw, sx) for k in range(KD) for sw, sx in PAIRS]
                                for j, (k, sw, sx) in enumerate(todo):
                                    last = mm(gu[:, f % 2, a], w[sw][:, par, a, k, f * P:(f + 1) * P], x[sx][:, k],
                                              start=(j == 0), stop=(j == len(todo) - 1))
                            last.then_inc(gu_ready, 1)
                        if more or ch < EC - 1:
                            turn(pr, i + 1)
                        for t in range(CT):
                            at_least(pe, (y_put0, y_put1)[t % 2], n * 2 + t // 2)
                            todo = [(f, sh, sw) for f in range(FT) for sh, sw in PAIRS]
                            for j, (f, sh, sw) in enumerate(todo):
                                if t == 0 and j % len(PAIRS) == 0:
                                    pe.wait_ge(h_lo_done, n * FT + f + 1)
                                last = mm(yp[:, t % 2, 0:D], h[sh][:, f, t * P:(t + 1) * P], wd[sw][:, par, f],
                                          start=(j == 0), stop=(j == len(todo) - 1))
                            last.then_inc(y_ready, 1)
                turn(0, 0)
                loop_experts(pe, body)


def build_combine(nc, c, x1rows, yrows, out):
    W = c["W"]
    with ExitStack() as ctx:
        def sb(n, s, t): return ctx.enter_context(nc.sbuf_tensor(n, s, t))
        def sem(n): return ctx.enter_context(nc.semaphore(n))
        GC = 4
        NGR = C64 // GC
        X = sb("x_again", [P, NGR, GC, D], F32)
        Y = sb("y_again", [P, NGR, GC, 2, D], F32)
        y = yrows[0:B * S * 2].rearrange("(p g r) d -> g p (r d)", p=P, g=NGR)
        rows_in = [sem(f"c_rows_in{g}") for g in range(NGR)]
        first_added, added, out_done = sem("first_added"), sem("c_added"), sem("out_done")
        with nc.Block() as block:
            @block.sync
            def _(sp):
                for g in range(NGR):
                    b, j = g * GC // J, g * GC % J
                    sp.dma_start(X[:, g], x1rows[b, :, j:j + GC]).then_inc(rows_in[g], 16)
                    sp.dma_start(Y[:, g].rearrange("p c k d -> p (c k d)"), y[g]).then_inc(rows_in[g], 16)

            @block.vector
            def _(dve):
                for g in range(NGR):
                    dve.wait_ge(rows_in[g], 32)
                    for k in range(2):
                        for i in range(GC):
                            n = g * GC + i
                            if k:
                                dve.wait_ge(first_added, n + 1)
                            nc.vector.scalar_tensor_tensor(out=X[:, g, i], in0=Y[:, g, i, k], scalar=W[:, k, n:n + 1],
                                                           in1=X[:, g, i], op0=ALU.mult, op1=ALU.add).then_inc(
                                                               (first_added, added)[k], 1)

            @block.scalar
            def _(act):
                for g in range(NGR):
                    b, j = g * GC // J, g * GC % J
                    act.wait_ge(added, (g + 1) * GC)
                    nc.scalar.dma_start(out[b, :, j:j + GC], X[:, g]).then_inc(out_done, 16)
                act.wait_ge(out_done, 16 * NGR)


def build(nc, t):
    def dram(n, shape, dt): return nc.dram_tensor(n, shape, dt, kind="Internal").ap()
    qparts = dram("qparts", [NQ, NC, 3, HD, QH * CH], BF16)
    kparts = dram("kparts", [NQ, NC, 3, HD, QH * CH], BF16)
    vstore = dram("vstore", [NQ, P, J, QH * VW], F32)
    x1rows = dram("x1rows", [B, P, J, D], F32)
    xrows = dram("xrows", [B * S, D], F32)
    yrows = dram("yrows", [2 * B * S + SLOTS, D], F32)
    with ExitStack() as ctx:
        def sb(n, s, dt): return ctx.enter_context(nc.sbuf_tensor(n, s, dt))
        c = {"rowof": sb("rowof", [P, TILES], I32), "dest": sb("dest", [P, TILES], I32),
             "W": sb("W", [P, 2, C64], F32)}
        c["ident"], c["identb"], c["maskb"] = build_constants(nc, ctx)
        with nc.sbuf_tensor("X", [P, B, J, D], F32) as c["X"], nc.sbuf_tensor("wsum", [P, B * D], F32) as c["wsum"]:
            build_project(nc, c, t["x"], t["wq"], t["wk"], t["wv"], t["w_out"], qparts, kparts, vstore)
            build_attend(nc, c, qparts, kparts, vstore, yrows)
            build_route(nc, c, t["gate_w"], t["wi_gate"], t["wi_up"], t["wo"], xrows, x1rows)
            build_experts(nc, c, t["wi_gate"], t["wi_up"], t["wo"], xrows, yrows)
        build_combine(nc, c, x1rows, yrows, t["out"])


def kernel(L0_attn_x, L0_attn_W_qkv, L0_attn_W_out, L0_ffn_gate_w, L0_ffn_wi_gate, L0_ffn_wi_up, L0_ffn_wo):
    import concourse.bacc as bacc
    from concourse.bass_utils import run_bass_kernel_spmd

    def lay(a, *shape_and_order):
        shape, order = shape_and_order
        return np.ascontiguousarray(np.asarray(a).reshape(shape).transpose(order))

    w = np.asarray(L0_attn_W_qkv)
    arrays = {"x": np.asarray(L0_attn_x).reshape(B, P, J, D)}
    for i, n in enumerate(("wq", "wk")):
        arrays[n] = lay(w[:, :, i * HD:(i + 1) * HD], (4, QH, KD, P, HD), (3, 2, 0, 4, 1)).reshape(P, KD, D)
    arrays["wv"] = lay(w[:, :, 2 * HD:], (NH, KD, P, HD), (2, 1, 0, 3)).reshape(P, KD, D)
    arrays["w_out"] = lay(L0_attn_W_out, (KD, P, D), (1, 0, 2))
    arrays["gate_w"] = lay(L0_ffn_gate_w, (E, KD, P), (2, 1, 0))
    arrays["wi_gate"] = lay(L0_ffn_wi_gate, (E, F, KD, P), (0, 3, 2, 1))
    arrays["wi_up"] = lay(L0_ffn_wi_up, (E, F, KD, P), (0, 3, 2, 1))
    arrays["wo"] = lay(L0_ffn_wo, (E, D, F // P, P), (0, 3, 2, 1))
    nc = bacc.Bacc("TRN2", target_bir_lowering=False, num_devices=1)
    t = {n: nc.dram_tensor(n + "_in", a.shape, mybir.dt.from_np(a.dtype), kind="ExternalInput").ap()
         for n, a in arrays.items()}
    t["out"] = nc.dram_tensor("out", (B, P, J, D), F32, kind="ExternalOutput").ap()
    build(nc, t)
    r = run_bass_kernel_spmd(nc, [{n + "_in": np.ascontiguousarray(a) for n, a in arrays.items()}], core_ids=[0])
    return r.results[0]["out"].reshape(B, S, D)
```
